# Optimizing a Trainium2 kernel written in Bass

```python
import numpy as np
import jax
import jax.numpy as jnp

def _softmax(x, axis=-1):
    return jax.nn.softmax(x, axis=axis)

def _gelu(x):
    return jax.nn.gelu(x, approximate=True)

def _silu(x):
    return jax.nn.silu(x)

def _sigmoid(x):
    return jax.nn.sigmoid(x)

def _layernorm(x, axis=-1, eps=1e-05):
    m = jnp.mean(x, axis=axis, keepdims=True)
    v = jnp.var(x, axis=axis, keepdims=True)
    return (x - m) / jnp.sqrt(v + eps)

def _scatter_add(tgt, idx, src, axis=0):
    return tgt.at[idx].add(src)

def _segment_sum(src, seg, n):
    return jax.ops.segment_sum(src, seg, n)
kernel_name = 'mk_adj_preln_d4_adj_r2_7a081c'

def setup_inputs(seed: int=0):
    np.random.seed(seed)
    _w = jnp.asarray

    def _rec_inputs():
        import jax
        import jax.numpy as jnp
        _gk = jax.random.key(seed)
        x = -0.0002928 + 1 * jax.random.normal(jax.random.fold_in(_gk, 1), (64, 128, 256), jnp.float32)
        _w = (1.0 + jnp.arange(128, dtype=jnp.float32)) ** (-0.5)
        _w = _w / _w.mean()
        _pij = jnp.clip(0.125 * _w[:, None] * _w[None, :], 0.0, 1.0)
        _a = jax.random.uniform(jax.random.fold_in(_gk, 2), (64, 128, 128)) < _pij
        adj = _a.astype(jnp.int32)
        return (x, adj)
    x, adj = _rec_inputs()

    def _L0_gnn_setup():
        import jax, jax.numpy as jnp
        import numpy as np
        L = 3
        D = 256
        B, N = (8, 512)
        EPS = 1e-05

        def layernorm(x, gamma, beta):
            mu = jnp.mean(x, axis=-1, keepdims=True)
            var = jnp.var(x, axis=-1, keepdims=True)
            return (x - mu) * jax.lax.rsqrt(var + EPS) * gamma + beta
        key = jax.random.key(seed)
        ks = jax.random.split(key, 12)
        s = 1.0 / np.sqrt(D)
        node_features = jax.random.normal(ks[0], (B, N, D), dtype=jnp.float32)
        adjacency_matrix = jax.random.randint(ks[1], (B, N, N), 0, 2, dtype=jnp.int32)
        return {'node_features': node_features, 'adjacency_matrix': adjacency_matrix, 'attn_w': jax.random.normal(ks[2], (L, 2 * D), dtype=jnp.float32) * (1.0 / np.sqrt(2 * D)), 'attn_b': jax.random.normal(ks[3], (L,), dtype=jnp.float32) * 0.01, 'W1': jax.random.normal(ks[4], (L, D, 4 * D), dtype=jnp.float32) * s, 'b1': jnp.zeros((L, 4 * D), dtype=jnp.float32), 'W2': jax.random.normal(ks[5], (L, 4 * D, D), dtype=jnp.float32) * (1.0 / np.sqrt(4 * D)), 'b2': jnp.zeros((L, D), dtype=jnp.float32), 'g1': jnp.ones((L, D), dtype=jnp.float32), 'beta1': jnp.zeros((L, D), dtype=jnp.float32), 'g2': jnp.ones((L, D), dtype=jnp.float32), 'beta2': jnp.zeros((L, D), dtype=jnp.float32)}
    _L0_gnn_all = _L0_gnn_setup()
    _L0_gnn_in = {k: v for k, v in _L0_gnn_all.items() if k in ('attn_w', 'attn_b', 'W1', 'b1', 'W2', 'b2', 'g1', 'beta1', 'g2', 'beta2')}
    del _L0_gnn_all

    def _L1_gnn_setup():
        import jax, jax.numpy as jnp
        import numpy as np
        ALPHA = 0.2
        MASK_VAL = -1000000000.0
        key = jax.random.key(seed)
        k1, k2, k3, k4 = jax.random.split(key, 4)
        B, N, F_in, F_out = (8, 1024, 256, 256)
        h = jax.random.normal(k1, (B, N, F_in), dtype=jnp.float32)
        adj = jax.random.randint(k2, (B, N, N), 0, 2, dtype=jnp.int32)

        def xavier(k, shape, gain=1.414):
            fan_in, fan_out = (shape[0], shape[1])
            bound = gain * np.sqrt(6.0 / (fan_in + fan_out))
            return jax.random.uniform(k, shape, jnp.float32, -bound, bound)
        W = xavier(k3, (F_in, F_out))
        a = xavier(k4, (2 * F_out, 1))
        return {'h': h, 'adj': adj, 'W': W, 'a': a}
    _L1_gnn_all = _L1_gnn_setup()
    _L1_gnn_in = {k: v for k, v in _L1_gnn_all.items() if k in ('W', 'a')}
    del _L1_gnn_all

    def _L2_gnn_setup():
        import jax, jax.numpy as jnp
        import numpy as np
        NEG_INF = -1e+30
        NEG_SLOPE = 0.2
        key = jax.random.key(seed)
        k1, k2, k3, k4, k5 = jax.random.split(key, 5)
        B, N, D, H = (2, 1024, 256, 8)
        k = D // H
        return {'x': jax.random.normal(k1, (B, N, D), dtype=jnp.float32), 'A': jax.random.randint(k2, (B, N, N), 0, 2, dtype=jnp.int32), 'W_proj': jax.random.normal(k3, (D, D), dtype=jnp.float32) * (1.0 / np.sqrt(D)), 'W_att': jax.random.normal(k4, (H, 2 * k), dtype=jnp.float32) * (1.0 / np.sqrt(2 * k)), 'b_att': jax.random.normal(k5, (H,), dtype=jnp.float32) * 0.01}
    _L2_gnn_all = _L2_gnn_setup()
    _L2_gnn_in = {k: v for k, v in _L2_gnn_all.items() if k in ('W_proj', 'W_att', 'b_att')}
    del _L2_gnn_all

    def _L3_gnn_setup():
        import jax, jax.numpy as jnp
        import numpy as np
        B, N, D = (32, 128, 256)
        DIR = 2
        NUM_LABELS = 16
        key = jax.random.key(seed)
        k1, k2, k3, k4 = jax.random.split(key, 4)
        feature = jax.random.normal(k1, (B, N, D), dtype=jnp.float32)
        graph = jax.random.randint(k2, (B, N, N), 0, NUM_LABELS, dtype=jnp.int64)
        weights = jax.random.normal(k3, (DIR, D, D), dtype=jnp.float32) * (1.0 / np.sqrt(D))
        stdv = 1.0 / np.sqrt(D)
        bias = jax.random.uniform(k4, (NUM_LABELS, D), dtype=jnp.float32, minval=-stdv, maxval=stdv)
        return {'feature': feature, 'graph': graph, 'weights': weights, 'bias': bias}
    _L3_gnn_all = _L3_gnn_setup()
    _L3_gnn_in = {k: v for k, v in _L3_gnn_all.items() if k in ('weights', 'bias')}
    del _L3_gnn_all
    return {'x': x, 'adj': adj, 'L0_gnn_attn_w': _L0_gnn_in['attn_w'], 'L0_gnn_attn_b': _L0_gnn_in['attn_b'], 'L0_gnn_W1': _L0_gnn_in['W1'], 'L0_gnn_b1': _L0_gnn_in['b1'], 'L0_gnn_W2': _L0_gnn_in['W2'], 'L0_gnn_b2': _L0_gnn_in['b2'], 'L0_gnn_g1': _L0_gnn_in['g1'], 'L0_gnn_beta1': _L0_gnn_in['beta1'], 'L0_gnn_g2': _L0_gnn_in['g2'], 'L0_gnn_beta2': _L0_gnn_in['beta2'], 'L1_gnn_W': _L1_gnn_in['W'], 'L1_gnn_a': _L1_gnn_in['a'], 'L2_gnn_W_proj': _L2_gnn_in['W_proj'], 'L2_gnn_W_att': _L2_gnn_in['W_att'], 'L2_gnn_b_att': _L2_gnn_in['b_att'], 'L3_gnn_weights': _L3_gnn_in['weights'], 'L3_gnn_bias': _L3_gnn_in['bias']}

def reference(x, adj, L0_gnn_attn_w, L0_gnn_attn_b, L0_gnn_W1, L0_gnn_b1, L0_gnn_W2, L0_gnn_b2, L0_gnn_g1, L0_gnn_beta1, L0_gnn_g2, L0_gnn_beta2, L1_gnn_W, L1_gnn_a, L2_gnn_W_proj, L2_gnn_W_att, L2_gnn_b_att, L3_gnn_weights, L3_gnn_bias):
    import jax
    import jax.numpy as jnp

    def _L0_gnn_ref(node_features, adjacency_matrix, attn_w, attn_b, W1, b1, W2, b2, g1, beta1, g2, beta2):
        import jax, jax.numpy as jnp
        import numpy as np
        L = 3
        D = 256
        B, N = (8, 512)
        EPS = 1e-05

        def layernorm(x, gamma, beta):
            mu = jnp.mean(x, axis=-1, keepdims=True)
            var = jnp.var(x, axis=-1, keepdims=True)
            return (x - mu) * jax.lax.rsqrt(var + EPS) * gamma + beta
        n = adjacency_matrix.shape[-1]
        mask = adjacency_matrix.astype(jnp.float32) + jnp.eye(n, dtype=jnp.float32) > 0
        x = node_features
        d = x.shape[-1]
        for l in range(attn_w.shape[0]):
            si = x @ attn_w[l, :d]
            sj = x @ attn_w[l, d:]
            scores = si[:, :, None] + sj[:, None, :] + attn_b[l]
            scores = jnp.where(scores >= 0, scores, 0.2 * scores)
            scores = jnp.where(mask, scores, -jnp.inf)
            attn = jax.nn.softmax(scores, axis=-1)
            agg = jnp.einsum('bij,bjd->bid', attn, x)
            h = layernorm(x + agg, g1[l], beta1[l])
            ff = jax.nn.gelu(h @ W1[l] + b1[l], approximate=False) @ W2[l] + b2[l]
            x = layernorm(h + ff, g2[l], beta2[l])
        return x

    def _L1_gnn_ref(h, adj, W, a):
        import jax, jax.numpy as jnp
        import numpy as np
        ALPHA = 0.2
        MASK_VAL = -1000000000.0
        Fout = W.shape[1]
        Wh = jnp.matmul(h, W)
        a1 = a[:Fout, 0]
        a2 = a[Fout:, 0]
        e_i = jnp.einsum('bnf,f->bn', Wh, a1)
        e_j = jnp.einsum('bnf,f->bn', Wh, a2)
        e = e_i[:, :, None] + e_j[:, None, :]
        e = jax.nn.leaky_relu(e, negative_slope=ALPHA)
        e = jnp.where(adj == 0, MASK_VAL, e)
        attention = jax.nn.softmax(e, axis=2)
        h_prime = jnp.matmul(attention, Wh)
        return jax.nn.elu(h_prime)

    def _L2_gnn_ref(x, A, W_proj, W_att, b_att):
        import jax, jax.numpy as jnp
        import numpy as np
        NEG_INF = -1e+30
        NEG_SLOPE = 0.2
        B, N, _ = x.shape
        H, two_k = W_att.shape
        k = two_k // 2
        xp = jnp.einsum('bnd,do->bno', x, W_proj)
        xh = xp.reshape(B, N, H, k).transpose(0, 2, 1, 3)
        a_src = jnp.einsum('bhnk,hk->bhn', xh, W_att[:, :k])
        a_dst = jnp.einsum('bhnk,hk->bhn', xh, W_att[:, k:])
        scores = a_src[:, :, :, None] + a_dst[:, :, None, :] + b_att[None, :, None, None]
        scores = jax.nn.leaky_relu(scores, negative_slope=NEG_SLOPE)
        mask = (A > 0)[:, None, :, :]
        scores = jnp.where(mask, scores, NEG_INF)
        att = jax.nn.softmax(scores, axis=-1)
        out = jax.nn.relu(jnp.einsum('bhij,bhjk->bhik', att, xh))
        return out.transpose(0, 2, 1, 3).reshape(B, N, H * k)

    def _L3_gnn_ref(feature, graph, weights, bias):
        import jax, jax.numpy as jnp
        import numpy as np
        B, N, D = (32, 128, 256)
        DIR = 2
        NUM_LABELS = 16
        out = feature + jnp.einsum('bni,doi->bno', feature, weights)
        out = out + jnp.take(bias, graph, axis=0).sum(axis=2)
        return out
    h = jnp.maximum(_layernorm(x, axis=-1), 0.0)
    x = x + _L0_gnn_ref(h, adj, L0_gnn_attn_w, L0_gnn_attn_b, L0_gnn_W1, L0_gnn_b1, L0_gnn_W2, L0_gnn_b2, L0_gnn_g1, L0_gnn_beta1, L0_gnn_g2, L0_gnn_beta2)
    h = jnp.maximum(_layernorm(x, axis=-1), 0.0)
    x = x + _L1_gnn_ref(h, adj, L1_gnn_W, L1_gnn_a)
    h = jnp.maximum(_layernorm(x, axis=-1), 0.0)
    x = x + _L2_gnn_ref(h, adj, L2_gnn_W_proj, L2_gnn_W_att, L2_gnn_b_att)
    h = jnp.maximum(_layernorm(x, axis=-1), 0.0)
    x = x + _L3_gnn_ref(h, adj, L3_gnn_weights, L3_gnn_bias)
    return x

_drawn_inputs = setup_inputs


def setup_inputs(seed=0):
    import zlib

    import numpy as np

    out = dict(_drawn_inputs(seed))
    spreads = {'L0_gnn_b1': (0.0, 0.1),
     'L0_gnn_b2': (0.0, 0.1),
     'L0_gnn_g1': (1.0, 0.2),
     'L0_gnn_beta1': (0.0, 0.1),
     'L0_gnn_g2': (1.0, 0.2),
     'L0_gnn_beta2': (0.0, 0.1)}
    factors = {'L0_gnn_attn_b': 200.0, 'L2_gnn_W_att': 5.764, 'L2_gnn_b_att': 200.0}
    for name, (base, spread) in spreads.items():
        noise = np.random.default_rng([zlib.crc32(name.encode()), seed]).standard_normal(out[name].shape)
        drawn = base * np.exp(spread * noise) if base else spread * noise
        out[name] = jnp.asarray(drawn.astype(out[name].dtype))
    for name, factor in factors.items():
        out[name] = (out[name] * factor).astype(out[name].dtype)
    return out
```

```python
from contextlib import ExitStack

import concourse.bass as bass
from concourse import mybir
from concourse.alu_op_type import AluOpType as ALU

ACT = mybir.ActivationFunctionType
AX = mybir.AxisListType
F32 = mybir.dt.float32
F32R = mybir.dt.float32r
BF16 = mybir.dt.bfloat16
I32 = mybir.dt.int32

P = 128
D = 256
KC = D // P
G = 4
C = G * P
HALF = 16
EPS = 1e-5
SLOPE = 0.2
MASKED = -1e30

M_NORM2 = 1
M_XT = 5
M_ROWS = 6
M_SCORES = 7
M_ET = 9
M_AGG = 10
M_HT = 13
T_LN = 0
T_ZT = 3
T_V = 4
T_ROWS = 5
T_SCORES = 6
T_ET = 9
T_AGG = 10
T_BT = 5
T_HEADS = (7, 9, 11, 13)
T_BACK = 15
T_CNT = 4
T_OUT = 6


class Seg:

    def __init__(self, it, mult, off):
        self.it, self.mult, self.off = it, mult, off


class Signal:

    def __init__(self, sem, per, step=1):
        self.sem, self.per, self.step = sem, per, step

    def __call__(self, seg, k):
        if isinstance(seg, int):
            return self.sem, (seg * self.per + k) * self.step
        const = (seg.off * self.per + k) * self.step
        if isinstance(seg.it, int):
            return self.sem, seg.it * (seg.mult * self.per * self.step) + const
        return self.sem, seg.it * (seg.mult * self.per * self.step) + const


def build(nc, x, adj, attn_w, attn_b, W1, b1, W2, b2, g1, beta1, g2, beta2,
          L1_W, L1_a, L2_Wp, L2_Wa, L2_ba, L3_W, L3_bias, out):
    B = x.shape[0]
    L = attn_w.shape[0]
    F = W1.shape[2]
    FC = F // P
    H = L2_Wa.shape[0]
    DH = D // H
    NLAB = L3_bias.shape[0]
    ITS = B // (2 * G)
    SL = 2 * L
    VW = D + 2 * H
    HPB = P // DH

    scratch = nc.dram_tensor("target_rows", (G * H, P), F32, kind="Internal").ap()

    with ExitStack() as ctx:
        def sb(name, shape, dt=F32):
            return ctx.enter_context(nc.sbuf_tensor(name, shape, dt))

        def signal(name, per=1, step=1):
            return Signal(ctx.enter_context(nc.semaphore(name)), per, step)

        W1h = sb("W1h", [P, L, KC, F], F32R)
        W1l = sb("W1l", [P, L, KC, F], F32R)
        W2h = sb("W2h", [P, L, FC, D], F32R)
        W2l = sb("W2l", [P, L, FC, D], F32R)
        Wg1 = sb("Wg1", [P, KC, D])
        Wg2 = sb("Wg2", [P, KC, VW])
        Wg3 = sb("Wg3", [P, KC, D])
        wrow0 = sb("wrow0", [P, L, KC, 33])
        wrow1 = sb("wrow1", [P, KC, 33])
        gamma2 = sb("gamma2", [P, L, D])
        betab2 = sb("betab2", [P, L, D])
        identf = sb("identf", [P, P])
        identb = sb("identb", [P, P], BF16)
        offdiag = sb("offdiag", [P, P], BF16)
        table = sb("table", [32, D])
        b1T = sb("b1T", [P, L, FC])
        b2T = sb("b2T", [P, L, KC])
        g1T = sb("g1T", [P, L, KC])
        beta1T = sb("beta1T", [P, L, KC])
        batt = sb("batt", [P, H])
        attb = sb("attb", [1, L])
        mhalf = sb("mhalf", [P, G])
        epsG = sb("epsG", [P, G])
        idleP = sb("idleP", [P, G])
        idleV = sb("idleV", [P, 2])
        rowL = sb("rowL", [P, C])
        rowR = sb("rowR", [P, C])
        xc = [sb(f"xc{s}", [P, G, D]) for s in range(2)]
        hT = [sb(f"hT{s}", [P, KC, C]) for s in range(2)]
        hTh = [sb(f"hTh{s}", [P, KC, C], F32R) for s in range(2)]
        hTl = [sb(f"hTl{s}", [P, KC, C], F32R) for s in range(2)]
        xt = [sb(f"xt{s}", [P, G, D]) for s in range(2)]
        neg0 = [sb(f"neg0{s}", [P, G, P], BF16) for s in range(2)]
        adjT = sb("adjT", [P, G, P], I32)
        neg1 = sb("neg1", [P, G, P], BF16)
        NG, NS = 2, 3
        gf = sb("gf", [P, NG, C])
        gh = sb("gh", [P, NS, C], F32R)
        gl = sb("gl", [P, NS, C], F32R)
        wk = sb("wk", [P, G * D])
        wkT = wk[:, :].rearrange("p (c n) -> p c n", c=KC)
        wkN = wk[:, :].rearrange("p (g d) -> p g d", g=G)
        tE = sb("tE", [P, G, P])
        lE = sb("lE", [P, G, P])
        adjM = tE[:, :, :].bitcast(I32)
        z = sb("z", [P, G * D])
        zN = z[:, :].rearrange("p (g d) -> p g d", g=G)
        qT = sb("qT", [P, KC, C])
        V = sb("V", [P, G, D])
        srcT = sb("srcT", [P, G, H])
        dstT = sb("dstT", [P, G * H])
        u = sb("u", [P, 2, H, P])
        cnt = sb("cnt", [P, G, 32])
        cntT = u[0:32, 1, 0:G, :].rearrange("p g n -> p (g n)")
        bT = sb("bT", [G * H, P])[:, :]
        st6 = [sb(f"st6{i}", [P, G, 6]) for i in range(2)]
        mv = [sb(f"mv{i}", [P, G, 2]) for i in range(2)]
        ve = [sb(f"ve{i}", [P, G]) for i in range(2)]
        rstd = [sb(f"rstd{i}", [P, G]) for i in range(2)]
        nmx = sb("nmx", [P, G])
        ssum = sb("ssum", [P, G])
        rsum = sb("rsum", [P, G])
        nmxT = sb("nmxT", [P, 2, H])
        ssumT = sb("ssumT", [P, G, H])
        rsumT = sb("rsumT", [P, G, H])

        ps = ctx.enter_context(nc.psum_tensor("ps", [P, 8, 512], F32))
        FF1, FF2, MB, TB = 0, 2, 4, 6

        i_stage = [signal(f"i_stage{k}", 1, 16) for k in range(2)]
        i_hi = signal("i_hi")
        i_lo = signal("i_lo")
        i_cols = signal("i_cols")
        i_zero = signal("i_zero")
        i_rows0 = signal("i_rows0", 4)
        i_small = signal("i_small", 14, 16)
        i_tabs = signal("i_tabs", 9, 16)
        i_pool = signal("i_pool")
        i_ident = signal("i_ident")
        i_fold = signal("i_fold")
        i_sum3 = signal("i_sum3")
        i_t3 = signal("i_t3")
        i_w3 = signal("i_w3")
        x_loaded = [signal(f"x_loaded{s}", 1, 16) for s in range(2)]
        adjM_loaded = signal("adjM_loaded", 1, 16)
        neg_part = signal("neg_part")
        neg0_ready = signal("neg0_ready")
        ln0_bn = signal("ln0_bn")
        ln0_mv = signal("ln0_mv")
        ln0_ve = signal("ln0_ve")
        ln0_rstd = signal("ln0_rstd")
        ln0_z = signal("ln0_z")
        xc_ready = [signal("xc0_ready"), signal("xcl_ready")]
        xT_filled = signal("xT_filled", KC)
        xT_ready = signal("xT_ready", KC)
        rows_filled = signal("rows_filled")
        rowa_ready = signal("rowa_ready")
        rowb_ready = signal("rowb_ready")
        s_filled = signal("s_filled")
        t_ready = signal("t_ready")
        l_ready = signal("l_ready")
        m_ready = signal("m_ready")
        e_ready = signal("e_ready")
        r_ready = signal("r_ready")
        eT_filled = signal("eT_filled")
        eT_ready = signal("eT_ready")
        agg_filled = signal("agg_filled", 2)
        hp_ready = signal("hp_ready", G)
        n1_bn = signal("n1_bn")
        n1_mv = signal("n1_mv")
        n1_ve = signal("n1_ve")
        n1_rstd = signal("n1_rstd")
        hn_ready = signal("hn_ready")
        hnT_filled = signal("hnT_filled", KC)
        hT_ready = signal("hT_ready", KC)
        hTh_ready = signal("hTh_ready", KC)
        hTl_ready = signal("hTl_ready", KC)
        ff1_filled = signal("ff1_filled", FC)
        gf_ready = signal("gf_ready", FC)
        gh_ready = signal("gh_ready", FC)
        gl_ready = signal("gl_ready", FC)
        g_used = signal("g_used", FC)
        yT_ready = signal("yT_ready", KC)
        y_filled = signal("y_filled", 2)
        n2_bn = signal("n2_bn")
        n2_mv = signal("n2_mv")
        n2_ve = signal("n2_ve")
        n2_rstd = signal("n2_rstd")
        xn_ready = signal("xn_ready")
        xg_ready = signal("xg_ready")
        xg2_ready = signal("xg2_ready")
        xt_loaded = [signal(f"xt_loaded{s}", 1, 16) for s in range(2)]
        x1_ready = signal("x1_ready")
        adjT_loaded = signal("adjT_loaded", 1, 16)
        neg1_ready = signal("neg1_ready")
        q_bn = signal("q_bn", 3)
        q_mv = signal("q_mv", 3)
        q_ve = signal("q_ve", 3)
        q_rstd = signal("q_rstd", 3)
        q_z = signal("q_z", 3)
        q_zT = signal("q_zT", 3 * KC)
        q_T = signal("q_T", 3 * KC)
        v1_filled = signal("v1_filled", 2)
        v1_ready = signal("v1_ready", 2)
        r1_filled = signal("r1_filled")
        r1a_ready = signal("r1a_ready")
        r1b_ready = signal("r1b_ready")
        s1_filled = signal("s1_filled")
        t1_ready = signal("t1_ready")
        l1_ready = signal("l1_ready")
        m1_ready = signal("m1_ready")
        e1_ready = signal("e1_ready")
        d1_ready = signal("d1_ready")
        eT1_filled = signal("eT1_filled")
        eT1_ready = signal("eT1_ready")
        agg1_filled = signal("agg1_filled", 2)
        mn_ready = signal("mn_ready")
        ex_ready = signal("ex_ready")
        em_ready = signal("em_ready")
        el_ready = signal("el_ready")
        x2_ready = signal("x2_ready")
        v2_filled = signal("v2_filled", G)
        v2_ready = signal("v2_ready", G)
        a2_ready = signal("a2_ready", G)
        b2_filled = signal("b2_filled")
        b2_ready = signal("b2_ready")
        b2_stored = signal("b2_stored", 1, 16)
        b2_spread = [signal(f"b2_spread{k}", 2, 16) for k in range(2)]
        u2_ready = signal("u2_ready", G)
        l2_ready = signal("l2_ready", G)
        m2_ready = signal("m2_ready", G)
        e2_ready = signal("e2_ready", G)
        eT2_filled = signal("eT2_filled", 2 * G)
        eT2_ready = signal("eT2_ready", 2 * G)
        agg2_filled = signal("agg2_filled", G)
        agg2_ready = signal("agg2_ready", G)
        d2_ready = signal("d2_ready")
        back_filled = signal("back_filled", 2)
        bn_ready = signal("bn_ready", 2)
        x3_ready = signal("x3_ready")
        oh_ready = signal("oh_ready", NLAB)
        cnt_ready = signal("cnt_ready", NLAB)
        cntT_filled = signal("cntT_filled")
        cntT_ready = signal("cntT_ready")
        res_ready = signal("res_ready")
        o_filled = signal("o_filled", 2)
        o_ready = signal("o_ready", 2)
        o_stored = signal("o_stored", 1, 16)

        EARLIER = 4
        pieces = []
        for l in range(L):
            w1 = W1[l].rearrange("(c p) f -> p c f", p=P)
            w2 = W2[l].rearrange("(c p) d -> p c d", p=P)
            for c in range(KC):
                pieces.append((W1h[:, l, c, :], W1l[:, l, c, :], w1[:, c, :], F // 1))
            for c in range(0, FC, EARLIER):
                pieces.append((W2h[:, l, c:c + EARLIER, :].rearrange("p c d -> p (c d)"),
                               W2l[:, l, c:c + EARLIER, :].rearrange("p c d -> p (c d)"),
                               w2[:, c:c + EARLIER, :], None))
        stage = [u[:, k, :, :].rearrange("p h n -> p (h n)") for k in range(2)]
        abc = qT[:, 0, :]
        wabc = qT[:, 1, :]
        raw3 = z[:, :].rearrange("p (d i) -> p d i", d=4)
        prod = V[:, :, :].rearrange("p g n -> p (g n)")[:, 0:D]
        prod2 = V[:, :, :].rearrange("p g n -> p (g n)")[:, D:2 * D]
        prod3 = hT[1][:, 0, 0:KC * D].rearrange("p (c n) -> p c n", c=KC)

        def graphs(t, g0, n=G):
            return t[bass.ds(g0, n)].rearrange("g p d -> p g d")

        def schedule(eng, slot, tail_end, loop=True):
            def body(it, first, last):
                for l in range(L):
                    for s in range(2):
                        slot(it, l, s, first, last)
            body(0, True, False)
            with eng.Fori(1, ITS - 1) as it:
                body(it, False, False)
            body(ITS - 1, False, True)
            tail_end()

        def plan(it, l, s, first, last):
            if l == 0 and s == 0:
                main = (it, 0, 1)
            elif s == 0:
                main = (it, l, 1)
            elif l < L - 1:
                main = (it, l + 1, 0)
            else:
                main = (it + 1, 0, 0)
            stages = {(0, 0): (2, -1, 0), (0, 1): (3, -1, 0), (1, 0): (1, -1, 1), (1, 1): (2, -1, 1),
                      (2, 0): (3, -1, 1), (2, 1): (1, 0, 0)}
            stage_no, d_it, ts = stages[(l, s)]
            tail = None if (first and d_it < 0) else (stage_no, it + d_it, ts)
            return main, tail

        def chain(m, it, l, s, first, last):
            mit, ml, ms = m
            attend = not (last and (l, s) == (L - 1, 1))
            if (l, s) == (0, 0):
                norm = None if first else (it - 1, L - 1, 1)
            elif s == 0:
                norm = (it, l - 1, 1)
            else:
                norm = (it, l, 0)
            return mit, ml, ms, norm, attend, first and ml == 0 and ms == 1

        def seg6(it, l, s):
            return Seg(it, SL, 2 * l + s)

        def seg4(it, l, s):
            return Seg(it, 2 * (L - 1), 2 * (l - 1) + s)

        def seg2(it, s):
            return Seg(it, 2, s)

        def seg1(it):
            return Seg(it, 1, 0)

        block = ctx.enter_context(nc.Block())

        @block.sync
        def _(sp):
            def load_x(it, s):
                sp.dma_start(xc[s][:, :, :], graphs(x, it * (2 * G) + s * G)).then_inc(x_loaded[s].sem, 16)

            def load_adjM(it, s, first):
                if not first:
                    sp.wait_ge(*eT_filled(Seg(it, SL, s - 1), 1))
                sp.dma_start(adjM, graphs(adj, it * (2 * G) + s * G)).then_inc(adjM_loaded.sem, 16)

            load_x(0, 0)
            load_adjM(0, 0, True)
            load_x(0, 1)
            for k, (_, _, src, _) in enumerate(pieces):
                if k >= 2:
                    sp.wait_ge(*i_lo(0, k - 1))
                dst = stage[k % 2]
                if len(src.shape) == 3:
                    dst = dst.rearrange("p (c d) -> p c d", d=D)
                sp.dma_start(dst, src).then_inc(i_stage[k % 2].sem, 16)

            def spread(it, s):
                q = seg2(it, s)
                sp.wait_ge(*b2_ready(q, 1))
                sp.dma_start(scratch, bT).then_inc(b2_stored.sem, 16)
                sp.wait_ge(*b2_stored(q, 1))
                for g in range(G):
                    if g >= 2:
                        sp.wait_ge(*eT2_filled(q, 2 * (g - 1)))
                    src = scratch[g * H:(g + 1) * H, :].rearrange("(a h) n -> a (h n)", a=1)
                    sp.dma_start(u[:, g % 2, :, :].rearrange("p h n -> p (h n)"),
                                 src.to_broadcast([P, H * P])).then_inc(b2_spread[g % 2].sem, 16)

            def store(it, s):
                q = seg2(it, s)
                sp.wait_ge(*o_ready(q, 2))
                sp.dma_start(graphs(out, it * (2 * G) + s * G), V[:, :, 0:D]).then_inc(o_stored.sem, 16)

            def load_adjT(it, s, first):
                if not first:
                    sp.wait_ge(*oh_ready(Seg(it, 2, s - 1), NLAB))
                sp.dma_start(adjT[:, :, :], graphs(adj, it * (2 * G) + s * G)).then_inc(adjT_loaded.sem, 16)

            def load_xt(it, s, first):
                if not first:
                    sp.wait_ge(*res_ready(Seg(it, 2, s - 2), 1))
                sp.dma_start(xt[s][:, :, :], graphs(x, it * (2 * G) + s * G)).then_inc(xt_loaded[s].sem, 16)

            def slot(it, l, s, first, last):
                _, tail = plan(it, l, s, first, last)
                if (l, s) == (1, 0):
                    load_xt(it, 0, first)
                    if not first:
                        load_adjT(it - 1, 1, False)
                if (l, s) == (2, 0) and not last:
                    sp.wait_ge(*hp_ready(seg6(it, L - 1, 0), G))
                    load_x(it + 1, 0)
                if (l, s) == (0, 0):
                    load_adjM(it, 1, False)
                if (l, s) == (2, 1):
                    load_adjT(it, 0, first)
                    load_xt(it, 1, first)
                    if not last:
                        sp.wait_ge(*hp_ready(seg6(it, L - 1, 1), G))
                        load_x(it + 1, 1)
                        load_adjM(it + 1, 0, False)
                if tail and tail[0] == 2:
                    spread(tail[1], tail[2])
                if tail and tail[0] == 3:
                    store(tail[1], tail[2])

            def end():
                it = ITS - 1
                spread(it, 0)
                store(it, 0)
                load_adjT(it, 1, False)
                spread(it, 1)
                store(it, 1)
                sp.wait_ge(*o_stored(seg2(it, 1), 1))

            schedule(sp, slot, end)

        @block.gpsimd
        def _(pool):
            pool.memset(identf[:, :], 0.0).then_inc(i_pool.sem, 1)
            pool.memset(identb[:, :], 0.0).then_inc(i_pool.sem, 1)
            pool.memset(offdiag[:, :], 1.0).then_inc(i_pool.sem, 1)
            pool.memset(mhalf[:, :], -0.5).then_inc(i_pool.sem, 1)
            pool.memset(cnt[:, :, :], 0.0).then_inc(i_pool.sem, 1)
            pool.memset(epsG[:, :], EPS).then_inc(i_pool.sem, 1)
            pool.wait_ge(*i_pool(0, 6))
            for t, fill in ((identf, 1.0), (identb, 1.0), (offdiag, 0.0)):
                pool.affine_select(out=t[:, :], in_=t[:, :], compare_op=ALU.not_equal, fill=fill,
                                   base=0, pattern=[[-1, P]], channel_multiplier=1).then_inc(i_ident.sem, 1)
            pool.wait_ge(*i_ident(0, 3))
            tabs = [
                (gamma2[:, :, :].rearrange("p l d -> p (l d)"),
                 g2.rearrange("(a l) d -> a (l d)", a=1).to_broadcast([P, L * D])),
                (betab2[:, :, :].rearrange("p l d -> p (l d)"),
                 beta2.rearrange("(a l) d -> a (l d)", a=1).to_broadcast([P, L * D])),
                (b1T[:, :, :], b1.rearrange("l (c p) -> p l c", p=P)),
                (b2T[:, :, :], b2.rearrange("l (c p) -> p l c", p=P)),
                (g1T[:, :, :], g1.rearrange("l (c p) -> p l c", p=P)),
                (beta1T[:, :, :], beta1.rearrange("l (c p) -> p l c", p=P)),
                (batt[:, :], L2_ba.rearrange("(a h) -> a h", a=1).to_broadcast([P, H])),
                (attb[:, :], attn_b.rearrange("(a l) -> a l", a=1)),
                (Wg1[:, :, :], L1_W.rearrange("(c p) f -> p c f", p=P)),
            ]
            assert len(tabs) == i_tabs.per
            for dst, src in tabs:
                pool.dma_start(dst, src, allow_slow_non_contiguous=True).then_inc(i_tabs.sem, 16)
            small = [
                (Wg2[:, :, 0:D], L2_Wp.rearrange("(c p) f -> p c f", p=P)),
                (abc, L1_a.rearrange("(a k) o -> a (k o)", a=1).to_broadcast([P, 2 * D])),
                (wabc, L2_Wa.rearrange("(a h) k -> a (h k)", a=1).to_broadcast([P, H * 2 * DH])),
            ]
            for d in range(2):
                for oc in range(KC):
                    small.append((raw3[:, 2 * d + oc, :], L3_W[d, oc * P:(oc + 1) * P, :]))
            small.append((table[0:NLAB, :], L3_bias))
            pool.wait_ge(*i_zero(0, 4))
            for l in range(L):
                for t in range(2):
                    w = attn_w[l, t * D:(t + 1) * D].rearrange("(c p) -> p c", p=P)
                    small.append((wrow0[:, l, :, 32 * t], w))
            assert len(small) == i_small.per, len(small)
            for dst, src in small:
                pool.dma_start(dst, src, allow_slow_non_contiguous=True).then_inc(i_small.sem, 16)

            def carry_waits():
                pool.tensor_tensor(idleP[:, :], mhalf[:, :], mhalf[:, :], ALU.mult)

            def mask0(it, s, first):
                q = seg2(it, s)
                pool.wait_ge(*adjM_loaded(q, 1))
                if not first:
                    pool.wait_ge(*s_filled(Seg(it, SL, s - 2), 1))
                carry_waits()
                for g in range(G):
                    pool.tensor_scalar(neg0[s][:, g, :], adjM[:, g, :], 0, MASKED, ALU.is_le,
                                       ALU.mult).then_inc(neg_part.sem, 1)
                pool.wait_ge(*neg_part(Seg(it, 2 * G, s * G), G))
                for g in range(G):
                    i = pool.tensor_tensor(neg0[s][:, g, :], neg0[s][:, g, :], offdiag[:, :], ALU.mult)
                i.then_inc(neg0_ready.sem, 1)

            def rsqrt(i, mv_ready, ve_ready, out_ready, seg, k=1):
                pool.wait_ge(*mv_ready(seg, k))
                pool.tensor_tensor(ve[i][:, :], mv[i][:, :, 1], epsG[:, :], ALU.add).then_inc(ve_ready.sem, 1)
                pool.wait_ge(*ve_ready(seg, k))
                pool.tensor_tensor(rstd[i][:, :], ve[i][:, :], mhalf[:, :], ALU.pow).then_inc(out_ready.sem, 1)

            def norm2(it, l, s):
                n = seg6(it, l, s)
                rsqrt(0, n2_mv, n2_ve, n2_rstd, n)
                pool.wait_ge(*xn_ready(n, 1))
                gb = gamma2[:, l:l + 1, :].to_broadcast([P, G, D])
                bb = betab2[:, l:l + 1, :].to_broadcast([P, G, D])
                dst = xc[s][:, :, :] if l < L - 1 else wkN
                pool.tensor_tensor(dst, wkN, gb, ALU.mult).then_inc(xg_ready.sem, 1)
                pool.wait_ge(*xg_ready(n, 1))
                i = pool.tensor_tensor(dst, dst, bb, ALU.add)
                if l < L - 1:
                    i.then_inc(xc_ready[1].sem, 1)
                else:
                    q = seg2(it, s)
                    i.then_inc(xg2_ready.sem, 1)
                    pool.wait_ge(*xg2_ready(q, 1))
                    pool.wait_ge(*xt_loaded[s](seg1(it), 1))
                    pool.tensor_tensor(xt[s][:, :, :], xt[s][:, :, :], wkN, ALU.add).then_inc(x1_ready.sem, 1)

            def main(h, mit, ml, ms, norm, attend, first):
                n = seg6(mit, ml, ms)
                if h == M_NORM2:
                    if norm is not None:
                        norm2(*norm)
                if not attend:
                    return
                if h == 3 and ml == 0:
                    rsqrt(0, ln0_mv, ln0_ve, ln0_rstd, seg2(mit, ms))
                if h == 4 and ml == 0:
                    mask0(mit, ms, first)
                if h == M_AGG:
                    rsqrt(0, n1_mv, n1_ve, n1_rstd, n)
                if h == M_HT:
                    for c in range(KC):
                        pool.wait_ge(*hTh_ready(n, c + 1))
                        pool.tensor_tensor(hTl[ms][:, c, :], hT[ms][:, c, :], hTh[ms][:, c, :].bitcast(F32),
                                           ALU.subtract).then_inc(hTl_ready.sem, 1)

            def tail(h, stage_no, it, s):
                q = seg2(it, s)
                if h == T_LN:
                    if stage_no == 1:
                        pool.wait_ge(*adjT_loaded(q, 1))
                        carry_waits()
                        for g in range(G):
                            i = pool.tensor_scalar(neg1[:, g, :], adjT[:, g, :], 0, MASKED, ALU.is_le, ALU.mult)
                        i.then_inc(neg1_ready.sem, 1)
                if h == (T_LN + 1 if stage_no > 1 else T_ZT - 1):
                    rsqrt(1, q_mv, q_ve, q_rstd, q, stage_no)

            def slot(it, l, s, first, last):
                m, t = plan(it, l, s, first, last)
                n = seg6(it, l, s)
                for h in range(HALF):
                    if h % 2 == 1:
                        c = h // 2
                        pool.wait_ge(*gh_ready(n, c + 1))
                        if c >= NS:
                            pool.wait_ge(*g_used(n, c + 1 - NS))
                        elif not (first and l == 0 and s == 0):
                            pool.wait_ge(*g_used(Seg(it, SL, 2 * l + s - 1), FC + c + 1 - NS))
                        pool.tensor_tensor(gl[:, (FC * (2 * l + s) + c) % NS, :], gf[:, c % NG, :],
                                           gh[:, (FC * (2 * l + s) + c) % NS, :].bitcast(F32),
                                           ALU.subtract).then_inc(gl_ready.sem, 1)
                    main(h, *chain(m, it, l, s, first, last))
                    if t:
                        tail(h, *t)

            def end():
                it = ITS - 1
                norm2(it, L - 1, 1)
                for t in ((2, it, 0), (3, it, 0), (1, it, 1), (2, it, 1), (3, it, 1)):
                    for h in range(HALF):
                        tail(h, *t)

            mask0(0, 0, True)
            rsqrt(0, ln0_mv, ln0_ve, ln0_rstd, seg2(0, 0))
            for h in (M_AGG, M_HT):
                main(h, 0, 0, 0, None, True, True)
            schedule(pool, slot, end)

        @block.scalar
        def _(act):
            for k, (hi, _, _, _) in enumerate(pieces):
                act.wait_ge(*i_stage[k % 2](0, k // 2 + 1))
                act.activation(hi, stage[k % 2], ACT.Copy).then_inc(i_hi.sem, 1)
            act.wait_ge(*i_tabs(0, i_tabs.per))
            for c in range(KC):
                act.wait_ge(*i_t3(0, c + 1))
                act.activation(Wg3[:, c, :], ps[:, TB + c, 0:D], ACT.Copy).then_inc(i_w3.sem, 1)

            def main(h, mit, ml, ms, norm, attend, first):
                n = seg6(mit, ml, ms)
                if not attend:
                    return
                if h == M_XT:
                    for c in range(KC):
                        act.wait_ge(*xT_filled(n, c + 1))
                        act.activation(wkT[:, c, :], ps[:, MB + c, :], ACT.Copy).then_inc(xT_ready.sem, 1)
                if h == M_ROWS:
                    act.wait_ge(*rows_filled(n, 1))
                    act.activation(rowL[0:1, :], ps[0:1, MB, :], ACT.Identity,
                                   bias=attb[0:1, ml:ml + 1]).then_inc(rowa_ready.sem, 1)
                if h == M_SCORES:
                    act.wait_ge(*s_filled(n, 1))
                    act.activation(tE[:, :, :].rearrange("p g n -> p (g n)"), ps[:, MB + 1, :], ACT.Copy,
                                   scale=SLOPE).then_inc(t_ready.sem, 1)
                    act.wait_ge(*m_ready(n, 1))
                    for g in range(G):
                        i = act.activation(tE[:, g, :], lE[:, g, :], ACT.Exp, bias=nmx[:, g:g + 1],
                                           accum_out=ssum[:, g:g + 1])
                    i.then_inc(e_ready.sem, 1)
                if h == M_ET:
                    act.wait_ge(*eT_filled(n, 1))
                    act.activation(lE[:, :, :].rearrange("p g n -> p (g n)"), ps[:, MB, :],
                                   ACT.Copy).then_inc(eT_ready.sem, 1)
                if h == M_HT:
                    for c in range(KC):
                        act.wait_ge(*hnT_filled(n, c + 1))
                        act.activation(hT[ms][:, c, :], ps[:, MB + c, :], ACT.Identity,
                                       scale=g1T[:, ml, c:c + 1],
                                       bias=beta1T[:, ml, c:c + 1]).then_inc(hT_ready.sem, 1)

            def tail(h, stage_no, it, s):
                q = seg2(it, s)
                if h == T_ZT:
                    for c in range(KC):
                        act.wait_ge(*q_zT(q, KC * (stage_no - 1) + c + 1))
                        act.activation(qT[:, c, :], ps[:, TB + c, :], ACT.Relu).then_inc(q_T.sem, 1)
                if stage_no == 1:
                    if h == T_V:
                        for c in range(2):
                            act.wait_ge(*v1_filled(q, c + 1))
                            act.activation(V[:, 2 * c:2 * c + 2, 0:D],
                                           ps[:, TB + c, :].rearrange("p (g d) -> p g d", g=2),
                                           ACT.Copy).then_inc(v1_ready.sem, 1)
                    if h == T_ROWS:
                        act.wait_ge(*r1_filled(q, 1))
                        act.activation(rowL[64:65, :], ps[64:65, TB, :], ACT.Copy).then_inc(r1a_ready.sem, 1)
                    if h == T_SCORES:
                        act.wait_ge(*s1_filled(q, 1))
                        act.activation(u[:, 0, 0:G, :].rearrange("p g n -> p (g n)"), ps[:, TB + 1, :],
                                       ACT.Copy, scale=SLOPE).then_inc(t1_ready.sem, 1)
                    if h == T_SCORES + 1:
                        act.wait_ge(*m1_ready(q, 1))
                        for g in range(G):
                            i = act.activation(u[:, 0, g, :], u[:, 0, G + g, :], ACT.Exp,
                                               bias=nmxT[:, 0, g:g + 1], accum_out=ssumT[:, 0, g:g + 1])
                        i.then_inc(e1_ready.sem, 1)
                    if h == T_ET:
                        act.wait_ge(*eT1_filled(q, 1))
                        act.activation(z[:, 0:C], ps[:, TB, :], ACT.Copy).then_inc(eT1_ready.sem, 1)
                    if h == T_AGG + 1:
                        act.wait_ge(*mn_ready(q, 1))
                        u1 = u[:, 1, :, :].rearrange("p h n -> p (h n)")
                        act.activation(u1, u1, ACT.Exp).then_inc(ex_ready.sem, 1)
                if stage_no == 2:
                    if h == T_V:
                        for g in range(G):
                            act.wait_ge(*v2_filled(q, g + 1))
                            act.activation(V[:, g, :], ps[:, TB + g % 2, 0:D], ACT.Copy).then_inc(v2_ready.sem, 1)
                    if h == T_BT:
                        act.wait_ge(*b2_filled(q, 1))
                        act.activation(bT, ps[0:G * H, TB, 0:P], ACT.Copy).then_inc(b2_ready.sem, 1)
                    if h in T_HEADS:
                        g = T_HEADS.index(h)
                        act.wait_ge(*m2_ready(q, g + 1))
                        for hd in range(H):
                            i = act.activation(u[:, g % 2, hd, :], u[:, g % 2, hd, :], ACT.Exp,
                                               bias=nmxT[:, g % 2, hd:hd + 1], accum_out=ssumT[:, g, hd:hd + 1])
                        i.then_inc(e2_ready.sem, 1)
                        for c in range(2):
                            act.wait_ge(*eT2_filled(q, 2 * g + c + 1))
                            act.activation(z[:, c * C:(c + 1) * C], ps[:, TB + c, :], ACT.Copy).then_inc(eT2_ready.sem, 1)
                        act.wait_ge(*agg2_filled(q, g + 1))
                        act.activation(qT[:, :, g * P:(g + 1) * P],
                                       ps[:, TB, 0:2 * P].rearrange("p (c n) -> p c n", c=2),
                                       ACT.Copy).then_inc(agg2_ready.sem, 1)
                if stage_no == 3:
                    if h == T_CNT:
                        act.wait_ge(*cntT_filled(q, 1))
                        act.activation(cntT, ps[0:32, TB, :], ACT.Copy).then_inc(cntT_ready.sem, 1)

            def slot(it, l, s, first, last):
                m, t = plan(it, l, s, first, last)
                n = seg6(it, l, s)
                prev = Seg(it, SL, 2 * l + s - 1)
                for h in range(HALF):
                    if h % 2 == 0:
                        c = h // 2
                        act.wait_ge(*ff1_filled(n, c + 1))
                        if c >= NG:
                            act.wait_ge(*gl_ready(n, c + 1 - NG))
                        elif not (first and l == 0 and s == 0):
                            act.wait_ge(*gl_ready(prev, FC + c + 1 - NG))
                        act.activation(gf[:, c % NG, :], ps[:, FF1 + c % 2, :], ACT.Gelu,
                                       bias=b1T[:, l, c:c + 1]).then_inc(gf_ready.sem, 1)
                    main(h, *chain(m, it, l, s, first, last))
                    if t:
                        tail(h, *t)

            def end():
                it = ITS - 1
                for t in ((2, it, 0), (3, it, 0), (1, it, 1), (2, it, 1), (3, it, 1)):
                    for h in range(HALF):
                        tail(h, *t)

            for h in range(HALF):
                main(h, 0, 0, 0, None, True, True)
            schedule(act, slot, end)

        @block.vector
        def _(dve):
            dve.memset(wrow0[:, :, :, :], 0.0).then_inc(i_zero.sem, 1)
            dve.memset(wrow1[:, :, :], 0.0).then_inc(i_zero.sem, 1)
            dve.memset(rowL[:, :], 0.0).then_inc(i_zero.sem, 1)
            dve.memset(rowR[:, :], 0.0).then_inc(i_zero.sem, 1)
            dve.memset(idleV[:, :], 0.0)
            dve.wait_ge(*i_zero(0, 4))
            for p in (0, 64):
                dve.memset(rowR[p:p + 1, :], 1.0).then_inc(i_rows0.sem, 1)
                dve.memset(rowL[p + 32:p + 33, :], 1.0).then_inc(i_rows0.sem, 1)

            def stats(i, src, bn_ready_, mv_ready, seg, k=1):
                for g in range(G):
                    ins = dve.bn_stats(st6[i][:, g, :], src(g))
                ins.then_inc(bn_ready_.sem, 1)
                dve.wait_ge(*bn_ready_(seg, k))
                dve.tensor_copy(idleV[:, 1:2], idleV[:, 0:1])
                for g in range(G):
                    ins = dve.bn_aggr(mv[i][:, g, :], st6[i][:, g, :])
                ins.then_inc(mv_ready.sem, 1)

            def normalise(i, dst, src, rstd_ready, done, seg, k=1):
                dve.wait_ge(*rstd_ready(seg, k))
                for g in range(G):
                    ins = dve.tensor_scalar(dst(g), src(g), mv[i][:, g, 0:1], rstd[i][:, g:g + 1],
                                            ALU.subtract, ALU.mult)
                ins.then_inc(done.sem, 1)

            def norm0(it, s):
                q = seg2(it, s)
                dve.wait_ge(*x_loaded[s](seg1(it), 1))
                stats(0, lambda g: xc[s][:, g, :], ln0_bn, ln0_mv, q)

            def norm0_apply(it, s):
                q = seg2(it, s)
                normalise(0, lambda g: xc[s][:, g, :], lambda g: xc[s][:, g, :], ln0_rstd, ln0_z, q)
                dve.wait_ge(*ln0_z(q, 1))
                dve.tensor_scalar(xc[s][:, :, :], xc[s][:, :, :], 0.0, None, ALU.max).then_inc(xc_ready[0].sem, 1)

            def norm2(it, l, s):
                n = seg6(it, l, s)
                for c in range(2):
                    dve.wait_ge(*y_filled(n, c + 1))
                yp = lambda g: ps[:, MB + g // 2, (g % 2) * D:(g % 2 + 1) * D]
                stats(0, yp, n2_bn, n2_mv, n)
                normalise(0, lambda g: wkN[:, g, :], yp, n2_rstd, xn_ready, n)

            def y(it, l, s):
                n = seg6(it, l, s)
                dve.wait_ge(*g_used(n, FC))
                for c in range(KC):
                    dve.scalar_tensor_tensor(hT[s][:, c, :], ps[:, FF2 + c, :], b2T[:, l, c:c + 1],
                                             hT[s][:, c, :], ALU.add, ALU.add).then_inc(yT_ready.sem, 1)

            def main(h, mit, ml, ms, norm, attend, first):
                n = seg6(mit, ml, ms)
                if h == 0 and norm is not None:
                    y(*norm)
                if h == M_NORM2 and norm is not None:
                    norm2(*norm)
                if not attend:
                    return
                if h == 2 and ml == 0:
                    norm0(mit, ms)
                if h == 3 and ml == 0:
                    norm0_apply(mit, ms)
                if h == M_ROWS:
                    dve.wait_ge(*rows_filled(n, 1))
                    dve.tensor_copy(rowR[32:33, :], ps[32:33, MB, :]).then_inc(rowb_ready.sem, 1)
                if h == M_SCORES:
                    flat = lambda t: t[:, :, :].rearrange("p g n -> p (g n)")
                    dve.wait_ge(*t_ready(n, 1))
                    dve.tensor_tensor(flat(lE), ps[:, MB + 1, :], flat(tE), ALU.max).then_inc(l_ready.sem, 1)
                    dve.wait_ge(*l_ready(n, 1))
                    dve.tensor_reduce(nmx[:, :], lE[:, :, :], AX.X, ALU.max, negate=True).then_inc(m_ready.sem, 1)
                if h == M_ET:
                    dve.wait_ge(*e_ready(n, 1))
                    dve.reciprocal(rsum[:, :], ssum[:, :]).then_inc(r_ready.sem, 1)
                if h == M_AGG:
                    dve.wait_ge(*r_ready(n, 1))
                    for g in range(G):
                        if g % 2 == 0:
                            dve.wait_ge(*agg_filled(n, g // 2 + 1))
                        dve.scalar_tensor_tensor(wkN[:, g, :], ps[:, MB + g // 2, (g % 2) * D:(g % 2 + 1) * D],
                                                 rsum[:, g:g + 1], xc[ms][:, g, :], ALU.mult,
                                                 ALU.add).then_inc(hp_ready.sem, 1)
                    dve.wait_ge(*hp_ready(n, G))
                    stats(0, lambda g: wkN[:, g, :], n1_bn, n1_mv, n)
                if h == M_AGG + 1:
                    normalise(0, lambda g: wkN[:, g, :], lambda g: wkN[:, g, :], n1_rstd, hn_ready, n)
                if h == M_HT:
                    for c in range(KC):
                        dve.wait_ge(*hT_ready(n, c + 1))
                        dve.tensor_copy(hTh[ms][:, c, :], hT[ms][:, c, :]).then_inc(hTh_ready.sem, 1)

            def tail(h, stage_no, it, s):
                q = seg2(it, s)
                if h == (T_LN if stage_no > 1 else T_ZT - 1):
                    if stage_no == 1:
                        dve.wait_ge(*x1_ready(q, 1))
                    else:
                        dve.wait_ge(*(x2_ready(q, 1) if stage_no == 2 else x3_ready(q, 1)))
                    stats(1, lambda g: xt[s][:, g, :], q_bn, q_mv, q, stage_no)
                if h == (T_LN + 1 if stage_no > 1 else T_ZT - 1):
                    normalise(1, lambda g: zN[:, g, :], lambda g: xt[s][:, g, :], q_rstd, q_z, q, stage_no)
                if stage_no == 1:
                    if h == T_ROWS:
                        dve.wait_ge(*r1_filled(q, 1))
                        dve.tensor_copy(rowR[96:97, :], ps[96:97, TB, :]).then_inc(r1b_ready.sem, 1)
                    if h == T_SCORES:
                        dve.wait_ge(*t1_ready(q, 1))
                        fl = lambda a: u[:, 0, a * G:(a + 1) * G, :].rearrange("p g n -> p (g n)")
                        dve.tensor_tensor(fl(1), ps[:, TB + 1, :], fl(0), ALU.max).then_inc(l1_ready.sem, 1)
                        dve.wait_ge(*l1_ready(q, 1))
                        dve.tensor_reduce(nmxT[:, 0, 0:G], u[:, 0, G:2 * G, :], AX.X, ALU.max,
                                          negate=True).then_inc(m1_ready.sem, 1)
                    if h == T_ET:
                        dve.wait_ge(*e1_ready(q, 1))
                        dve.reciprocal(rsumT[:, 0, 0:G], ssumT[:, 0, 0:G]).then_inc(d1_ready.sem, 1)
                    if h == T_AGG:
                        dve.wait_ge(*d1_ready(q, 1))
                        for g in range(G):
                            if g % 2 == 0:
                                dve.wait_ge(*agg1_filled(q, g // 2 + 1))
                            i = dve.tensor_scalar(u[:, 1, 2 * g:2 * g + 2, :].rearrange("p h n -> p (h n)"),
                                                  ps[:, TB + g // 2, (g % 2) * D:(g % 2 + 1) * D],
                                                  rsumT[:, 0, g:g + 1], 0.0, ALU.mult, ALU.min)
                        i.then_inc(mn_ready.sem, 1)
                    if h == T_AGG + 2:
                        dve.wait_ge(*ex_ready(q, 1))
                        u1 = u[:, 1, :, :].rearrange("p h n -> p (h n)")
                        dve.tensor_scalar(u1, u1, -1.0, None, ALU.add).then_inc(em_ready.sem, 1)
                        dve.wait_ge(*em_ready(q, 1))
                        for g in range(G):
                            ug = u[:, 1, 2 * g:2 * g + 2, :].rearrange("p h n -> p (h n)")
                            i = dve.scalar_tensor_tensor(ug, ps[:, TB + g // 2, (g % 2) * D:(g % 2 + 1) * D],
                                                         rsumT[:, 0, g:g + 1], ug, ALU.mult, ALU.max)
                        i.then_inc(el_ready.sem, 1)
                        dve.wait_ge(*el_ready(q, 1))
                        xf = xt[s][:, :, :].rearrange("p g d -> p (g d)")
                        dve.tensor_tensor(xf, xf, u1, ALU.add).then_inc(x2_ready.sem, 1)
                if stage_no == 2:
                    if h == T_V:
                        for g in range(G):
                            dve.wait_ge(*v2_ready(q, g + 1))
                            dve.tensor_copy(dstT[:, g * H:(g + 1) * H], ps[:, TB + g % 2, D + H:D + 2 * H])
                            dve.tensor_tensor(srcT[:, g, :], ps[:, TB + g % 2, D:D + H], batt[:, :],
                                              ALU.add).then_inc(a2_ready.sem, 1)
                    if h in T_HEADS:
                        g = T_HEADS.index(h)
                        if g == 0:
                            dve.wait_ge(*a2_ready(q, G))
                        dve.wait_ge(*b2_spread[g % 2](q, g // 2 + 1))
                        for hd in range(H):
                            i = dve.scalar_tensor_tensor(u[:, g % 2, hd, :], u[:, g % 2, hd, :],
                                                         srcT[:, g, hd:hd + 1], neg1[:, g, :],
                                                         ALU.add, ALU.add)
                        i.then_inc(u2_ready.sem, 1)
                        dve.wait_ge(*u2_ready(q, g + 1))
                        ug = u[:, g % 2, :, :].rearrange("p h n -> p (h n)")
                        dve.scalar_tensor_tensor(ug, ug, SLOPE, ug, ALU.mult, ALU.max).then_inc(l2_ready.sem, 1)
                        dve.wait_ge(*l2_ready(q, g + 1))
                        if g >= 2:
                            dve.wait_ge(*e2_ready(q, g - 1))
                        dve.tensor_reduce(nmxT[:, g % 2, :], u[:, g % 2, :, :], AX.X, ALU.max,
                                          negate=True).then_inc(m2_ready.sem, 1)
                    if h == T_BACK:
                        dve.wait_ge(*e2_ready(q, G))
                        dve.reciprocal(rsumT[:, :, :], ssumT[:, :, :]).then_inc(d2_ready.sem, 1)
                        dve.wait_ge(*d2_ready(q, 1))
                        for c in range(2):
                            dve.wait_ge(*back_filled(q, c + 1))
                            dve.tensor_tensor(z[:, c * C:(c + 1) * C].rearrange("p (g h k) -> p (g h) k", g=2, h=H),
                                              ps[:, TB + c, :].rearrange("p (g h k) -> p (g h) k", g=2, h=H),
                                              rsumT[:, 2 * c:2 * c + 2, :].rearrange("p g (h a) -> p (g h) a", a=1)
                                              .to_broadcast([P, 2 * H, DH]), ALU.mult).then_inc(bn_ready.sem, 1)
                        dve.wait_ge(*bn_ready(q, 2))
                        xf = xt[s][:, :, :].rearrange("p g d -> p (g d)")
                        dve.scalar_tensor_tensor(xf, z[:, :], 0.0, xf, ALU.max, ALU.add).then_inc(x3_ready.sem, 1)
                if stage_no == 3:
                    oh = u[:, 0, 0:2 * G, :].rearrange("p h n -> p (h n)").rearrange("p (k n) -> p k n", k=2)
                    if h == T_LN + 2:
                        for v in range(NLAB):
                            ohv = oh[:, v % 2, :].rearrange("p (g n) -> p g n", g=G)
                            dve.tensor_scalar(ohv, adjT[:, :, :], v, None, ALU.is_equal).then_inc(oh_ready.sem, 1)
                            dve.wait_ge(*oh_ready(q, v + 1))
                            dve.tensor_reduce(cnt[:, :, v], ohv, AX.X, ALU.add).then_inc(cnt_ready.sem, 1)
                    if h == T_CNT:
                        xf = xt[s][:, :, :].rearrange("p g d -> p (g d)")
                        dve.wait_ge(*q_zT(q, 3 * KC))
                        dve.scalar_tensor_tensor(z[:, :], z[:, :], 0.0, xf, ALU.max, ALU.add).then_inc(res_ready.sem, 1)
                    if h == T_OUT:
                        dve.wait_ge(*res_ready(q, 1))
                        for c in range(2):
                            dve.wait_ge(*o_filled(q, c + 1))
                            dve.tensor_tensor(V[:, 2 * c:2 * c + 2, 0:D],
                                              ps[:, TB + c, :].rearrange("p (g d) -> p g d", g=2),
                                              zN[:, 2 * c:2 * c + 2, :], ALU.add).then_inc(o_ready.sem, 1)

            def slot(it, l, s, first, last):
                m, t = plan(it, l, s, first, last)
                n = seg6(it, l, s)
                for h in range(HALF):
                    if h % 2 == 1:
                        c = h // 2
                        dve.wait_ge(*gf_ready(n, c + 1))
                        if c >= NS:
                            dve.wait_ge(*g_used(n, c + 1 - NS))
                        elif not (first and l == 0 and s == 0):
                            dve.wait_ge(*g_used(Seg(it, SL, 2 * l + s - 1), FC + c + 1 - NS))
                        dve.tensor_copy(gh[:, (FC * (2 * l + s) + c) % NS, :], gf[:, c % NG, :]).then_inc(gh_ready.sem, 1)
                    main(h, *chain(m, it, l, s, first, last))
                    if t:
                        tail(h, *t)

            def end():
                it = ITS - 1
                y(it, L - 1, 1)
                norm2(it, L - 1, 1)
                for t in ((2, it, 0), (3, it, 0), (1, it, 1), (2, it, 1), (3, it, 1)):
                    for h in range(HALF):
                        tail(h, *t)

            norm0(0, 0)
            norm0_apply(0, 0)
            for k, (hi, lo, _, _) in enumerate(pieces):
                dve.wait_ge(*i_hi(0, k + 1))
                dve.tensor_tensor(lo, stage[k % 2], hi.bitcast(F32), ALU.subtract).then_inc(i_lo.sem, 1)
            dve.wait_ge(*i_tabs(0, i_tabs.per))
            dve.wait_ge(*i_small(0, i_small.per))
            for c in range(KC):
                for t in range(2):
                    dve.tensor_tensor_reduce(prod, Wg1[:, c, :], abc[:, t * D:(t + 1) * D], 1.0, 0.0,
                                             ALU.mult, ALU.add,
                                             wrow1[:, c, 32 * t:32 * t + 1]).then_inc(i_fold.sem, 1)
                    wa = wabc.rearrange("p (h t k) -> p h t k", h=H, t=2)[:, :, t, :]
                    dve.tensor_tensor(prod2.rearrange("p (h k) -> p h k", h=H),
                                      Wg2[:, c, 0:D].rearrange("p (h k) -> p h k", h=H), wa,
                                      ALU.mult).then_inc(i_cols.sem, 1)
                    dve.wait_ge(*i_cols(0, 2 * c + t + 1))
                    dve.tensor_reduce(Wg2[:, c, D + t * H:D + (t + 1) * H],
                                      prod2.rearrange("p (h k) -> p h k", h=H), AX.X,
                                      ALU.add).then_inc(i_fold.sem, 1)
                    dve.wait_ge(*i_fold(0, 4 * c + 2 * t + 2))
            dve.tensor_tensor(prod3, raw3[:, 0:2, :], raw3[:, 2:4, :], ALU.add).then_inc(i_sum3.sem, 1)

            for h in range(4, HALF):
                main(h, 0, 0, 0, None, True, True)
            schedule(dve, slot, end)

        @block.tensor
        def _(pe):
            def transposes(bank, src, n, done):
                for i in range(n):
                    ins = pe.transpose(ps[:, bank, i * P:(i + 1) * P], src(i), identf[:, :])
                ins.then_inc(done.sem, 1)

            def rows(bank, w, src, base, done):
                for c in range(KC):
                    ins = pe.matmul(ps[base:base + 33, bank, :], w(c), src[:, c, :], start=(c == 0),
                                    stop=(c == KC - 1))
                ins.then_inc(done.sem, 1)

            def scores(bank, neg, base, done):
                pe.matmul(ps[:, bank, :], identb[:, :], neg[:, :, :].rearrange("p g n -> p (g n)"),
                          start=True, stop=False, skip_group_check=True)
                for g in range(G):
                    ins = pe.matmul(ps[:, bank, g * P:(g + 1) * P], rowL[base:base + 33, g * P:(g + 1) * P],
                                    rowR[base:base + 33, g * P:(g + 1) * P], start=False, stop=(g == G - 1),
                                    skip_group_check=True)
                ins.then_inc(done.sem, 1)

            def aggregate(bank, eT, v, done):
                for c in range(2):
                    for g in (2 * c, 2 * c + 1):
                        ins = pe.matmul(ps[:, bank + c, (g % 2) * D:(g % 2 + 1) * D], eT(g), v(g),
                                        start=True, stop=True)
                    ins.then_inc(done.sem, 1)

            def main(h, mit, ml, ms, norm, attend, first):
                n = seg6(mit, ml, ms)
                if h == M_NORM2 and norm is not None:
                    nit, nl, ns = norm
                    nn = seg6(nit, nl, ns)
                    pe.wait_ge(*yT_ready(nn, KC))
                    pe.wait_ge(*hT_ready(Seg(nit, SL, 2 * nl + ns + 1), KC))
                    for c in range(2):
                        transposes(MB + c, lambda i: hT[ns][:, i % KC, (2 * c + i // KC) * P:(2 * c + i // KC + 1) * P],
                                   G, y_filled)
                if not attend:
                    return
                if h == M_XT:
                    if ml == 0:
                        pe.wait_ge(*xc_ready[0](seg2(mit, ms), 1))
                        if not (norm is None):
                            nn = seg6(*norm)
                            pe.wait_ge(*xn_ready(nn, 1))
                        elif first and ms == 1:
                            pe.wait_ge(*hT_ready(0, KC))
                    else:
                        pe.wait_ge(*xc_ready[1](seg4(mit, ml, ms), 1))
                    for c in range(KC):
                        transposes(MB + c, lambda g: xc[ms][:, g, c * P:(c + 1) * P], G, xT_filled)
                if h == M_ROWS:
                    pe.wait_ge(*xT_ready(n, KC))
                    rows(MB, lambda c: wrow0[:, ml, c, :], wkT, 0, rows_filled)
                if h == M_SCORES:
                    pe.wait_ge(*rowa_ready(n, 1))
                    pe.wait_ge(*rowb_ready(n, 1))
                    if ml == 0:
                        pe.wait_ge(*neg0_ready(seg2(mit, ms), 1))
                    scores(MB + 1, neg0[ms], 0, s_filled)
                if h == M_ET:
                    pe.wait_ge(*e_ready(n, 1))
                    transposes(MB, lambda g: tE[:, g, :], G, eT_filled)
                if h == M_AGG:
                    pe.wait_ge(*eT_ready(n, 1))
                    aggregate(MB, lambda g: lE[:, g, :], lambda g: xc[ms][:, g, :], agg_filled)
                if h == M_HT:
                    pe.wait_ge(*hn_ready(n, 1))
                    for c in range(KC):
                        transposes(MB + c, lambda g: wkN[:, g, c * P:(c + 1) * P], G, hnT_filled)

            def tail(h, stage_no, it, s, first=False):
                q = seg2(it, s)
                if h == T_ZT:
                    pe.wait_ge(*q_z(q, stage_no))
                    if stage_no == 1 and not first:
                        pe.wait_ge(*o_ready(Seg(it, 2, s - 1), 2))
                    for c in range(KC):
                        transposes(TB + c, lambda g: zN[:, g, c * P:(c + 1) * P], G, q_zT)
                if stage_no == 1:
                    if h == T_V:
                        pe.wait_ge(*q_T(q, KC))
                        if not first:
                            pe.wait_ge(*o_stored(Seg(it, 2, s - 1), 1))
                        for c in range(2):
                            for g in (2 * c, 2 * c + 1):
                                for k in range(KC):
                                    i = pe.matmul(ps[:, TB + c, (g % 2) * D:(g % 2 + 1) * D],
                                                  qT[:, k, g * P:(g + 1) * P], Wg1[:, k, :],
                                                  start=(k == 0), stop=(k == KC - 1))
                            i.then_inc(v1_filled.sem, 1)
                    if h == T_ROWS:
                        pe.wait_ge(*v1_ready(q, 1))
                        rows(TB, lambda c: wrow1[:, c, :], qT, 64, r1_filled)
                    if h == T_SCORES:
                        pe.wait_ge(*r1a_ready(q, 1))
                        pe.wait_ge(*r1b_ready(q, 1))
                        pe.wait_ge(*neg1_ready(q, 1))
                        pe.wait_ge(*v1_ready(q, 2))
                        scores(TB + 1, neg1, 64, s1_filled)
                    if h == T_ET:
                        pe.wait_ge(*e1_ready(q, 1))
                        transposes(TB, lambda g: u[:, 0, g, :], G, eT1_filled)
                    if h == T_AGG:
                        pe.wait_ge(*eT1_ready(q, 1))
                        aggregate(TB, lambda g: z[:, g * P:(g + 1) * P], lambda g: V[:, g, 0:D], agg1_filled)
                if stage_no == 2:
                    if h == T_V:
                        pe.wait_ge(*q_T(q, 2 * KC))
                        for g in range(G):
                            if g >= 2:
                                pe.wait_ge(*a2_ready(q, g - 1))
                            for k in range(KC):
                                i = pe.matmul(ps[:, TB + g % 2, 0:VW], qT[:, k, g * P:(g + 1) * P],
                                              Wg2[:, k, :], start=(k == 0), stop=(k == KC - 1))
                            i.then_inc(v2_filled.sem, 1)
                    if h == T_BT:
                        pe.wait_ge(*a2_ready(q, G))
                        pe.transpose(ps[0:G * H, TB, 0:P], dstT[:, :], identf[:, :]).then_inc(b2_filled.sem, 1)
                    if h in T_HEADS:
                        g = T_HEADS.index(h)
                        pe.wait_ge(*e2_ready(q, g + 1))
                        if g >= 1:
                            pe.wait_ge(*agg2_ready(q, g))
                        for c in range(2):
                            transposes(TB + c, lambda i: u[:, g % 2, 4 * c + i, :], 4, eT2_filled)
                        pe.wait_ge(*eT2_ready(q, 2 * g + 2))
                        for hd in range(H):
                            r = hd % HPB * DH
                            i = pe.matmul(ps[r:r + DH, TB, hd // HPB * P:(hd // HPB + 1) * P],
                                          V[:, g, hd * DH:(hd + 1) * DH], z[:, hd * P:(hd + 1) * P],
                                          start=True, stop=True)
                        i.then_inc(agg2_filled.sem, 1)
                    if h == T_BACK:
                        pe.wait_ge(*agg2_ready(q, G))
                        for c in range(2):
                            transposes(TB + c, lambda i: qT[:, i % 2, (2 * c + i // 2) * P:(2 * c + i // 2 + 1) * P],
                                       4, back_filled)
                if stage_no == 3:
                    if h == T_CNT:
                        pe.wait_ge(*cnt_ready(q, NLAB))
                        pe.wait_ge(*q_T(q, 3 * KC))
                        for g in range(G):
                            i = pe.transpose(ps[0:32, TB, g * P:(g + 1) * P], cnt[:, g, :], identf[:, :])
                        i.then_inc(cntT_filled.sem, 1)
                    if h == T_OUT:
                        pe.wait_ge(*cntT_ready(q, 1))
                        for c in range(2):
                            for g in (2 * c, 2 * c + 1):
                                o = ps[:, TB + c, (g % 2) * D:(g % 2 + 1) * D]
                                for k in range(KC):
                                    pe.matmul(o, qT[:, k, g * P:(g + 1) * P], Wg3[:, k, :], start=(k == 0),
                                              stop=False)
                                i = pe.matmul(o, cntT[0:NLAB, g * P:(g + 1) * P], table[0:NLAB, :], start=False,
                                              stop=True)
                            i.then_inc(o_filled.sem, 1)

            def ff1(n, l, s, c, first):
                if c >= 2:
                    pe.wait_ge(*gf_ready(n, c - 1))
                elif not first:
                    pe.wait_ge(*gf_ready(Seg(n.it, n.mult, n.off - 1), FC + c - 1))
                ins = None
                for i, (w, v) in enumerate(((W1h, hTh), (W1h, hTl), (W1l, hTh))):
                    if c == 0:
                        pe.wait_ge(*(hTh_ready(n, KC) if i != 1 else hTl_ready(n, KC)))
                    for k in range(KC):
                        ins = pe.matmul(ps[:, FF1 + c % 2, :], w[:, l, k, c * P:(c + 1) * P], v[s][:, k, :],
                                        start=(i == 0 and k == 0), stop=(i == 2 and k == KC - 1))
                ins.then_inc(ff1_filled.sem, 1)

            def ff2(n, l, s, c, first):
                r = (FC * (2 * l + s) + c) % NS
                if c == 0 and not first:
                    pe.wait_ge(*yT_ready(Seg(n.it, n.mult, n.off - 1), KC))
                ins = None
                for i, (w, v) in enumerate(((W2h, gh), (W2l, gh), (W2h, gl))):
                    if i != 1:
                        pe.wait_ge(*(gh_ready(n, c + 1) if i == 0 else gl_ready(n, c + 1)))
                    for k in range(KC):
                        ins = pe.matmul(ps[:, FF2 + k, :], w[:, l, c, k * P:(k + 1) * P], v[:, r, :],
                                        start=(c == 0 and i == 0), stop=(c == FC - 1 and i == 2))
                ins.then_inc(g_used.sem, 1)

            def slot(it, l, s, first, last):
                m, t = plan(it, l, s, first, last)
                n = seg6(it, l, s)
                fst = first and l == 0 and s == 0
                for h in range(HALF):
                    c = h // 2
                    if h % 2 == 0:
                        ff1(n, l, s, c, fst)
                    elif c >= 1:
                        ff2(n, l, s, c - 1, fst)
                    main(h, *chain(m, it, l, s, first, last))
                    if t:
                        tail(h, *t, first=first)
                ff2(n, l, s, FC - 1, fst)

            def end():
                it = ITS - 1
                nn = seg6(it, L - 1, 1)
                pe.wait_ge(*yT_ready(nn, KC))
                for c in range(2):
                    transposes(MB + c, lambda i: hT[1][:, i % KC, (2 * c + i // KC) * P:(2 * c + i // KC + 1) * P],
                               G, y_filled)
                for t in ((2, it, 0), (3, it, 0), (1, it, 1), (2, it, 1), (3, it, 1)):
                    for h in range(HALF):
                        tail(h, *t)

            pe.wait_ge(*i_ident(0, 3))
            pe.wait_ge(*i_rows0(0, 4))
            pe.wait_ge(*i_small(0, i_small.per))
            pe.wait_ge(*i_sum3(0, 1))
            pe.wait_ge(*i_fold(0, 8))
            for c in range(KC):
                transposes(TB + c, lambda o: prod3[:, o, c * P:(c + 1) * P], KC, i_t3)
            pe.wait_ge(*i_w3(0, KC))
            pe.wait_ge(*i_lo(0, len(pieces)))
            for h in range(HALF):
                main(h, 0, 0, 0, None, True, True)
            schedule(pe, slot, end)


_INS = ["x", "adj", "L0_gnn_attn_w", "L0_gnn_attn_b", "L0_gnn_W1", "L0_gnn_b1", "L0_gnn_W2", "L0_gnn_b2",
        "L0_gnn_g1", "L0_gnn_beta1", "L0_gnn_g2", "L0_gnn_beta2", "L1_gnn_W", "L1_gnn_a", "L2_gnn_W_proj",
        "L2_gnn_W_att", "L2_gnn_b_att", "L3_gnn_weights", "L3_gnn_bias"]


def kernel(**inputs):
    import numpy as _np
    import concourse.bacc as _bacc
    from concourse import mybir as _mybir
    from concourse.bass_utils import run_bass_kernel_spmd as _run

    nc = _bacc.Bacc("TRN2", target_bir_lowering=False, num_devices=1)
    arrays, args = {}, []
    for name in _INS:
        a = _np.ascontiguousarray(inputs[name])
        arrays[f"in_{name}_dram"] = a
        args.append(nc.dram_tensor(f"in_{name}_dram", a.shape, _mybir.dt.from_np(a.dtype), kind="ExternalInput").ap())
    shape = inputs["x"].shape
    out = nc.dram_tensor("out_dram", shape, _mybir.dt.float32, kind="ExternalOutput").ap()
    build(nc, *args, out)
    r = _run(nc, [arrays], core_ids=[0])
    return r.results[0]["out_dram"]
```

```python
from contextlib import ExitStack

import concourse.bass as bass
from concourse import mybir
from concourse.alu_op_type import AluOpType as ALU

ACT = mybir.ActivationFunctionType
AX = mybir.AxisListType
F32 = mybir.dt.float32
F32R = mybir.dt.float32r
BF16 = mybir.dt.bfloat16
I32 = mybir.dt.int32

P = 128
D = 256
KC = D // P
G = 4
C = G * P
GM = 2
CM = GM * P
NSTR = 4
T = 40
LEAD = 3
PHASES = 6
EPS = 1e-5
SLOPE = 0.2
MASKED = -1e30

FF1_AT = (0, 10, 20, 30)
GELU_AT = (3, 13, 23, 33)
GH_AT = (4, 15, 25, 35)
GL_AT = (6, 16, 26, 36)
FF2_AT = (12, 22, 32, 43)
M_Y, M_YBACK, M_N2, M_N2_RS, M_XN, M_XB, M_X1 = 4, 8, 10, 14, 14, 18, 19
M_LN0, M_LN0_RS, M_Z0, M_MASK = 11, 15, 19, 15
M_XT, M_XT_COPY = 26, 31
M_ROWS, M_ROW_COPY = 34, 36
M_SCORES, M_T, M_MAX, M_EXP = 42, 45, 45, 51
M_ET, M_ET_COPY, M_RECIP = 58, 60, 60
M_AGG, M_HP, M_N1_RS, M_HN = 68, 70, 75, 75
M_HT, M_HT_COPY, M_HTH, M_HTL = 99, 101, 102, 113
COUNT_AT = (0, 6, 20, 26)
TREE_AT = (11, 30)
N_AT = (22, 79, 212)
N_RS = (21, 82, 215)
N_Z = (25, 82, 215)
N_ZT = (31, 84, 220)
N_ZT_COPY = (31, 85, 222)
G1_V, G1_V_COPY, G1_ROWS, G1_ROW_COPY = 36, 39, 37, 43
G1_SCORES, G1_T, G1_MAX, G1_EXP = 44, 47, 49, 49
G1_ET, G1_ET_COPY, G1_RECIP, G1_AGG, G1_MIN, G1_ELU_EXP, G1_ELU = 60, 59, 59, 60, 64, 72, 74
G2_V = (88, 90, 92, 94)
G2_V_COPY = (89, 92, 94, 96)
G2_BT, G2_BT_COPY = 99, 100
G2_SUM = (113, 129, 153, 173)
G2_LEAKY = (118, 138, 158, 181)
G2_MAX = (123, 143, 163, 182)
G2_EXP = (128, 147, 165, 188)
G2_ET = (135, 155, 175, 195)
G2_ET_COPY = (137, 158, 177, 198)
G2_AGG = (141, 161, 181, 201)
G2_AGG_COPY = (146, 163, 180, 203)
G2_BACK, G2_X3 = 206, 209
G3_CNT, G3_CNT_COPY, G3_RES, G3_OUT, G3_SUM = 208, 212, 226, 224, 232
PIECES_AT = (6, 26)


class Seg:

    def __init__(self, it, mult, off):
        self.it, self.mult, self.off = it, mult, off


class Signal:

    def __init__(self, sem, per, step=1):
        self.sem, self.per, self.step = sem, per, step

    def __call__(self, seg, k):
        if isinstance(seg, int):
            return self.sem, (seg * self.per + k) * self.step
        const = (seg.off * self.per + k) * self.step
        if isinstance(seg.it, int):
            return self.sem, seg.it * (seg.mult * self.per * self.step) + const
        return self.sem, seg.it * (seg.mult * self.per * self.step) + const


def build(nc, x, adj, attn_w, attn_b, W1, b1, W2, b2, g1, beta1, g2, beta2,
          L1_W, L1_a, L2_Wp, L2_Wa, L2_ba, L3_W, L3_bias, out):
    B = x.shape[0]
    L = attn_w.shape[0]
    F = W1.shape[2]
    FC = F // P
    H = L2_Wa.shape[0]
    DH = D // H
    NLAB = L3_bias.shape[0]
    FP = FC // 2
    ITS = B // (NSTR * GM)
    SL = NSTR * L
    NSEG = ITS * SL
    VW = D + 2 * H
    HPB = P // DH

    scratch = nc.dram_tensor("target_rows", (G * H, P), F32, kind="Internal").ap()

    with ExitStack() as ctx:
        def sb(name, shape, dt=F32):
            return ctx.enter_context(nc.sbuf_tensor(name, shape, dt))

        def signal(name, per=1, step=1):
            return Signal(ctx.enter_context(nc.semaphore(name)), per, step)

        W1h = sb("W1h", [P, L, KC, F], F32R)
        W1l = sb("W1l", [P, L, KC, F], F32R)
        W2h = sb("W2h", [P, L, FC, D], F32R)
        W2l = sb("W2l", [P, L, FC, D], F32R)
        Wg1 = sb("Wg1", [P, KC, D])
        Wg2 = sb("Wg2", [P, KC, VW])
        Wg3 = sb("Wg3", [P, KC, D])
        wrow0 = sb("wrow0", [P, L, KC, 33])
        wrow1 = sb("wrow1", [P, KC, 33])
        gamma2 = sb("gamma2", [P, L, D])
        betab2 = sb("betab2", [P, L, D])
        identf = sb("identf", [P, P])
        identb = sb("identb", [P, P], BF16)
        offdiag = sb("offdiag", [P, P], BF16)
        table = sb("table", [NLAB, D])
        b1T = sb("b1T", [P, L, FC])
        b2T = sb("b2T", [P, L, KC])
        g1T = sb("g1T", [P, L, KC])
        beta1T = sb("beta1T", [P, L, KC])
        batt = sb("batt", [P, H])
        attb = sb("attb", [1, L])
        mhalf = sb("mhalf", [P, G])
        epsG = sb("epsG", [P, G])
        idleP = sb("idleP", [P, G])
        idleV = sb("idleV", [P, 2])
        rowL = sb("rowL", [P, C])
        rowR = sb("rowR", [P, C])
        xc = [sb(f"xc{s}", [P, GM, D]) for s in range(NSTR)]
        hT = [sb(f"hT{s}", [P, KC, CM]) for s in range(NSTR)]
        hTh = [sb(f"hTh{s}", [P, KC, CM], F32R) for s in range(NSTR)]
        hTl = [sb(f"hTl{s}", [P, KC, CM], F32R) for s in range(NSTR)]
        xt = [sb(f"xt{r}", [P, G, D]) for r in range(2)]
        neg0 = [sb(f"neg0{s}", [P, GM, P], BF16) for s in range(NSTR)]
        adjT = sb("adjT", [P, G, P], I32)
        neg1 = sb("neg1", [P, G, P], BF16)
        NG, NS = 3, 3
        gf = sb("gf", [P, NG, 2 * CM])
        gh = sb("gh", [P, NS, 2 * CM], F32R)
        gl = sb("gl", [P, NS, 2 * CM], F32R)
        wx = sb("wx", [P, GM * D])
        wxT = wx[:, :].rearrange("p (c n) -> p c n", c=KC)
        wxN = wx[:, :].rearrange("p (g d) -> p g d", g=GM)
        wh = sb("wh", [P, GM, D])
        tE = sb("tE", [P, GM, P])
        lE = sb("lE", [P, GM, P])
        adjM = sb("adjM", [P, GM, P], I32)
        z = sb("z", [P, G * D])
        zN = z[:, :].rearrange("p (g d) -> p g d", g=G)
        qT = sb("qT", [P, KC, C])
        V = sb("V", [P, G, D])
        srcT = sb("srcT", [P, G, H])
        dstT = sb("dstT", [P, G * H])
        u = sb("u", [P, 2, H, P])
        cnt = sb("cnt", [P, G, NLAB])
        oh = u[:, :, :, :].rearrange("p a h n -> p (a h n)").bitcast(BF16).rearrange(
            "p (v g n) -> p v g n", v=NLAB // 2, g=G)
        cntT = u[0:NLAB, 1, 0:G, :].rearrange("p g n -> p (g n)")
        bT = sb("bT", [G * H, P])[:, :]
        N2, TL, N1, N0 = range(4)
        ng = (GM, G, GM, GM)
        st6 = [sb(f"st6{i}", [P, ng[i], 6]) for i in range(4)]
        mv = [sb(f"mv{i}", [P, ng[i], 2]) for i in range(4)]
        ve = [sb(f"ve{i}", [P, ng[i]]) for i in range(4)]
        rstd = [sb(f"rstd{i}", [P, ng[i]]) for i in range(4)]
        nmx = sb("nmx", [P, GM])
        ssum = sb("ssum", [P, GM])
        rsum = sb("rsum", [P, GM])
        nmxT = sb("nmxT", [P, 2, H])
        ssumT = sb("ssumT", [P, G, H])
        rsumT = sb("rsumT", [P, G, H])

        ps = ctx.enter_context(nc.psum_tensor("ps", [P, 8, 512], F32))
        FF1, FF2, YB, XB, SB, TB = 0, 2, 3, 4, 5, 6

        i_stage = [signal(f"i_stage{k}", 1, 16) for k in range(2)]
        i_hi = signal("i_hi")
        i_lo = signal("i_lo")
        i_cols = signal("i_cols")
        i_zero = signal("i_zero")
        i_rows0 = signal("i_rows0", 4)
        i_small = signal("i_small", 14, 16)
        i_tabs = signal("i_tabs", 9, 16)
        i_pool = signal("i_pool")
        i_ident = signal("i_ident")
        i_fold = signal("i_fold")
        i_sum3 = signal("i_sum3")
        i_t3 = signal("i_t3")
        i_w3 = signal("i_w3")
        x_loaded = [signal(f"x_loaded{s}", 1, 16) for s in range(NSTR)]
        adjM_loaded = signal("adjM_loaded", 1, 16)
        neg_part = signal("neg_part")
        neg0_ready = signal("neg0_ready")
        ln0_bn = signal("ln0_bn")
        ln0_mv = signal("ln0_mv")
        ln0_ve = signal("ln0_ve")
        ln0_rstd = signal("ln0_rstd")
        ln0_z = signal("ln0_z")
        xc_ready = signal("xc_ready")
        xT_filled = signal("xT_filled")
        xT_ready = signal("xT_ready")
        rows_filled = signal("rows_filled")
        rowa_ready = signal("rowa_ready")
        rowb_ready = signal("rowb_ready")
        s_filled = signal("s_filled")
        t_ready = signal("t_ready")
        l_ready = signal("l_ready")
        m_ready = signal("m_ready")
        e_ready = signal("e_ready")
        r_ready = signal("r_ready")
        eT_filled = signal("eT_filled")
        eT_ready = signal("eT_ready")
        agg_filled = signal("agg_filled")
        hp_ready = signal("hp_ready")
        n1_bn = signal("n1_bn")
        n1_mv = signal("n1_mv")
        n1_ve = signal("n1_ve")
        n1_rstd = signal("n1_rstd")
        hn_ready = signal("hn_ready")
        hnT_filled = signal("hnT_filled")
        hT_ready = signal("hT_ready", KC)
        hTh_ready = signal("hTh_ready")
        hTl_ready = signal("hTl_ready")
        ff1_filled = signal("ff1_filled", FP)
        gf_ready = signal("gf_ready", FP)
        gh_ready = signal("gh_ready", FP)
        gl_ready = signal("gl_ready", FP)
        g_used = signal("g_used", FP)
        yT_ready = signal("yT_ready", KC)
        y_filled = signal("y_filled")
        n2_bn = signal("n2_bn")
        n2_mv = signal("n2_mv")
        n2_ve = signal("n2_ve")
        n2_rstd = signal("n2_rstd")
        xn_ready = signal("xn_ready")
        xg_ready = signal("xg_ready")
        xt_loaded = [signal(f"xt_loaded{r}", 1, 16) for r in range(2)]
        x1_ready = signal("x1_ready", 2)
        adjT_loaded = signal("adjT_loaded", 1, 16)
        neg1_ready = signal("neg1_ready")
        q_bn = signal("q_bn", 3)
        q_mv = signal("q_mv", 3)
        q_ve = signal("q_ve", 3)
        q_rstd = signal("q_rstd", 3)
        q_z = signal("q_z", 3)
        q_zT = signal("q_zT", 3 * KC)
        q_T = signal("q_T", 3 * KC)
        v1_filled = signal("v1_filled", 2)
        v1_ready = signal("v1_ready", 2)
        r1_filled = signal("r1_filled")
        r1a_ready = signal("r1a_ready")
        r1b_ready = signal("r1b_ready")
        s1_filled = signal("s1_filled")
        t1_ready = signal("t1_ready")
        l1_ready = signal("l1_ready")
        m1_ready = signal("m1_ready")
        e1_ready = signal("e1_ready")
        d1_ready = signal("d1_ready")
        eT1_filled = signal("eT1_filled")
        eT1_ready = signal("eT1_ready")
        agg1_filled = signal("agg1_filled", 2)
        mn_ready = signal("mn_ready")
        ex_ready = signal("ex_ready")
        em_ready = signal("em_ready")
        el_ready = signal("el_ready")
        x2_ready = signal("x2_ready")
        v2_filled = signal("v2_filled", G)
        v2_ready = signal("v2_ready", G)
        a2_ready = signal("a2_ready", G)
        b2_filled = signal("b2_filled")
        b2_ready = signal("b2_ready")
        b2_stored = signal("b2_stored", 1, 16)
        b2_spread = [signal(f"b2_spread{k}", 2, 16) for k in range(2)]
        u2_ready = signal("u2_ready", G)
        l2_ready = signal("l2_ready", G)
        m2_ready = signal("m2_ready", G)
        e2_ready = signal("e2_ready", G)
        eT2_filled = signal("eT2_filled", 2 * G)
        eT2_ready = signal("eT2_ready", 2 * G)
        agg2_filled = signal("agg2_filled", G)
        agg2_ready = signal("agg2_ready", G)
        d2_ready = signal("d2_ready")
        back_filled = signal("back_filled", 2)
        bn_ready = signal("bn_ready", 2)
        x3_ready = signal("x3_ready")
        oh_ready = signal("oh_ready", 2)
        sum1_ready = signal("sum1_ready", 2)
        sum2_ready = signal("sum2_ready", 2)
        sum3_ready = signal("sum3_ready", 2)
        cnt_ready = signal("cnt_ready", 2)
        cntT_filled = signal("cntT_filled")
        cntT_ready = signal("cntT_ready")
        res_ready = signal("res_ready")
        o_filled = signal("o_filled", 2)
        o_ready = signal("o_ready", 2)
        o_stored = signal("o_stored", 1, 16)

        EARLIER = 4
        pieces = []
        for l in range(L):
            w1 = W1[l].rearrange("(c p) f -> p c f", p=P)
            w2 = W2[l].rearrange("(c p) d -> p c d", p=P)
            for c in range(KC):
                pieces.append((W1h[:, l, c, :], W1l[:, l, c, :], w1[:, c, :], F // 1))
            for c in range(0, FC, EARLIER):
                pieces.append((W2h[:, l, c:c + EARLIER, :].rearrange("p c d -> p (c d)"),
                               W2l[:, l, c:c + EARLIER, :].rearrange("p c d -> p (c d)"),
                               w2[:, c:c + EARLIER, :], None))
        PPL = len(pieces) // L
        stage = [u[:, k, :, :].rearrange("p h n -> p (h n)") for k in range(2)]
        abc = qT[:, 0, :]
        wabc = qT[:, 1, :]
        raw3 = z[:, :].rearrange("p (d i) -> p d i", d=4)
        prod = V[:, :, :].rearrange("p g n -> p (g n)")[:, 0:D]
        prod2 = V[:, :, :].rearrange("p g n -> p (g n)")[:, D:2 * D]
        prod3 = V[:, 2:4, :]

        def graphs(t, g0, n=G):
            return t[bass.ds(g0, n)].rearrange("g p d -> p g d")

        class Chain:

            def __init__(self, it, o):
                self.it, self.o = it, o
                self.l, self.s, self.group = o // NSTR % L, o % NSTR, o // SL
                self.n = Seg(it, SL, o)
                self.new = self.l == 0
                self.post = exists(it, o - NSTR)
                self.attend = exists(it, o)
                self.before = Seg(it, SL, o - NSTR)
                self.before_l = (self.l - 1) % L
                self.n0 = Seg(it, NSTR, NSTR * self.group + self.s)
                self.xt = self.s // 2
                self.half = slice(self.s % 2 * GM, (self.s % 2 + 1) * GM)
                self.done = Seg(it, NSTR, NSTR * (self.group - 1) + self.s)
                self.q = Seg(it, 2, 2 * (self.group - 1) + self.xt)

        def exists(it, o):
            return not isinstance(it, int) or 0 <= it * SL + o < NSEG

        def schedule(eng, init, ff, main, tail):
            def slot(it, o):
                third = tail_phase(it, o)
                for h in range(T):
                    if isinstance(it, int) and it == 0:
                        init(h, o)
                    for back in (1, 0):
                        if exists(it, o - back):
                            ff(h + T * back, it, o - back)
                    for j in reversed(range(LEAD)):
                        if exists(it, o + LEAD - j) or exists(it, o + LEAD - j - NSTR):
                            if not isinstance(it, int) or it * SL + o + LEAD - j >= 0:
                                main(h + T * j, Chain(it, o + LEAD - j))
                    if third:
                        phase, tit, r = third
                        tail(h + T * phase, tit, r)

            for o in range(-LEAD, 0):
                slot(0, o)
            for o in range(SL):
                slot(0, o)
            with eng.Fori(1, ITS - 1) as it:
                for o in range(SL):
                    slot(it, o)
            for o in range(SL):
                slot(ITS - 1, o)
            for o in range(SL, R0_AT + 2 * PHASES):
                slot(ITS - 1, o)

        R0_AT = SL - 2

        def piece_at(h, o):
            if h in PIECES_AT and 0 <= o + 2 < len(pieces) // 2:
                return 2 * (o + 2) + PIECES_AT.index(h)
            return None

        def tail_phase(it, o):
            if o >= SL and isinstance(it, int):
                it, o = it + 1, o - SL
            d = o - R0_AT
            if d < 0:
                it, d = it - 1, d + SL
            if isinstance(it, int) and (it < 0 or it >= ITS):
                return None
            return d % PHASES, it, d // PHASES

        def first_group(it, r):
            return isinstance(it, int) and it == 0 and r == 0

        def seg2(it, s):
            return Seg(it, 2, s)

        def seg1(it):
            return Seg(it, 1, 0)

        block = ctx.enter_context(nc.Block())

        @block.sync
        def _(sp):
            def load_x(it, group, s):
                sp.dma_start(xc[s][:, :, :], graphs(x, it * (NSTR * GM) + (group * NSTR + s) * GM,
                                                    GM)).then_inc(x_loaded[s].sem, 16)

            def load_adjM(it, group, s):
                if exists(it, group * SL + s - 1):
                    sp.wait_ge(*neg0_ready(Seg(it, NSTR, group * NSTR + s - 1), 1))
                sp.dma_start(adjM[:, :, :], graphs(adj, it * (NSTR * GM) + (group * NSTR + s) * GM,
                                                   GM)).then_inc(adjM_loaded.sem, 16)

            def load_piece(k):
                if k >= 2:
                    sp.wait_ge(*i_lo(0, k - 1))
                src = pieces[k][2]
                dst = stage[k % 2]
                if len(src.shape) == 3:
                    dst = dst.rearrange("p (c d) -> p c d", d=D)
                sp.dma_start(dst, src).then_inc(i_stage[k % 2].sem, 16)

            def load_adjT(it, r):
                if not first_group(it, r):
                    sp.wait_ge(*oh_ready(Seg(it, 2, r - 1), 2))
                    sp.wait_ge(*neg1_ready(Seg(it, 2, r - 1), 1))
                sp.dma_start(adjT[:, :, :], graphs(adj, it * (2 * G) + r * G)).then_inc(adjT_loaded.sem, 16)

            def load_xt(it, r, first):
                if not first:
                    sp.wait_ge(*res_ready(Seg(it, 2, r - 2), 1))
                sp.dma_start(xt[r][:, :, :], graphs(x, it * (2 * G) + r * G)).then_inc(xt_loaded[r].sem, 16)

            def spread(q, g):
                if g >= 2:
                    sp.wait_ge(*eT2_filled(q, 2 * (g - 1)))
                src = scratch[g * H:(g + 1) * H, :].rearrange("(a h) n -> a (h n)", a=1)
                sp.dma_start(u[:, g % 2, :, :].rearrange("p h n -> p (h n)"),
                             src.to_broadcast([P, H * P])).then_inc(b2_spread[g % 2].sem, 16)

            load_x(0, 0, 0)
            load_adjM(0, 0, 0)
            for k in range(2):
                load_x(0, 0, 1 + k)
                load_piece(k)
            load_x(0, 0, 3)

            def init(h, o):
                if h == 1 and 0 <= o + 2 < len(pieces) // 2 - 1:
                    load_piece(2 * (o + 3))
                    load_piece(2 * (o + 3) + 1)
                if h == 0 and o == R0_AT - 2:
                    load_adjT(0, 0)

            def ff(h, it, o):
                first = isinstance(it, int) and it == 0
                if h != 0:
                    return
                if o == 4:
                    load_xt(it, 0, first)
                if o == 10:
                    load_xt(it, 1, first)

            def main(h, c):
                if h == 0:
                    ahead = Chain(c.it, c.o + 2)
                    if ahead.new and ahead.attend and ahead.post:
                        sp.wait_ge(*hp_ready(ahead.before, 1))
                        load_x(ahead.it, ahead.group, ahead.s)
                    ahead = Chain(c.it, c.o + 1)
                    if ahead.new and ahead.attend:
                        load_adjM(ahead.it, ahead.group, ahead.s)

            def tail(h, it, r):
                q = seg2(it, r)
                if h == G2_BT_COPY // T * T:
                    sp.wait_ge(*b2_ready(q, 1))
                    sp.dma_start(scratch, bT).then_inc(b2_stored.sem, 16)
                    sp.wait_ge(*b2_stored(q, 1))
                    spread(q, 0)
                    spread(q, 1)
                if h == G2_ET[0] // T * T + 1:
                    spread(q, 2)
                if h == G2_ET[1] // T * T + 2:
                    spread(q, 3)
                if h == 5 * T + 3:
                    if r == 0:
                        load_adjT(it, 1)
                    elif not (isinstance(it, int) and it == ITS - 1):
                        load_adjT(it + 1, 0)
                    sp.wait_ge(*o_ready(q, 2))
                    sp.dma_start(graphs(out, it * (2 * G) + r * G), V[:, :, 0:D]).then_inc(o_stored.sem, 16)

            schedule(sp, init, ff, main, tail)
            sp.wait_ge(*o_stored(seg2(ITS - 1, 1), 1))

        @block.gpsimd
        def _(pool):
            pool.memset(identf[:, :], 0.0).then_inc(i_pool.sem, 1)
            pool.memset(identb[:, :], 0.0).then_inc(i_pool.sem, 1)
            pool.memset(offdiag[:, :], 1.0).then_inc(i_pool.sem, 1)
            pool.memset(mhalf[:, :], -0.5).then_inc(i_pool.sem, 1)
            pool.memset(epsG[:, :], EPS).then_inc(i_pool.sem, 1)
            pool.wait_ge(*i_pool(0, 5))
            for t, fill in ((identf, 1.0), (identb, 1.0), (offdiag, 0.0)):
                pool.affine_select(out=t[:, :], in_=t[:, :], compare_op=ALU.not_equal, fill=fill,
                                   base=0, pattern=[[-1, P]], channel_multiplier=1).then_inc(i_ident.sem, 1)
            pool.wait_ge(*i_ident(0, 3))
            tabs = [
                (gamma2[:, :, :].rearrange("p l d -> p (l d)"),
                 g2.rearrange("(a l) d -> a (l d)", a=1).to_broadcast([P, L * D])),
                (betab2[:, :, :].rearrange("p l d -> p (l d)"),
                 beta2.rearrange("(a l) d -> a (l d)", a=1).to_broadcast([P, L * D])),
                (b1T[:, :, :], b1.rearrange("l (c p) -> p l c", p=P)),
                (b2T[:, :, :], b2.rearrange("l (c p) -> p l c", p=P)),
                (g1T[:, :, :], g1.rearrange("l (c p) -> p l c", p=P)),
                (beta1T[:, :, :], beta1.rearrange("l (c p) -> p l c", p=P)),
                (batt[:, :], L2_ba.rearrange("(a h) -> a h", a=1).to_broadcast([P, H])),
                (attb[:, :], attn_b.rearrange("(a l) -> a l", a=1)),
                (Wg1[:, :, :], L1_W.rearrange("(c p) f -> p c f", p=P)),
            ]
            assert len(tabs) == i_tabs.per
            for dst, src in tabs:
                pool.dma_start(dst, src, allow_slow_non_contiguous=True).then_inc(i_tabs.sem, 16)
            def carry_waits():
                pool.tensor_tensor(idleP[:, :], mhalf[:, :], mhalf[:, :], ALU.mult)

            def mask0(c):
                pool.wait_ge(*adjM_loaded(c.n0, 1))
                if c.post:
                    pool.wait_ge(*s_filled(c.before, 1))
                carry_waits()
                pool.tensor_scalar(neg0[c.s][:, :, :], adjM[:, :, :], 0, MASKED, ALU.is_le,
                                   ALU.mult).then_inc(neg_part.sem, 1)
                pool.wait_ge(*neg_part(c.n0, 1))
                pool.tensor_tensor(neg0[c.s][:, :, :], neg0[c.s][:, :, :],
                                   offdiag[:, :].rearrange("p (a n) -> p a n", a=1).to_broadcast([P, GM, P]),
                                   ALU.mult).then_inc(neg0_ready.sem, 1)

            def rsqrt(i, mv_ready, ve_ready, out_ready, seg, k=1):
                pool.wait_ge(*mv_ready(seg, k))
                pool.tensor_tensor(ve[i][:, :], mv[i][:, :, 1], epsG[:, 0:ng[i]], ALU.add).then_inc(ve_ready.sem, 1)
                pool.wait_ge(*ve_ready(seg, k))
                pool.tensor_tensor(rstd[i][:, :], ve[i][:, :], mhalf[:, 0:ng[i]], ALU.pow).then_inc(out_ready.sem, 1)

            def main(h, c):
                if h == M_N2_RS and c.post:
                    rsqrt(N2, n2_mv, n2_ve, n2_rstd, c.before)
                if h == M_X1 and c.post and c.new:
                    pool.wait_ge(*xg_ready(c.done, 1))
                    pool.wait_ge(*xt_loaded[c.xt](Seg(c.it, 1, c.group - 1), 1))
                    pool.tensor_tensor(xt[c.xt][:, c.half, :], xt[c.xt][:, c.half, :], wxN,
                                       ALU.add).then_inc(x1_ready.sem, 1)
                if not c.attend:
                    return
                if h == M_LN0_RS and c.new:
                    rsqrt(N0, ln0_mv, ln0_ve, ln0_rstd, c.n0)
                if h == M_MASK and c.new:
                    mask0(c)
                if h == M_N1_RS:
                    rsqrt(N1, n1_mv, n1_ve, n1_rstd, c.n)
                if h == M_HTL:
                    pool.wait_ge(*hTh_ready(c.n, 1))
                    pool.tensor_tensor(hTl[c.s][:, :, :], hT[c.s][:, :, :], hTh[c.s][:, :, :].bitcast(F32),
                                       ALU.subtract).then_inc(hTl_ready.sem, 1)

            def tail(h, it, r):
                q = seg2(it, r)
                if h == 0:
                    pool.wait_ge(*adjT_loaded(q, 1))
                    if not first_group(it, r):
                        pool.wait_ge(*o_filled(Seg(it, 2, r - 1), 2))
                    carry_waits()
                    pool.tensor_scalar(neg1[:, :, :], adjT[:, :, :], 0, MASKED, ALU.is_le,
                                       ALU.mult).then_inc(neg1_ready.sem, 1)
                for stage_no in (1, 2, 3):
                    if h == N_RS[stage_no - 1]:
                        rsqrt(TL, q_mv, q_ve, q_rstd, q, stage_no)

            def ff(h, it, o):
                n, before = Seg(it, SL, o), Seg(it, SL, o - 1)
                if h in GL_AT:
                    p = GL_AT.index(h)
                    pool.wait_ge(*gh_ready(n, p + 1))
                    pool.tensor_tensor(gl[:, (FP * o + p) % NS, :], gf[:, (FP * o + p) % NG, :],
                                       gh[:, (FP * o + p) % NS, :].bitcast(F32),
                                       ALU.subtract).then_inc(gl_ready.sem, 1)

            schedule(pool, lambda h, o: None, ff, main, tail)

        @block.scalar
        def _(act):
            act.wait_ge(*i_zero(0, 4))
            small = []
            for l in range(L):
                for t in range(2):
                    w = attn_w[l, t * D:(t + 1) * D].rearrange("(c p) -> p c", p=P)
                    small.append((wrow0[:, l, :, 32 * t], w))
            small += [
                (Wg2[:, :, 0:D], L2_Wp.rearrange("(c p) f -> p c f", p=P)),
                (abc, L1_a.rearrange("(a k) o -> a (k o)", a=1).to_broadcast([P, 2 * D])),
                (wabc, L2_Wa.rearrange("(a h) k -> a (h k)", a=1).to_broadcast([P, H * 2 * DH])),
            ]
            for d in range(2):
                for oc in range(KC):
                    small.append((raw3[:, 2 * d + oc, :], L3_W[d, oc * P:(oc + 1) * P, :]))
            small.append((table[0:NLAB, :], L3_bias))
            assert len(small) == i_small.per, len(small)
            for dst, src in small:
                act.dma_start(dst, src, allow_slow_non_contiguous=True).then_inc(i_small.sem, 16)

            def init(h, o):
                k = piece_at(h, o)
                if k is not None:
                    act.wait_ge(*i_stage[k % 2](0, k // 2 + 1))
                    act.activation(pieces[k][0], stage[k % 2], ACT.Copy).then_inc(i_hi.sem, 1)
                if (o, h) == (-LEAD, M_XT_COPY):
                    act.wait_ge(*i_tabs(0, i_tabs.per))
                if (o, h) == (6, 12):
                    for c in range(KC):
                        act.wait_ge(*i_t3(0, c + 1))
                        act.activation(Wg3[:, c, :], ps[:, TB + c, 0:D], ACT.Copy).then_inc(i_w3.sem, 1)

            def main(h, c):
                if not c.attend:
                    return
                if h == M_XT_COPY:
                    act.wait_ge(*xT_filled(c.n, 1))
                    if c.post and c.new:
                        act.wait_ge(*x1_ready(c.q, c.s % 2 + 1))
                    act.activation(wx[:, :], ps[:, XB, :], ACT.Copy).then_inc(xT_ready.sem, 1)
                if h == M_ROW_COPY:
                    act.wait_ge(*rows_filled(c.n, 1))
                    act.activation(rowL[0:1, 0:CM], ps[0:1, XB, 0:CM], ACT.Identity,
                                   bias=attb[0:1, c.l:c.l + 1]).then_inc(rowa_ready.sem, 1)
                if h == M_T:
                    act.wait_ge(*s_filled(c.n, 1))
                    act.activation(tE[:, :, :].rearrange("p g n -> p (g n)"), ps[:, SB, 0:CM], ACT.Copy,
                                   scale=SLOPE).then_inc(t_ready.sem, 1)
                if h == M_EXP:
                    act.wait_ge(*m_ready(c.n, 1))
                    for g in range(GM):
                        i = act.activation(tE[:, g, :], lE[:, g, :], ACT.Exp, bias=nmx[:, g:g + 1],
                                           accum_out=ssum[:, g:g + 1])
                    i.then_inc(e_ready.sem, 1)
                if h == M_ET_COPY:
                    act.wait_ge(*eT_filled(c.n, 1))
                    act.activation(lE[:, :, :].rearrange("p g n -> p (g n)"), ps[:, SB, 0:CM],
                                   ACT.Copy).then_inc(eT_ready.sem, 1)
                if h == M_HT_COPY:
                    act.wait_ge(*hnT_filled(c.n, 1))
                    for k in range(KC):
                        act.activation(hT[c.s][:, k, :], ps[:, YB, k * CM:(k + 1) * CM], ACT.Identity,
                                       scale=g1T[:, c.l, k:k + 1],
                                       bias=beta1T[:, c.l, k:k + 1]).then_inc(hT_ready.sem, 1)

            def tail(h, it, s):
                q = seg2(it, s)
                for stage_no in (1, 2, 3):
                    if h == N_ZT_COPY[stage_no - 1]:
                        for c in range(KC):
                            act.wait_ge(*q_zT(q, KC * (stage_no - 1) + c + 1))
                            act.activation(qT[:, c, :], ps[:, TB + c, :], ACT.Relu).then_inc(q_T.sem, 1)
                if h == G1_V_COPY:
                    for c in range(2):
                        act.wait_ge(*v1_filled(q, c + 1))
                        act.activation(V[:, 2 * c:2 * c + 2, 0:D],
                                       ps[:, TB + c, :].rearrange("p (g d) -> p g d", g=2),
                                       ACT.Copy).then_inc(v1_ready.sem, 1)
                if h == G1_ROW_COPY:
                    act.wait_ge(*r1_filled(q, 1))
                    act.activation(rowL[64:65, :], ps[64:65, TB, :], ACT.Copy).then_inc(r1a_ready.sem, 1)
                if h == G1_T:
                    act.wait_ge(*s1_filled(q, 1))
                    act.wait_ge(*cnt_ready(q, 2))
                    act.activation(u[:, 0, 0:G, :].rearrange("p g n -> p (g n)"), ps[:, TB + 1, :],
                                   ACT.Copy, scale=SLOPE).then_inc(t1_ready.sem, 1)
                if h == G1_EXP:
                    act.wait_ge(*m1_ready(q, 1))
                    for g in range(G):
                        i = act.activation(u[:, 0, g, :], u[:, 0, G + g, :], ACT.Exp,
                                           bias=nmxT[:, 0, g:g + 1], accum_out=ssumT[:, 0, g:g + 1])
                    i.then_inc(e1_ready.sem, 1)
                if h == G1_ET_COPY:
                    act.wait_ge(*eT1_filled(q, 1))
                    act.activation(z[:, 0:C], ps[:, TB, :], ACT.Copy).then_inc(eT1_ready.sem, 1)
                if h == G1_ELU_EXP:
                    act.wait_ge(*mn_ready(q, 1))
                    u1 = u[:, 1, :, :].rearrange("p h n -> p (h n)")
                    act.activation(u1, u1, ACT.Exp).then_inc(ex_ready.sem, 1)
                if h in G2_V_COPY:
                    g = G2_V_COPY.index(h)
                    act.wait_ge(*v2_filled(q, g + 1))
                    act.activation(V[:, g, :], ps[:, TB + g % 2, 0:D], ACT.Copy).then_inc(v2_ready.sem, 1)
                if h == G2_BT_COPY:
                    act.wait_ge(*b2_filled(q, 1))
                    act.activation(bT, ps[0:G * H, TB, 0:P], ACT.Copy).then_inc(b2_ready.sem, 1)
                for g in range(G):
                    if h == G2_EXP[g]:
                        act.wait_ge(*m2_ready(q, g + 1))
                        for hd in range(H):
                            i = act.activation(u[:, g % 2, hd, :], u[:, g % 2, hd, :], ACT.Exp,
                                               bias=nmxT[:, g % 2, hd:hd + 1], accum_out=ssumT[:, g, hd:hd + 1])
                        i.then_inc(e2_ready.sem, 1)
                    if h == G2_ET_COPY[g]:
                        for c in range(2):
                            act.wait_ge(*eT2_filled(q, 2 * g + c + 1))
                            act.activation(z[:, c * C:(c + 1) * C], ps[:, TB + c, :], ACT.Copy).then_inc(eT2_ready.sem, 1)
                    if h == G2_AGG_COPY[g]:
                        act.wait_ge(*agg2_filled(q, g + 1))
                        act.activation(qT[:, :, g * P:(g + 1) * P],
                                       ps[:, TB, 0:2 * P].rearrange("p (c n) -> p c n", c=2),
                                       ACT.Copy).then_inc(agg2_ready.sem, 1)
                if h == G3_CNT_COPY:
                    act.wait_ge(*cntT_filled(q, 1))
                    act.activation(cntT, ps[0:NLAB, TB, :], ACT.Copy).then_inc(cntT_ready.sem, 1)

            def ff(h, it, o):
                n, before, l = Seg(it, SL, o), Seg(it, SL, o - 1), o // NSTR % L
                if h in GELU_AT:
                    p = GELU_AT.index(h)
                    act.wait_ge(*ff1_filled(n, p + 1))
                    if p >= NG:
                        act.wait_ge(*gl_ready(n, p + 1 - NG))
                    elif exists(it, o - 1):
                        act.wait_ge(*gl_ready(before, FP + p + 1 - NG))
                    for c in range(2):
                        i = act.activation(gf[:, (FP * o + p) % NG, c * CM:(c + 1) * CM],
                                           ps[:, FF1 + p % 2, c * CM:(c + 1) * CM], ACT.Gelu,
                                           bias=b1T[:, l, 2 * p + c:2 * p + c + 1])
                    i.then_inc(gf_ready.sem, 1)

            schedule(act, init, ff, main, tail)

        @block.vector
        def _(dve):
            dve.memset(wrow0[:, :, :, :], 0.0).then_inc(i_zero.sem, 1)
            dve.memset(wrow1[:, :, :], 0.0).then_inc(i_zero.sem, 1)
            dve.memset(rowL[:, :], 0.0).then_inc(i_zero.sem, 1)
            dve.memset(rowR[:, :], 0.0).then_inc(i_zero.sem, 1)
            dve.memset(idleV[:, :], 0.0)
            dve.wait_ge(*i_zero(0, 4))
            for p in (0, 64):
                dve.memset(rowR[p:p + 1, :], 1.0).then_inc(i_rows0.sem, 1)
                dve.memset(rowL[p + 32:p + 33, :], 1.0).then_inc(i_rows0.sem, 1)

            def stats(i, src, bn_ready_, mv_ready, seg, k=1):
                for g in range(ng[i]):
                    ins = dve.bn_stats(st6[i][:, g, :], src(g))
                ins.then_inc(bn_ready_.sem, 1)
                dve.wait_ge(*bn_ready_(seg, k))
                dve.tensor_copy(idleV[:, 1:2], idleV[:, 0:1])
                for g in range(ng[i]):
                    ins = dve.bn_aggr(mv[i][:, g, :], st6[i][:, g, :])
                ins.then_inc(mv_ready.sem, 1)

            def normalise(i, dst, src, rstd_ready, done, seg, k=1):
                dve.wait_ge(*rstd_ready(seg, k))
                for g in range(ng[i]):
                    ins = dve.tensor_scalar(dst(g), src(g), mv[i][:, g, 0:1], rstd[i][:, g:g + 1],
                                            ALU.subtract, ALU.mult)
                ins.then_inc(done.sem, 1)

            yp = lambda g: ps[:, YB, g * D:(g + 1) * D]

            def main(h, c):
                if c.post:
                    l, s = c.before_l, c.s
                if h == M_Y and c.post:
                    dve.wait_ge(*g_used(c.before, FP))
                    for k in range(KC):
                        dve.scalar_tensor_tensor(hT[s][:, k, :], ps[:, FF2, k * CM:(k + 1) * CM],
                                                 b2T[:, l, k:k + 1], hT[s][:, k, :], ALU.add,
                                                 ALU.add).then_inc(yT_ready.sem, 1)
                if h == M_N2 and c.post:
                    dve.wait_ge(*y_filled(c.before, 1))
                    stats(N2, yp, n2_bn, n2_mv, c.before)
                if h == M_XN and c.post:
                    dve.wait_ge(*n2_mv(c.before, 1))
                    for g in range(GM):
                        i = dve.scalar_tensor_tensor(wxN[:, g, :], yp(g), mv[N2][:, g, 0:1], gamma2[:, l, :],
                                                     ALU.subtract, ALU.mult)
                    i.then_inc(xn_ready.sem, 1)
                if h == M_XB and c.post:
                    dve.wait_ge(*n2_rstd(c.before, 1))
                    dve.wait_ge(*xn_ready(c.before, 1))
                    for g in range(GM):
                        dst = wxN[:, g, :] if c.new else xc[s][:, g, :]
                        i = dve.scalar_tensor_tensor(dst, wxN[:, g, :], rstd[N2][:, g:g + 1], betab2[:, l, :],
                                                     ALU.mult, ALU.add)
                    i.then_inc((xg_ready if c.new else xc_ready).sem, 1)
                if not c.attend:
                    return
                if h == M_LN0 and c.new:
                    dve.wait_ge(*x_loaded[c.s](Seg(c.it, 1, c.group), 1))
                    stats(N0, lambda g: xc[c.s][:, g, :], ln0_bn, ln0_mv, c.n0)
                if h == M_Z0 and c.new:
                    normalise(N0, lambda g: xc[c.s][:, g, :], lambda g: xc[c.s][:, g, :], ln0_rstd,
                              ln0_z, c.n0)
                    dve.wait_ge(*ln0_z(c.n0, 1))
                    dve.tensor_scalar(xc[c.s][:, :, :], xc[c.s][:, :, :], 0.0, None,
                                      ALU.max).then_inc(xc_ready.sem, 1)
                if h == M_ROW_COPY:
                    dve.wait_ge(*rows_filled(c.n, 1))
                    dve.tensor_copy(rowR[32:33, 0:CM], ps[32:33, XB, 0:CM]).then_inc(rowb_ready.sem, 1)
                if h == M_MAX:
                    flat = lambda t: t[:, :, :].rearrange("p g n -> p (g n)")
                    dve.wait_ge(*t_ready(c.n, 1))
                    dve.tensor_tensor(flat(lE), ps[:, SB, 0:CM], flat(tE), ALU.max).then_inc(l_ready.sem, 1)
                    dve.wait_ge(*l_ready(c.n, 1))
                    dve.tensor_reduce(nmx[:, :], lE[:, :, :], AX.X, ALU.max, negate=True).then_inc(m_ready.sem, 1)
                if h == M_RECIP:
                    dve.wait_ge(*e_ready(c.n, 1))
                    dve.reciprocal(rsum[:, :], ssum[:, :]).then_inc(r_ready.sem, 1)
                if h == M_HP:
                    dve.wait_ge(*r_ready(c.n, 1))
                    dve.wait_ge(*agg_filled(c.n, 1))
                    for g in range(GM):
                        i = dve.scalar_tensor_tensor(wh[:, g, :], ps[:, SB, g * D:(g + 1) * D],
                                                     rsum[:, g:g + 1], xc[c.s][:, g, :], ALU.mult, ALU.add)
                    i.then_inc(hp_ready.sem, 1)
                    dve.wait_ge(*hp_ready(c.n, 1))
                    stats(N1, lambda g: wh[:, g, :], n1_bn, n1_mv, c.n)
                if h == M_HN:
                    normalise(N1, lambda g: wh[:, g, :], lambda g: wh[:, g, :], n1_rstd, hn_ready, c.n)
                if h == M_HTH:
                    dve.wait_ge(*hT_ready(c.n, KC))
                    dve.tensor_copy(hTh[c.s][:, :, :], hT[c.s][:, :, :]).then_inc(hTh_ready.sem, 1)

            def tail(h, it, s):
                q = seg2(it, s)
                if h in COUNT_AT:
                    part = COUNT_AT.index(h)
                    k = part // 2
                    if part == 0:
                        dve.wait_ge(*adjT_loaded(q, 1))
                        if not first_group(it, s):
                            dve.wait_ge(*o_filled(Seg(it, 2, s - 1), 2))
                    elif part == 2:
                        dve.wait_ge(*cnt_ready(q, 1))
                    for v in range(part % 2 * (NLAB // 4), (part % 2 + 1) * (NLAB // 4)):
                        i = dve.tensor_scalar(oh[:, v, :, :], adjT[:, :, :], k * (NLAB // 2) + v, None,
                                              ALU.is_equal)
                    if part % 2 == 1:
                        i.then_inc(oh_ready.sem, 1)
                if h in TREE_AT:
                    k = TREE_AT.index(h)
                    dve.wait_ge(*oh_ready(q, k + 1))
                    for w, done in ((P // 2, sum1_ready), (P // 4, sum2_ready), (P // 8, sum3_ready)):
                        dve.tensor_tensor(oh[:, :, :, 0:w], oh[:, :, :, 0:w], oh[:, :, :, w:2 * w],
                                          ALU.add).then_inc(done.sem, 1)
                        dve.wait_ge(*done(q, k + 1))
                    dve.tensor_reduce(cnt[:, :, k * (NLAB // 2):(k + 1) * (NLAB // 2)].rearrange("p g v -> p v g"),
                                      oh[:, :, :, 0:P // 8], AX.X, ALU.add).then_inc(cnt_ready.sem, 1)
                for stage_no in (1, 2, 3):
                    if h == N_AT[stage_no - 1]:
                        dve.wait_ge(*(x1_ready(q, 2), x2_ready(q, 1), x3_ready(q, 1))[stage_no - 1])
                        stats(1, lambda g: xt[s][:, g, :], q_bn, q_mv, q, stage_no)
                    if h == N_Z[stage_no - 1]:
                        normalise(1, lambda g: zN[:, g, :], lambda g: xt[s][:, g, :], q_rstd, q_z, q, stage_no)
                if h == G1_ROW_COPY:
                    dve.wait_ge(*r1_filled(q, 1))
                    dve.tensor_copy(rowR[96:97, :], ps[96:97, TB, :]).then_inc(r1b_ready.sem, 1)
                if h == G1_MAX:
                    dve.wait_ge(*t1_ready(q, 1))
                    fl = lambda a: u[:, 0, a * G:(a + 1) * G, :].rearrange("p g n -> p (g n)")
                    dve.tensor_tensor(fl(1), ps[:, TB + 1, :], fl(0), ALU.max).then_inc(l1_ready.sem, 1)
                    dve.wait_ge(*l1_ready(q, 1))
                    dve.tensor_reduce(nmxT[:, 0, 0:G], u[:, 0, G:2 * G, :], AX.X, ALU.max,
                                      negate=True).then_inc(m1_ready.sem, 1)
                if h == G1_RECIP:
                    dve.wait_ge(*e1_ready(q, 1))
                    dve.reciprocal(rsumT[:, 0, 0:G], ssumT[:, 0, 0:G]).then_inc(d1_ready.sem, 1)
                if h == G1_MIN:
                    dve.wait_ge(*d1_ready(q, 1))
                    for g in range(G):
                        if g % 2 == 0:
                            dve.wait_ge(*agg1_filled(q, g // 2 + 1))
                        i = dve.tensor_scalar(u[:, 1, 2 * g:2 * g + 2, :].rearrange("p h n -> p (h n)"),
                                              ps[:, TB + g // 2, (g % 2) * D:(g % 2 + 1) * D],
                                              rsumT[:, 0, g:g + 1], 0.0, ALU.mult, ALU.min)
                    i.then_inc(mn_ready.sem, 1)
                if h == G1_ELU:
                    dve.wait_ge(*ex_ready(q, 1))
                    u1 = u[:, 1, :, :].rearrange("p h n -> p (h n)")
                    dve.tensor_scalar(u1, u1, -1.0, None, ALU.add).then_inc(em_ready.sem, 1)
                    dve.wait_ge(*em_ready(q, 1))
                    for g in range(G):
                        ug = u[:, 1, 2 * g:2 * g + 2, :].rearrange("p h n -> p (h n)")
                        i = dve.scalar_tensor_tensor(ug, ps[:, TB + g // 2, (g % 2) * D:(g % 2 + 1) * D],
                                                     rsumT[:, 0, g:g + 1], ug, ALU.mult, ALU.max)
                    i.then_inc(el_ready.sem, 1)
                    dve.wait_ge(*el_ready(q, 1))
                    xf = xt[s][:, :, :].rearrange("p g d -> p (g d)")
                    dve.tensor_tensor(xf, xf, u1, ALU.add).then_inc(x2_ready.sem, 1)
                if h in G2_V_COPY:
                    g = G2_V_COPY.index(h)
                    dve.wait_ge(*v2_ready(q, g + 1))
                    dve.tensor_copy(dstT[:, g * H:(g + 1) * H], ps[:, TB + g % 2, D + H:D + 2 * H])
                    dve.tensor_tensor(srcT[:, g, :], ps[:, TB + g % 2, D:D + H], batt[:, :],
                                      ALU.add).then_inc(a2_ready.sem, 1)
                if h in G2_SUM:
                    g = G2_SUM.index(h)
                    if g == 0:
                        dve.wait_ge(*a2_ready(q, G))
                    dve.wait_ge(*b2_spread[g % 2](q, g // 2 + 1))
                    for hd in range(H):
                        i = dve.scalar_tensor_tensor(u[:, g % 2, hd, :], u[:, g % 2, hd, :],
                                                     srcT[:, g, hd:hd + 1], neg1[:, g, :],
                                                     ALU.add, ALU.add)
                    i.then_inc(u2_ready.sem, 1)
                if h in G2_LEAKY:
                    g = G2_LEAKY.index(h)
                    dve.wait_ge(*u2_ready(q, g + 1))
                    ug = u[:, g % 2, :, :].rearrange("p h n -> p (h n)")
                    dve.scalar_tensor_tensor(ug, ug, SLOPE, ug, ALU.mult, ALU.max).then_inc(l2_ready.sem, 1)
                if h in G2_MAX:
                    g = G2_MAX.index(h)
                    dve.wait_ge(*l2_ready(q, g + 1))
                    if g >= 2:
                        dve.wait_ge(*e2_ready(q, g - 1))
                    dve.tensor_reduce(nmxT[:, g % 2, :], u[:, g % 2, :, :], AX.X, ALU.max,
                                      negate=True).then_inc(m2_ready.sem, 1)
                if h == G2_X3:
                    dve.wait_ge(*e2_ready(q, G))
                    dve.reciprocal(rsumT[:, :, :], ssumT[:, :, :]).then_inc(d2_ready.sem, 1)
                    dve.wait_ge(*d2_ready(q, 1))
                    for c in range(2):
                        dve.wait_ge(*back_filled(q, c + 1))
                        dve.tensor_tensor(z[:, c * C:(c + 1) * C].rearrange("p (g h k) -> p (g h) k", g=2, h=H),
                                          ps[:, TB + c, :].rearrange("p (g h k) -> p (g h) k", g=2, h=H),
                                          rsumT[:, 2 * c:2 * c + 2, :].rearrange("p g (h a) -> p (g h) a", a=1)
                                          .to_broadcast([P, 2 * H, DH]), ALU.mult).then_inc(bn_ready.sem, 1)
                    dve.wait_ge(*bn_ready(q, 2))
                    xf = xt[s][:, :, :].rearrange("p g d -> p (g d)")
                    dve.scalar_tensor_tensor(xf, z[:, :], 0.0, xf, ALU.max, ALU.add).then_inc(x3_ready.sem, 1)
                if h == G3_RES:
                    xf = xt[s][:, :, :].rearrange("p g d -> p (g d)")
                    dve.wait_ge(*q_zT(q, 3 * KC))
                    dve.scalar_tensor_tensor(z[:, :], z[:, :], 0.0, xf, ALU.max, ALU.add).then_inc(res_ready.sem, 1)
                if h == G3_SUM:
                    dve.wait_ge(*res_ready(q, 1))
                    for c in range(2):
                        dve.wait_ge(*o_filled(q, c + 1))
                        dve.tensor_tensor(V[:, 2 * c:2 * c + 2, 0:D],
                                          ps[:, TB + c, :].rearrange("p (g d) -> p g d", g=2),
                                          zN[:, 2 * c:2 * c + 2, :], ALU.add).then_inc(o_ready.sem, 1)

            def init(h, o):
                k = piece_at(h, o)
                if k is not None:
                    dve.wait_ge(*i_hi(0, k + 1))
                    dve.tensor_tensor(pieces[k][1], stage[k % 2], pieces[k][0].bitcast(F32),
                                      ALU.subtract).then_inc(i_lo.sem, 1)
                if (o, h) == (0, 0):
                    dve.wait_ge(*i_tabs(0, i_tabs.per))
                if (o, h) == (4, 12):
                    dve.wait_ge(*i_small(0, i_small.per))
                    for c in range(KC):
                        for t in range(2):
                            dve.tensor_tensor_reduce(prod, Wg1[:, c, :], abc[:, t * D:(t + 1) * D], 1.0, 0.0,
                                                     ALU.mult, ALU.add,
                                                     wrow1[:, c, 32 * t:32 * t + 1]).then_inc(i_fold.sem, 1)
                            wa = wabc.rearrange("p (h t k) -> p h t k", h=H, t=2)[:, :, t, :]
                            dve.tensor_tensor(prod2.rearrange("p (h k) -> p h k", h=H),
                                              Wg2[:, c, 0:D].rearrange("p (h k) -> p h k", h=H), wa,
                                              ALU.mult).then_inc(i_cols.sem, 1)
                            dve.wait_ge(*i_cols(0, 2 * c + t + 1))
                            dve.tensor_reduce(Wg2[:, c, D + t * H:D + (t + 1) * H],
                                              prod2.rearrange("p (h k) -> p h k", h=H), AX.X,
                                              ALU.add).then_inc(i_fold.sem, 1)
                            dve.wait_ge(*i_fold(0, 4 * c + 2 * t + 2))
                    dve.tensor_tensor(prod3, raw3[:, 0:2, :], raw3[:, 2:4, :], ALU.add).then_inc(i_sum3.sem, 1)

            def ff(h, it, o):
                n, before = Seg(it, SL, o), Seg(it, SL, o - 1)
                if h in GH_AT:
                    p = GH_AT.index(h)
                    dve.wait_ge(*gf_ready(n, p + 1))
                    if p >= NS:
                        dve.wait_ge(*g_used(n, p + 1 - NS))
                    elif exists(it, o - 1):
                        dve.wait_ge(*g_used(before, FP + p + 1 - NS))
                    dve.tensor_copy(gh[:, (FP * o + p) % NS, :], gf[:, (FP * o + p) % NG, :]).then_inc(gh_ready.sem, 1)

            schedule(dve, init, ff, main, tail)

        @block.tensor
        def _(pe):
            def transposes(bank, src, n, done):
                for i in range(n):
                    ins = pe.transpose(ps[:, bank, i * P:(i + 1) * P], src(i), identf[:, :])
                ins.then_inc(done.sem, 1)

            def rows(bank, w, src, base, n, done):
                for c in range(KC):
                    ins = pe.matmul(ps[base:base + 33, bank, 0:n * P], w(c), src[:, c, :], start=(c == 0),
                                    stop=(c == KC - 1))
                ins.then_inc(done.sem, 1)

            def scores(bank, neg, base, n, done):
                pe.matmul(ps[:, bank, 0:n * P], identb[:, :], neg[:, :, :].rearrange("p g n -> p (g n)"),
                          start=True, stop=False, skip_group_check=True)
                for g in range(n):
                    ins = pe.matmul(ps[:, bank, g * P:(g + 1) * P], rowL[base:base + 33, g * P:(g + 1) * P],
                                    rowR[base:base + 33, g * P:(g + 1) * P], start=False, stop=(g == n - 1),
                                    skip_group_check=True)
                ins.then_inc(done.sem, 1)

            def aggregate(bank, eT, v, n, done):
                for c in range(n // 2):
                    for g in (2 * c, 2 * c + 1):
                        ins = pe.matmul(ps[:, bank + c, (g % 2) * D:(g % 2 + 1) * D], eT(g), v(g),
                                        start=True, stop=True)
                    ins.then_inc(done.sem, 1)

            def main(h, c):
                it, o = c.it, c.o
                if h == M_YBACK and c.post:
                    pe.wait_ge(*yT_ready(c.before, KC))
                    if exists(it, o - 3):
                        pe.wait_ge(*hT_ready(Seg(it, SL, o - 3), KC))
                    else:
                        pe.wait_ge(*xn_ready(Seg(it, SL, o - NSTR - 1), 1))
                    transposes(YB, lambda i: hT[c.s][:, i % KC, i // KC * P:(i // KC + 1) * P], GM * KC,
                               y_filled)
                if not c.attend:
                    return
                if h == M_XT:
                    pe.wait_ge(*xc_ready(c.n, 1))
                    if exists(it, o - 1):
                        pe.wait_ge(*rowa_ready(Seg(it, SL, o - 1), 1))
                        pe.wait_ge(*rowb_ready(Seg(it, SL, o - 1), 1))
                    transposes(XB, lambda i: xc[c.s][:, i % GM, i // GM * P:(i // GM + 1) * P], GM * KC,
                               xT_filled)
                if h == M_ROWS:
                    pe.wait_ge(*xT_ready(c.n, 1))
                    rows(XB, lambda k: wrow0[:, c.l, k, :], wxT, 0, GM, rows_filled)
                if h == M_SCORES:
                    pe.wait_ge(*rowa_ready(c.n, 1))
                    pe.wait_ge(*rowb_ready(c.n, 1))
                    if c.new:
                        pe.wait_ge(*neg0_ready(c.n0, 1))
                    if exists(it, o - 1):
                        pe.wait_ge(*hp_ready(Seg(it, SL, o - 1), 1))
                    scores(SB, neg0[c.s], 0, GM, s_filled)
                if h == M_ET:
                    pe.wait_ge(*e_ready(c.n, 1))
                    transposes(SB, lambda g: tE[:, g, :], GM, eT_filled)
                if h == M_AGG:
                    pe.wait_ge(*eT_ready(c.n, 1))
                    aggregate(SB, lambda g: lE[:, g, :], lambda g: xc[c.s][:, g, :], GM, agg_filled)
                if h == M_HT:
                    pe.wait_ge(*hn_ready(c.n, 1))
                    if exists(it, o - 2):
                        pe.wait_ge(*xn_ready(Seg(it, SL, o - 2), 1))
                    elif exists(it, o - 1):
                        pe.wait_ge(*hT_ready(Seg(it, SL, o - 1), KC))
                    transposes(YB, lambda i: wh[:, i % GM, i // GM * P:(i // GM + 1) * P], GM * KC,
                               hnT_filled)

            def tail(h, it, s):
                q = seg2(it, s)
                first = first_group(it, s)
                for stage_no in (1, 2, 3):
                    if h == N_ZT[stage_no - 1]:
                        pe.wait_ge(*q_z(q, stage_no))
                        if stage_no == 3:
                            pe.wait_ge(*cntT_ready(q, 1))
                        if stage_no == 1 and not first:
                            pe.wait_ge(*o_ready(Seg(it, 2, s - 1), 2))
                        for c in range(KC):
                            transposes(TB + c, lambda g: zN[:, g, c * P:(c + 1) * P], G, q_zT)
                if h == G1_V:
                    pe.wait_ge(*q_T(q, KC))
                    if not first:
                        pe.wait_ge(*o_stored(Seg(it, 2, s - 1), 1))
                    for c in range(2):
                        for g in (2 * c, 2 * c + 1):
                            for k in range(KC):
                                i = pe.matmul(ps[:, TB + c, (g % 2) * D:(g % 2 + 1) * D],
                                              qT[:, k, g * P:(g + 1) * P], Wg1[:, k, :],
                                              start=(k == 0), stop=(k == KC - 1))
                        i.then_inc(v1_filled.sem, 1)
                if h == G1_ROWS:
                    pe.wait_ge(*v1_ready(q, 1))
                    rows(TB, lambda c: wrow1[:, c, :], qT, 64, G, r1_filled)
                if h == G1_SCORES:
                    pe.wait_ge(*r1a_ready(q, 1))
                    pe.wait_ge(*r1b_ready(q, 1))
                    pe.wait_ge(*neg1_ready(q, 1))
                    pe.wait_ge(*v1_ready(q, 2))
                    scores(TB + 1, neg1, 64, G, s1_filled)
                if h == G1_ET:
                    pe.wait_ge(*e1_ready(q, 1))
                    transposes(TB, lambda g: u[:, 0, g, :], G, eT1_filled)
                if h == G1_AGG:
                    pe.wait_ge(*eT1_ready(q, 1))
                    aggregate(TB, lambda g: z[:, g * P:(g + 1) * P], lambda g: V[:, g, 0:D], G,
                              agg1_filled)
                if h in G2_V:
                    g = G2_V.index(h)
                    pe.wait_ge(*q_T(q, 2 * KC))
                    if g >= 2:
                        pe.wait_ge(*a2_ready(q, g - 1))
                    for k in range(KC):
                        i = pe.matmul(ps[:, TB + g % 2, 0:VW], qT[:, k, g * P:(g + 1) * P],
                                      Wg2[:, k, :], start=(k == 0), stop=(k == KC - 1))
                    i.then_inc(v2_filled.sem, 1)
                if h == G2_BT:
                    pe.wait_ge(*a2_ready(q, G))
                    pe.transpose(ps[0:G * H, TB, 0:P], dstT[:, :], identf[:, :]).then_inc(b2_filled.sem, 1)
                for g in range(G):
                    if h == G2_ET[g]:
                        pe.wait_ge(*e2_ready(q, g + 1))
                        if g >= 1:
                            pe.wait_ge(*agg2_ready(q, g))
                        for c in range(2):
                            transposes(TB + c, lambda i: u[:, g % 2, 4 * c + i, :], 4, eT2_filled)
                    if h == G2_AGG[g]:
                        pe.wait_ge(*eT2_ready(q, 2 * g + 2))
                        for hd in range(H):
                            r = hd % HPB * DH
                            i = pe.matmul(ps[r:r + DH, TB, hd // HPB * P:(hd // HPB + 1) * P],
                                          V[:, g, hd * DH:(hd + 1) * DH], z[:, hd * P:(hd + 1) * P],
                                          start=True, stop=True)
                        i.then_inc(agg2_filled.sem, 1)
                if h == G2_BACK:
                    pe.wait_ge(*agg2_ready(q, G))
                    for c in range(2):
                        transposes(TB + c, lambda i: qT[:, i % 2, (2 * c + i // 2) * P:(2 * c + i // 2 + 1) * P],
                                   4, back_filled)
                if h == G3_CNT:
                    pe.wait_ge(*cnt_ready(q, 2))
                    pe.wait_ge(*back_filled(q, 2))
                    pe.wait_ge(*bn_ready(q, 2))
                    for g in range(G):
                        i = pe.transpose(ps[0:NLAB, TB, g * P:(g + 1) * P], cnt[:, g, :], identf[:, :])
                    i.then_inc(cntT_filled.sem, 1)
                if h == G3_OUT:
                    pe.wait_ge(*cntT_ready(q, 1))
                    pe.wait_ge(*q_T(q, 3 * KC))
                    for c in range(2):
                        for g in (2 * c, 2 * c + 1):
                            o = ps[:, TB + c, (g % 2) * D:(g % 2 + 1) * D]
                            for k in range(KC):
                                pe.matmul(o, qT[:, k, g * P:(g + 1) * P], Wg3[:, k, :], start=(k == 0),
                                          stop=False)
                            i = pe.matmul(o, cntT[:, g * P:(g + 1) * P], table[0:NLAB, :], start=False,
                                          stop=True)
                        i.then_inc(o_filled.sem, 1)

            def ff1(it, o, p):
                n, l, s = Seg(it, SL, o), o // NSTR % L, o % NSTR
                if p >= 2:
                    pe.wait_ge(*gf_ready(n, p - 1))
                elif exists(it, o - 1):
                    pe.wait_ge(*gf_ready(Seg(it, SL, o - 1), FP + p - 1))
                ins = None
                for c in (2 * p, 2 * p + 1):
                    for i, (w, v) in enumerate(((W1h, hTh), (W1l, hTh), (W1h, hTl))):
                        if c == 0 and i != 1:
                            pe.wait_ge(*(hTh_ready if i == 0 else hTl_ready)(n, 1))
                        for k in range(KC):
                            ins = pe.matmul(ps[:, FF1 + p % 2, c % 2 * CM:(c % 2 + 1) * CM],
                                            w[:, l, k, c * P:(c + 1) * P], v[s][:, k, :],
                                            start=(i == 0 and k == 0), stop=(i == 2 and k == KC - 1))
                ins.then_inc(ff1_filled.sem, 1)

            def ff2(it, o, p):
                n, l, r = Seg(it, SL, o), o // NSTR % L, (FP * o + p) % NS
                if p == 0 and exists(it, o - 1):
                    pe.wait_ge(*yT_ready(Seg(it, SL, o - 1), KC))
                ins = None
                for i, (w, v) in enumerate(((W2h, gh), (W2l, gh), (W2h, gl))):
                    if i != 1:
                        pe.wait_ge(*(gh_ready if i == 0 else gl_ready)(n, p + 1))
                    for c in (2 * p, 2 * p + 1):
                        for k in range(KC):
                            ins = pe.matmul(ps[:, FF2, k * CM:(k + 1) * CM], w[:, l, c, k * P:(k + 1) * P],
                                            v[:, r, c % 2 * CM:(c % 2 + 1) * CM],
                                            start=(c == 0 and i == 0 and k == 0),
                                            stop=(c == FC - 1 and i == 2), skip_group_check=True)
                ins.then_inc(g_used.sem, 1)

            def ff(h, it, o):
                if h in FF1_AT:
                    ff1(it, o, FF1_AT.index(h))
                if h in FF2_AT:
                    ff2(it, o, FF2_AT.index(h))

            def init(h, o):
                if (o, h) == (-LEAD, M_ROWS):
                    pe.wait_ge(*i_rows0(0, 4))
                    pe.wait_ge(*i_small(0, i_small.per))
                if h == 0 and o in range(0, SL, NSTR):
                    pe.wait_ge(*i_lo(0, PPL * (o // NSTR + 1)))
                if (o, h) == (6, 10):
                    pe.wait_ge(*i_sum3(0, 1))
                    pe.wait_ge(*i_fold(0, 8))
                    for c in range(KC):
                        transposes(TB + c, lambda i: prod3[:, i, c * P:(c + 1) * P], KC, i_t3)
                if (o, h) == (7, 0):
                    pe.wait_ge(*i_w3(0, KC))

            pe.wait_ge(*i_ident(0, 3))
            schedule(pe, init, ff, main, tail)


_INS = ["x", "adj", "L0_gnn_attn_w", "L0_gnn_attn_b", "L0_gnn_W1", "L0_gnn_b1", "L0_gnn_W2", "L0_gnn_b2",
        "L0_gnn_g1", "L0_gnn_beta1", "L0_gnn_g2", "L0_gnn_beta2", "L1_gnn_W", "L1_gnn_a", "L2_gnn_W_proj",
        "L2_gnn_W_att", "L2_gnn_b_att", "L3_gnn_weights", "L3_gnn_bias"]


def kernel(**inputs):
    import numpy as _np
    import concourse.bacc as _bacc
    from concourse import mybir as _mybir
    from concourse.bass_utils import run_bass_kernel_spmd as _run

    nc = _bacc.Bacc("TRN2", target_bir_lowering=False, num_devices=1)
    arrays, args = {}, []
    for name in _INS:
        a = _np.ascontiguousarray(inputs[name])
        arrays[f"in_{name}_dram"] = a
        args.append(nc.dram_tensor(f"in_{name}_dram", a.shape, _mybir.dt.from_np(a.dtype), kind="ExternalInput").ap())
    shape = inputs["x"].shape
    out = nc.dram_tensor("out_dram", shape, _mybir.dt.float32, kind="ExternalOutput").ap()
    build(nc, *args, out)
    r = _run(nc, [arrays], core_ids=[0])
    return r.results[0]["out_dram"]
```

```python
from contextlib import ExitStack

import concourse.bass as bass
from concourse import mybir
from concourse.alu_op_type import AluOpType as ALU

ACT = mybir.ActivationFunctionType
AX = mybir.AxisListType
F32 = mybir.dt.float32
F32R = mybir.dt.float32r
BF16 = mybir.dt.bfloat16
I32 = mybir.dt.int32

P = 128
D = 256
KC = D // P
G = 4
C = G * P
GM = 2
CM = GM * P
NSTR = 4
T = 40
LEAD = 3
PHASES = 6
EPS = 1e-5
SLOPE = 0.2
MASKED = -1e30

FF1_AT = (0, 10, 20, 27)
GELU_AT = (3, 11, 22, 34)
GH_AT = (5, 15, 23, 36)
GL_AT = (7, 16, 30, 39)
FF2_AT = (12, 22, 33, 44)
M_N2, M_N2_RS, M_XN, M_XB, M_X1 = 9, 14, 14, 19, 19
M_LN0, M_LN0_RS, M_Z0, M_MASK = 12, 12, 16, 25
M_XT, M_XT_COPY = 30, 33
M_ROWS, M_ROW_COPY = 34, 36
M_SCORES, M_T, M_MAX, M_EXP = 42, 44, 45, 48
M_ET, M_ET_COPY, M_RECIP = 56, 56, 55
M_AGG, M_HP, M_N1_RS, M_HN = 64, 65, 72, 83
M_HT, M_HT_COPY, M_HTH, M_HTL = 99, 102, 105, 110
COUNT_AT = (0, 2, 20, 24)
TREE_AT = (9, 24)
N_AT = (20, 81, 212)
N_RS = (23, 80, 215)
N_Z = (22, 82, 216)
N_ZT = (30, 84, 225)
N_ZT_COPY = (29, 82, 218)
G1_V = (33, 34, 35, 36)
G1_V_COPY = (37, 41)
G1_ROWS, G1_ROW_COPY = 37, 40
G1_SCORES, G1_T, G1_MAX, G1_EXP = 43, 45, 48, 49
G1_ET, G1_ET_COPY, G1_RECIP, G1_AGG, G1_MIN, G1_ELU_EXP, G1_ELU = 58, 57, 57, 61, 63, 63, 72
G2_V = (88, 90, 93, 94)
G2_V_COPY = (87, 92, 94, 95)
G2_BT, G2_BT_COPY = 96, 100
G2_SUM = (107, 133, 150, 174)
G2_LEAKY = (117, 141, 163, 180)
G2_MAX = (125, 143, 163, 181)
G2_EXP = (128, 144, 167, 185)
G2_ET = (134, 154, 172, 193)
G2_ET_COPY = (137, 156, 181, 202)
G2_AGG = (141, 161, 180, 202)
G2_AGG_COPY = (146, 162, 183, 204)
G2_BACK, G2_X3 = 202, 207
G3_CNT, G3_CNT_COPY, G3_RES = 217, 213, 229
G3_OUT = (228, 229, 230, 231)
G3_SUM = (234, 235)
PIECES_AT = (6, 26)


class Seg:

    def __init__(self, it, mult, off):
        self.it, self.mult, self.off = it, mult, off


class Signal:

    def __init__(self, sem, per, step=1, base=0):
        self.sem, self.per, self.step, self.base = sem, per, step, base

    def __call__(self, seg, k):
        if isinstance(seg, int):
            return self.sem, (seg * self.per + k + self.base) * self.step
        const = (seg.off * self.per + k + self.base) * self.step
        if isinstance(seg.it, int):
            return self.sem, seg.it * (seg.mult * self.per * self.step) + const
        return self.sem, seg.it * (seg.mult * self.per * self.step) + const


def build(nc, x, adj, attn_w, attn_b, W1, b1, W2, b2, g1, beta1, g2, beta2,
          L1_W, L1_a, L2_Wp, L2_Wa, L2_ba, L3_W, L3_bias, out):
    B = x.shape[0]
    L = attn_w.shape[0]
    F = W1.shape[2]
    FC = F // P
    H = L2_Wa.shape[0]
    DH = D // H
    NLAB = L3_bias.shape[0]
    FP = FC // 2
    ITS = B // (NSTR * GM)
    SL = NSTR * L
    NSEG = ITS * SL
    VW = D + 2 * H
    HPB = P // DH

    scratch = nc.dram_tensor("target_rows", (2 * G * H, P), F32, kind="Internal").ap()

    with ExitStack() as ctx:
        def sb(name, shape, dt=F32):
            return ctx.enter_context(nc.sbuf_tensor(name, shape, dt))

        def signal(name, per=1, step=1):
            return Signal(ctx.enter_context(nc.semaphore(name)), per, step)

        W1h = sb("W1h", [P, L, KC, F], F32R)
        W1l = sb("W1l", [P, L, KC, F], F32R)
        W2h = sb("W2h", [P, L, FC, D], F32R)
        W2l = sb("W2l", [P, L, FC, D], F32R)
        Wg1 = sb("Wg1", [P, KC, D])
        Wg2 = sb("Wg2", [P, KC, VW])
        Wg3 = sb("Wg3", [P, KC, D])
        wrow0 = sb("wrow0", [P, L, KC, 33])
        wrow1 = sb("wrow1", [P, KC, 33])
        gamma2 = sb("gamma2", [P, L, D])
        betab2 = sb("betab2", [P, L, D])
        identf = sb("identf", [P, P])
        identb = sb("identb", [P, P], BF16)
        offdiag = sb("offdiag", [P, P], BF16)
        table = sb("table", [NLAB, D])
        b1T = sb("b1T", [P, L, FC])
        b2s = sb("b2s", [65, L * D], BF16)
        onesb = sb("onesb", [65, P], BF16)
        g1T = sb("g1T", [P, L, KC])
        beta1T = sb("beta1T", [P, L, KC])
        batt = sb("batt", [P, H])
        attb = sb("attb", [1, L])
        mhalf = sb("mhalf", [P, G])
        epsG = sb("epsG", [P, G])
        idleP = sb("idleP", [P, G])
        idleV = sb("idleV", [P, 2])
        rowL = sb("rowL", [P, C])
        rowR = sb("rowR", [P, C])
        xcA = sb("xc", [P, NSTR, GM, D])
        xc = [xcA[:, s, :, :] for s in range(NSTR)]
        hTA = sb("hT", [P, NSTR, KC, CM])
        hT = [hTA[:, s, :, :] for s in range(NSTR)]
        hTh = [sb(f"hTh{s}", [P, KC, CM], F32R) for s in range(NSTR)]
        hTl = [sb(f"hTl{s}", [P, KC, CM], F32R) for s in range(NSTR)]
        xt = [sb(f"xt{r}", [P, G, D]) for r in range(2)]
        neg0A = sb("neg0", [P, NSTR, GM, P], BF16)
        neg0 = [neg0A[:, s, :, :] for s in range(NSTR)]
        NG, NS = 2, 3
        gf = sb("gf", [P, NG, 2 * CM])
        gh = sb("gh", [P, NS, 2 * CM], F32R)
        gl = sb("gl", [P, NS, 2 * CM], F32R)
        wx = sb("wx", [P, GM * D])
        wxT = wx[:, :].rearrange("p (c n) -> p c n", c=KC)
        wxN = wx[:, :].rearrange("p (g d) -> p g d", g=GM)
        wh = sb("wh", [P, GM, D])
        tE = sb("tE", [P, GM, P])
        lE = sb("lE", [P, GM, P])
        adjM = sb("adjM", [P, GM, P], I32)
        z = sb("z", [P, G * D])
        qT = sb("qT", [P, KC, C])
        V = sb("V", [P, G, D])
        u = sb("u", [P, 2, H, P])
        N2, TL, N1, N0, TL2 = range(5)
        ng = (GM, G, GM, GM, G)
        st6 = [sb(f"st6{i}", [P, ng[i], 6])[:, :, :] for i in range(4)]
        mv = [sb(f"mv{i}", [P, ng[i], 2])[:, :, :] for i in range(4)]
        ve = [sb(f"ve{i}", [P, ng[i]])[:, :] for i in range(4)]
        rstd = [sb(f"rstd{i}", [P, ng[i]])[:, :] for i in range(4)]
        nmx = sb("nmx", [P, GM])
        ssum = sb("ssum", [P, GM])
        rsum = sb("rsum", [P, GM])

        class Work:

            def __init__(self, z, qT, V, u, adjT, neg1, small, base, bank, stat, rows, tag):
                self.z, self.qT, self.V, self.u, self.adjT, self.neg1 = z, qT, V, u, adjT, neg1
                self.zN = z.rearrange("p (g d) -> p g d", g=G)
                self.srcT = small("srcT", [P, G, H])
                self.dstT = small("dstT", [P, G * H])
                self.cnt = small("cnt", [P, G, NLAB])
                self.bT = small("bT", [G * H, P])
                self.nmxT = small("nmxT", [P, 2, H])
                self.ssumT = small("ssumT", [P, G, H])
                self.rsumT = small("rsumT", [P, G, H])
                self.oh = u.rearrange("p a h n -> p (a h n)").bitcast(BF16).rearrange(
                    "p (v g n) -> p v g n", v=NLAB // 2, g=G)
                self.cntT = u[0:NLAB, 1, 0:G, :].rearrange("p g n -> p (g n)")
                self.base, self.bank, self.stat, self.rows, self.tag = base, bank, stat, rows, tag

            def segment(self, it, r):
                return Seg(it, 2, r) if self.tag == "" else Seg(0, 1, 0)

            def first(self, it, r):
                return self.tag != "" or first_group(it, r)

        def first_group(it, r):
            return isinstance(it, int) and it == 0 and r == 0

        places = {"tE": 0, "lE": 0}

        def in_main(name, shape):
            n = 1
            for d in shape[1:]:
                n *= d
            k, t = ("tE", tE) if places["tE"] + n <= GM * P else ("lE", lE)
            a = t[0:shape[0], :, :].rearrange("p g n -> p (g n)")[:, places[k]:places[k] + n]
            places[k] += n
            assert places[k] <= GM * P
            return a if len(shape) == 2 else a.rearrange("p (a b) -> p a b", a=shape[1])

        for t, w in ((st6, 6), (mv, 2)):
            t.append(in_main("", [P, G, w]))
        for t in (ve, rstd):
            t.append(in_main("", [P, G]))
        work = [
            Work(z[:, :], qT[:, :, :], V[:, :, :], u[:, :, :, :], sb("adjT", [P, G, P], I32)[:, :, :],
                 sb("neg1", [P, G, P], BF16)[:, :, :],
                 lambda name, shape: sb(name, shape)[tuple(slice(None) for _ in shape)],
                 64, 6, TL, scratch[0:G * H, :], ""),
            Work(hTA[:, 0:2, :, :].rearrange("p s c n -> p (s c n)"),
                 hTA[:, 2:4, :, :].rearrange("p s c n -> p (s c n)").rearrange("p (c n) -> p c n", c=KC),
                 gf[:, 0:2, :].rearrange("p a n -> p (a n)").rearrange("p (g d) -> p g d", g=G),
                 xcA[:, :, :, :].rearrange("p s g d -> p (s g d)").rearrange("p (a h n) -> p a h n", a=2, h=H),
                 wh[:, :, :].rearrange("p g d -> p (g d)").bitcast(I32).rearrange("p (g n) -> p g n", g=G),
                 neg0A[:, 0:2, :, :].rearrange("p s g n -> p (s g) n"),
                 in_main, 0, 0, TL2, scratch[G * H:2 * G * H, :], "_last"),
        ]

        ps = ctx.enter_context(nc.psum_tensor("ps", [P, 8, 512], F32))
        FF1, FF2, XB, SB, TB = 0, 2, 4, 5, 6

        i_stage = [signal(f"i_stage{k}", 1, 16) for k in range(2)]
        i_hi = signal("i_hi")
        i_lo = signal("i_lo")
        i_cols = signal("i_cols")
        i_zero = signal("i_zero")
        i_rows0 = signal("i_rows0", 4)
        i_small = signal("i_small", 14, 16)
        i_tabs = signal("i_tabs", 8, 16)
        i_b2z = signal("i_b2z")
        i_b2x = signal("i_b2x", 3, 16)
        i_b2 = signal("i_b2", 6)
        i_pool = signal("i_pool")
        i_ident = signal("i_ident")
        i_fold = signal("i_fold")
        i_sum3 = signal("i_sum3")
        i_t3 = signal("i_t3")
        i_w3 = signal("i_w3")
        x_loaded = [signal(f"x_loaded{s}", 1, 16) for s in range(NSTR)]
        adjM_loaded = signal("adjM_loaded", 1, 16)
        neg_part = signal("neg_part")
        neg0_ready = signal("neg0_ready")
        ln0_bn = signal("ln0_bn")
        ln0_mv = signal("ln0_mv")
        ln0_ve = signal("ln0_ve")
        ln0_rstd = signal("ln0_rstd")
        ln0_z = signal("ln0_z")
        xc_ready = signal("xc_ready")
        xT_filled = signal("xT_filled")
        xT_ready = signal("xT_ready")
        rows_filled = signal("rows_filled")
        rowa_ready = signal("rowa_ready")
        rowb_ready = signal("rowb_ready")
        s_filled = signal("s_filled")
        t_ready = signal("t_ready")
        l_ready = signal("l_ready")
        m_ready = signal("m_ready")
        e_ready = signal("e_ready")
        r_ready = signal("r_ready")
        eT_filled = signal("eT_filled")
        eT_ready = signal("eT_ready")
        agg_filled = signal("agg_filled")
        hp_ready = signal("hp_ready")
        n1_bn = signal("n1_bn")
        n1_mv = signal("n1_mv")
        n1_ve = signal("n1_ve")
        n1_rstd = signal("n1_rstd")
        hn_ready = signal("hn_ready")
        hnT_filled = signal("hnT_filled")
        hT_ready = signal("hT_ready", KC)
        hTh_ready = signal("hTh_ready")
        hTl_ready = signal("hTl_ready")
        ff1_filled = signal("ff1_filled", FP)
        gf_ready = signal("gf_ready", FP)
        gh_ready = signal("gh_ready", FP)
        gl_ready = signal("gl_ready", FP)
        g_used = signal("g_used", FP)
        n2_bn = signal("n2_bn")
        n2_mv = signal("n2_mv")
        n2_ve = signal("n2_ve")
        n2_rstd = signal("n2_rstd")
        xn_ready = signal("xn_ready")
        xg_ready = signal("xg_ready")
        xt_loaded = [signal(f"xt_loaded{r}", 1, 16) for r in range(2)]
        x1_ready = signal("x1_ready", 2)
        goes_on = {"adjT_loaded": (adjM_loaded, NSEG // L), "neg1_ready": (neg0_ready, NSEG // L)}
        for name, earlier in (
                ("q_bn", n1_bn), ("q_mv", n1_mv), ("q_ve", n1_ve), ("q_rstd", n1_rstd), ("q_z", hn_ready),
                ("q_zT", hnT_filled), ("q_T", hT_ready), ("v1_filled", xT_filled), ("v1_ready", xT_ready),
                ("r1_filled", rows_filled), ("r1a_ready", rowa_ready), ("r1b_ready", rowb_ready),
                ("s1_filled", s_filled), ("t1_ready", t_ready), ("l1_ready", l_ready),
                ("m1_ready", m_ready), ("e1_ready", e_ready), ("d1_ready", r_ready),
                ("eT1_filled", eT_filled), ("eT1_ready", eT_ready), ("agg1_filled", agg_filled),
                ("x2_ready", xc_ready), ("v2_filled", ff1_filled), ("v2_ready", gf_ready),
                ("a2_ready", gh_ready), ("b2_filled", hTh_ready), ("b2_ready", hTl_ready),
                ("x3_ready", hp_ready)):
            goes_on[name] = (earlier, NSEG)
        for name, earlier in (("mn_ready", ln0_bn), ("em_ready", ln0_mv), ("el_ready", ln0_z),
                              ("ex_ready", ln0_rstd)):
            goes_on[name] = (earlier, NSEG // L)

        def tail_signal(w, name, per=1, step=1):
            if w is work[1] and name in goes_on:
                earlier, segments = goes_on[name]
                assert earlier.step == step
                return Signal(earlier.sem, per, step, segments * earlier.per)
            return signal(name + w.tag, per, step)

        for w in work:
            w.adjT_loaded = tail_signal(w, "adjT_loaded", 1, 16)
            w.neg1_ready = tail_signal(w, "neg1_ready")
            w.q_bn = tail_signal(w, "q_bn", 3)
            w.q_mv = tail_signal(w, "q_mv", 3)
            w.q_ve = tail_signal(w, "q_ve", 3)
            w.q_rstd = tail_signal(w, "q_rstd", 3)
            w.q_z = tail_signal(w, "q_z", 3)
            w.q_zT = tail_signal(w, "q_zT", 3 * KC)
            w.q_T = tail_signal(w, "q_T", 3 * KC)
            w.v1_filled = tail_signal(w, "v1_filled", 2)
            w.v1_ready = tail_signal(w, "v1_ready", 2)
            w.r1_filled = tail_signal(w, "r1_filled")
            w.r1a_ready = tail_signal(w, "r1a_ready")
            w.r1b_ready = tail_signal(w, "r1b_ready")
            w.s1_filled = tail_signal(w, "s1_filled")
            w.t1_ready = tail_signal(w, "t1_ready")
            w.l1_ready = tail_signal(w, "l1_ready")
            w.m1_ready = tail_signal(w, "m1_ready")
            w.e1_ready = tail_signal(w, "e1_ready")
            w.d1_ready = tail_signal(w, "d1_ready")
            w.eT1_filled = tail_signal(w, "eT1_filled")
            w.eT1_ready = tail_signal(w, "eT1_ready")
            w.agg1_filled = tail_signal(w, "agg1_filled", 2)
            w.mn_ready = tail_signal(w, "mn_ready")
            w.ex_ready = tail_signal(w, "ex_ready")
            w.em_ready = tail_signal(w, "em_ready")
            w.el_ready = tail_signal(w, "el_ready")
            w.x2_ready = tail_signal(w, "x2_ready")
            w.v2_filled = tail_signal(w, "v2_filled", G)
            w.v2_ready = tail_signal(w, "v2_ready", G)
            w.a2_ready = tail_signal(w, "a2_ready", G)
            w.b2_filled = tail_signal(w, "b2_filled")
            w.b2_ready = tail_signal(w, "b2_ready")
            w.b2_stored = tail_signal(w, "b2_stored", 1, 16)
            w.b2_spread = [signal(f"b2_spread{k}" + w.tag, 2, 16) for k in range(2)]
            w.u2_ready = tail_signal(w, "u2_ready", G)
            w.l2_ready = tail_signal(w, "l2_ready", G)
            w.m2_ready = tail_signal(w, "m2_ready", G)
            w.e2_ready = tail_signal(w, "e2_ready", G)
            w.eT2_filled = tail_signal(w, "eT2_filled", 2 * G)
            w.eT2_ready = tail_signal(w, "eT2_ready", 2 * G)
            w.agg2_filled = tail_signal(w, "agg2_filled", G)
            w.agg2_ready = tail_signal(w, "agg2_ready", G)
            w.d2_ready = tail_signal(w, "d2_ready")
            w.back_filled = tail_signal(w, "back_filled", 2)
            w.bn_ready = tail_signal(w, "bn_ready", 2)
            w.x3_ready = tail_signal(w, "x3_ready")
            w.oh_ready = tail_signal(w, "oh_ready", 2)
            w.sum1_ready = tail_signal(w, "sum1_ready", 2)
            w.sum2_ready = tail_signal(w, "sum2_ready", 2)
            w.sum3_ready = tail_signal(w, "sum3_ready", 2)
            w.cnt_ready = tail_signal(w, "cnt_ready", 2)
            w.cntT_filled = tail_signal(w, "cntT_filled")
            w.cntT_ready = tail_signal(w, "cntT_ready")
            w.res_ready = tail_signal(w, "res_ready")
            w.o_filled = tail_signal(w, "o_filled", 2)
            w.o_ready = tail_signal(w, "o_ready", 2)
            w.o_stored = tail_signal(w, "o_stored", 1, 16)

        WC = F // D
        pieces = []
        for l in range(L):
            w1 = W1[l].rearrange("(c p) f -> p c f", p=P)
            w2 = W2[l].rearrange("(c p) d -> p c d", p=P)
            for c in range(KC):
                pieces.append((W1h[:, l, c, :], W1l[:, l, c, :], w1[:, c, :]))
            for c in range(0, FC, WC):
                pieces.append((W2h[:, l, c:c + WC, :].rearrange("p c d -> p (c d)"),
                               W2l[:, l, c:c + WC, :].rearrange("p c d -> p (c d)"),
                               w2[:, c:c + WC, :]))
        PPL = len(pieces) // L
        stage = [u[:, k, :, :].rearrange("p h n -> p (h n)") for k in range(2)]
        abc = qT[:, 0, :]
        wabc = qT[:, 1, :]
        raw3 = z[:, :].rearrange("p (d i) -> p d i", d=4)
        prod = V[:, :, :].rearrange("p g n -> p (g n)")[:, 0:D]
        prod2 = V[:, :, :].rearrange("p g n -> p (g n)")[:, D:2 * D]
        prod3 = V[:, 2:4, :]
        b2x = hTA[0:65, 0:2, :, :].rearrange("p s c n -> p (s c n)")[:, 0:L * D]
        b2r = hTA[0:65, 2:4, :, :].rearrange("p s c n -> p (s c n)")[:, 0:L * D]

        def graphs(t, g0, n=G):
            return t[bass.ds(g0, n)].rearrange("g p d -> p g d")

        class Chain:

            def __init__(self, it, o):
                self.it, self.o = it, o
                self.l, self.s, self.group = o // NSTR % L, o % NSTR, o // SL
                self.n = Seg(it, SL, o)
                self.new = self.l == 0
                self.post = exists(it, o - NSTR)
                self.attend = exists(it, o)
                self.before = Seg(it, SL, o - NSTR)
                self.before_l = (self.l - 1) % L
                self.n0 = Seg(it, NSTR, NSTR * self.group + self.s)
                self.xt = self.s // 2
                self.half = slice(self.s % 2 * GM, (self.s % 2 + 1) * GM)
                self.done = Seg(it, NSTR, NSTR * (self.group - 1) + self.s)
                self.q = Seg(it, 2, 2 * (self.group - 1) + self.xt)

        def exists(it, o):
            return not isinstance(it, int) or 0 <= it * SL + o < NSEG

        def schedule(eng, init, ff, main, tail):
            def slot(it, o):
                part = tail_phase(it, o)
                for h in range(T):
                    if isinstance(it, int) and it == 0:
                        init(h, o)
                    for back in (1, 0):
                        if exists(it, o - back):
                            ff(h + T * back, it, o - back)
                    for j in reversed(range(LEAD)):
                        if exists(it, o + LEAD - j) or exists(it, o + LEAD - j - NSTR):
                            if not isinstance(it, int) or it * SL + o + LEAD - j >= 0:
                                main(h + T * j, Chain(it, o + LEAD - j))
                    if part:
                        phase, tit, r = part
                        tail(h + T * phase, tit, r, work[0])
                    if isinstance(it, int) and it == ITS - 1 and o >= SL:
                        tail(h + T * (o - SL), it, 1, work[1])

            for o in range(-LEAD, 0):
                slot(0, o)
            for o in range(SL):
                slot(0, o)
            with eng.Fori(1, ITS - 1) as it:
                for o in range(SL):
                    slot(it, o)
            for o in range(SL):
                slot(ITS - 1, o)
            for o in range(SL, SL + PHASES):
                slot(ITS - 1, o)

        R0_AT = SL - 2

        def piece_at(h, o):
            if h in PIECES_AT and 0 <= o + 2 < len(pieces) // 2:
                return 2 * (o + 2) + PIECES_AT.index(h)
            return None

        def tail_phase(it, o):
            if o >= SL and isinstance(it, int):
                it, o = it + 1, o - SL
            d = o - R0_AT
            if d < 0:
                it, d = it - 1, d + SL
            if isinstance(it, int) and (it < 0 or it >= ITS or (it, d // PHASES) == (ITS - 1, 1)):
                return None
            return d % PHASES, it, d // PHASES

        def seg2(it, s):
            return Seg(it, 2, s)

        block = ctx.enter_context(nc.Block())

        @block.sync
        def _(sp):
            def load_x(it, group, s):
                sp.dma_start(xc[s][:, :, :], graphs(x, it * (NSTR * GM) + (group * NSTR + s) * GM,
                                                    GM)).then_inc(x_loaded[s].sem, 16)

            def load_adjM(it, group, s):
                if exists(it, group * SL + s - 1):
                    sp.wait_ge(*neg0_ready(Seg(it, NSTR, group * NSTR + s - 1), 1))
                sp.dma_start(adjM[:, :, :], graphs(adj, it * (NSTR * GM) + (group * NSTR + s) * GM,
                                                   GM)).then_inc(adjM_loaded.sem, 16)

            def load_piece(k):
                if k >= 2:
                    sp.wait_ge(*i_lo(0, k - 1))
                src = pieces[k][2]
                dst = stage[k % 2]
                if len(src.shape) == 3:
                    dst = dst.rearrange("p (c d) -> p c d", d=D)
                sp.dma_start(dst, src).then_inc(i_stage[k % 2].sem, 16)

            def load_adjT(it, r, w):
                if w is work[1]:
                    sp.wait_ge(*hnT_filled(NSEG - 1, 1))
                elif not first_group(it, r):
                    sp.wait_ge(*work[0].oh_ready(Seg(it, 2, r - 1), 2))
                    sp.wait_ge(*work[0].neg1_ready(Seg(it, 2, r - 1), 1))
                sp.dma_start(w.adjT, graphs(adj, it * (2 * G) + r * G)).then_inc(w.adjT_loaded.sem, 16)

            def load_xt(it, r, first):
                if not first:
                    sp.wait_ge(*work[0].res_ready(Seg(it, 2, r - 2), 1))
                sp.dma_start(xt[r][:, :, :], graphs(x, it * (2 * G) + r * G)).then_inc(xt_loaded[r].sem, 16)

            def spread(q, g, w):
                if g >= 2:
                    sp.wait_ge(*w.eT2_filled(q, 2 * (g - 1)))
                src = w.rows[g * H:(g + 1) * H, :].rearrange("(a h) n -> a (h n)", a=1)
                sp.dma_start(w.u[:, g % 2, :, :].rearrange("p h n -> p (h n)"),
                             src.to_broadcast([P, H * P])).then_inc(w.b2_spread[g % 2].sem, 16)

            load_x(0, 0, 0)
            load_adjM(0, 0, 0)
            for k in range(2):
                load_x(0, 0, 1 + k)
                load_piece(k)
            load_x(0, 0, 3)

            def init(h, o):
                if h == 1 and 0 <= o + 2 < len(pieces) // 2 - 1:
                    load_piece(2 * (o + 3))
                    load_piece(2 * (o + 3) + 1)
                if h == 0 and o == R0_AT - 2:
                    load_adjT(0, 0, work[0])

            def ff(h, it, o):
                first = isinstance(it, int) and it == 0
                if h != 0:
                    return
                if o == 4:
                    load_xt(it, 0, first)
                if o == 10:
                    load_xt(it, 1, first)

            def main(h, c):
                if h == 0:
                    ahead = Chain(c.it, c.o + 2)
                    if ahead.new and ahead.attend and ahead.post:
                        sp.wait_ge(*hp_ready(ahead.before, 1))
                        load_x(ahead.it, ahead.group, ahead.s)
                    ahead = Chain(c.it, c.o + 1)
                    if ahead.new and ahead.attend:
                        load_adjM(ahead.it, ahead.group, ahead.s)

            def tail(h, it, r, w):
                q = w.segment(it, r)
                if w is work[1] and h == 0:
                    load_adjT(it, r, w)
                if h == G2_BT_COPY:
                    sp.wait_ge(*w.b2_ready(q, 1))
                    sp.dma_start(w.rows, w.bT).then_inc(w.b2_stored.sem, 16)
                    sp.wait_ge(*w.b2_stored(q, 1))
                    spread(q, 0, w)
                    spread(q, 1, w)
                for g in (2, 3):
                    if h == G2_ET[g - 2]:
                        spread(q, g, w)
                if h == (PHASES - 1) * T + 3 and w is work[0]:
                    last = isinstance(it, int) and it == ITS - 1
                    if r == 0 and not last:
                        load_adjT(it, 1, w)
                    elif r == 1:
                        load_adjT(it + 1, 0, w)
                if h == G3_SUM[-1]:
                    sp.wait_ge(*w.o_ready(q, 2))
                    sp.dma_start(graphs(out, it * (2 * G) + r * G), w.V).then_inc(w.o_stored.sem, 16)

            schedule(sp, init, ff, main, tail)
            sp.wait_ge(*work[0].o_stored(seg2(ITS - 1, 0), 1))
            sp.wait_ge(*work[1].o_stored(0, 1))

        @block.gpsimd
        def _(pool):
            pool.memset(identf[:, :], 0.0).then_inc(i_pool.sem, 1)
            pool.memset(identb[:, :], 0.0).then_inc(i_pool.sem, 1)
            pool.memset(offdiag[:, :], 1.0).then_inc(i_pool.sem, 1)
            pool.memset(mhalf[:, :], -0.5).then_inc(i_pool.sem, 1)
            pool.memset(epsG[:, :], EPS).then_inc(i_pool.sem, 1)
            pool.wait_ge(*i_pool(0, 5))
            for t, fill in ((identf, 1.0), (identb, 1.0), (offdiag, 0.0)):
                pool.affine_select(out=t[:, :], in_=t[:, :], compare_op=ALU.not_equal, fill=fill,
                                   base=0, pattern=[[-1, P]], channel_multiplier=1).then_inc(i_ident.sem, 1)
            pool.wait_ge(*i_ident(0, 3))
            def carry_waits():
                pool.tensor_tensor(idleP[:, :], mhalf[:, :], mhalf[:, :], ALU.mult)

            def mask0(c):
                pool.wait_ge(*adjM_loaded(c.n0, 1))
                if c.post:
                    pool.wait_ge(*s_filled(c.before, 1))
                carry_waits()
                pool.tensor_scalar(neg0[c.s][:, :, :], adjM[:, :, :], 0, MASKED, ALU.is_le,
                                   ALU.mult).then_inc(neg_part.sem, 1)
                pool.wait_ge(*neg_part(c.n0, 1))
                pool.tensor_tensor(neg0[c.s][:, :, :], neg0[c.s][:, :, :],
                                   offdiag[:, :].rearrange("p (a n) -> p a n", a=1).to_broadcast([P, GM, P]),
                                   ALU.mult).then_inc(neg0_ready.sem, 1)

            def rsqrt(i, mv_ready, ve_ready, out_ready, seg, k=1):
                pool.wait_ge(*mv_ready(seg, k))
                pool.tensor_tensor(ve[i][:, :], mv[i][:, :, 1], epsG[:, 0:ng[i]], ALU.add).then_inc(ve_ready.sem, 1)
                pool.wait_ge(*ve_ready(seg, k))
                pool.tensor_tensor(rstd[i][:, :], ve[i][:, :], mhalf[:, 0:ng[i]], ALU.pow).then_inc(out_ready.sem, 1)

            def main(h, c):
                if h == M_N2_RS and c.post:
                    rsqrt(N2, n2_mv, n2_ve, n2_rstd, c.before)
                if h == M_X1 and c.post and c.new:
                    pool.wait_ge(*xg_ready(c.done, 1))
                    pool.wait_ge(*xt_loaded[c.xt](Seg(c.it, 1, c.group - 1), 1))
                    pool.tensor_tensor(xt[c.xt][:, c.half, :], xt[c.xt][:, c.half, :], wxN,
                                       ALU.add).then_inc(x1_ready.sem, 1)
                if not c.attend:
                    return
                if h == M_LN0_RS and c.new:
                    rsqrt(N0, ln0_mv, ln0_ve, ln0_rstd, c.n0)
                if h == M_MASK and c.new:
                    mask0(c)
                if h == M_N1_RS:
                    rsqrt(N1, n1_mv, n1_ve, n1_rstd, c.n)
                if h == M_HTL:
                    pool.wait_ge(*hTh_ready(c.n, 1))
                    pool.tensor_tensor(hTl[c.s][:, :, :], hT[c.s][:, :, :], hTh[c.s][:, :, :].bitcast(F32),
                                       ALU.subtract).then_inc(hTl_ready.sem, 1)

            def tail(h, it, r, w):
                q = w.segment(it, r)
                if h == 0:
                    pool.wait_ge(*w.adjT_loaded(q, 1))
                    if not w.first(it, r):
                        pool.wait_ge(*w.o_filled(Seg(it, 2, r - 1), 2))
                    carry_waits()
                    pool.tensor_scalar(w.neg1[:, :, :], w.adjT[:, :, :], 0, MASKED, ALU.is_le,
                                       ALU.mult).then_inc(w.neg1_ready.sem, 1)
                for stage_no in (1, 2, 3):
                    if h == N_RS[stage_no - 1]:
                        rsqrt(w.stat, w.q_mv, w.q_ve, w.q_rstd, q, stage_no)

            def ff(h, it, o):
                n = Seg(it, SL, o)
                if h in GL_AT:
                    p = GL_AT.index(h)
                    pool.wait_ge(*gh_ready(n, p + 1))
                    pool.tensor_tensor(gl[:, (FP * o + p) % NS, :], gf[:, (FP * o + p) % NG, :],
                                       gh[:, (FP * o + p) % NS, :].bitcast(F32),
                                       ALU.subtract).then_inc(gl_ready.sem, 1)

            schedule(pool, lambda h, o: None, ff, main, tail)

        @block.scalar
        def _(act):
            act.wait_ge(*i_zero(0, 4))
            small = []
            for l in range(L):
                for t in range(2):
                    w = attn_w[l, t * D:(t + 1) * D].rearrange("(c p) -> p c", p=P)
                    small.append((wrow0[:, l, :, 32 * t], w))
            small += [
                (Wg2[:, :, 0:D], L2_Wp.rearrange("(c p) f -> p c f", p=P)),
                (abc, L1_a.rearrange("(a k) o -> a (k o)", a=1).to_broadcast([P, 2 * D])),
                (wabc, L2_Wa.rearrange("(a h) k -> a (h k)", a=1).to_broadcast([P, H * 2 * DH])),
            ]
            for d in range(2):
                for oc in range(KC):
                    small.append((raw3[:, 2 * d + oc, :], L3_W[d, oc * P:(oc + 1) * P, :]))
            small.append((table[0:NLAB, :], L3_bias))
            assert len(small) == i_small.per, len(small)
            for dst, src in small[:2 * L]:
                act.dma_start(dst, src, allow_slow_non_contiguous=True).then_inc(i_small.sem, 16)
            tabs = [
                (gamma2[:, :, :].rearrange("p l d -> p (l d)"),
                 g2.rearrange("(a l) d -> a (l d)", a=1).to_broadcast([P, L * D])),
                (betab2[:, :, :].rearrange("p l d -> p (l d)"),
                 beta2.rearrange("(a l) d -> a (l d)", a=1).to_broadcast([P, L * D])),
                (b1T[:, :, :], b1.rearrange("l (c p) -> p l c", p=P)),
                (g1T[:, :, :], g1.rearrange("l (c p) -> p l c", p=P)),
                (beta1T[:, :, :], beta1.rearrange("l (c p) -> p l c", p=P)),
                (batt[:, :], L2_ba.rearrange("(a h) -> a h", a=1).to_broadcast([P, H])),
                (attb[:, :], attn_b.rearrange("(a l) -> a l", a=1)),
                (Wg1[:, :, :], L1_W.rearrange("(c p) f -> p c f", p=P)),
            ]
            assert len(tabs) == i_tabs.per
            for dst, src in tabs:
                act.dma_start(dst, src, allow_slow_non_contiguous=True).then_inc(i_tabs.sem, 16)
            for dst, src in small[2 * L:]:
                act.dma_start(dst, src, allow_slow_non_contiguous=True).then_inc(i_small.sem, 16)
            act.wait_ge(*i_b2z(0, 1))
            for k in range(3):
                act.dma_start(b2x[32 * k:32 * k + 1, :], b2.rearrange("(a l) d -> a (l d)", a=1)).then_inc(i_b2x.sem, 16)

            def init(h, o):
                k = piece_at(h, o)
                if k is not None:
                    act.wait_ge(*i_stage[k % 2](0, k // 2 + 1))
                    act.activation(pieces[k][0], stage[k % 2], ACT.Copy).then_inc(i_hi.sem, 1)
                if (o, h) == (-LEAD, M_XT_COPY):
                    act.wait_ge(*i_tabs(0, i_tabs.per))
                if (o, h) == (6, 12):
                    for c in range(KC):
                        act.wait_ge(*i_t3(0, c + 1))
                        act.activation(Wg3[:, c, :], ps[:, TB + c, 0:D], ACT.Copy).then_inc(i_w3.sem, 1)

            def main(h, c):
                if not c.attend:
                    return
                if h == M_XT_COPY:
                    act.wait_ge(*xT_filled(c.n, 1))
                    if c.post and c.new:
                        act.wait_ge(*x1_ready(c.q, c.s % 2 + 1))
                    act.activation(wx[:, :], ps[:, XB, :], ACT.Copy).then_inc(xT_ready.sem, 1)
                if h == M_ROW_COPY:
                    act.wait_ge(*rows_filled(c.n, 1))
                    act.activation(rowL[0:1, 0:CM], ps[0:1, XB, 0:CM], ACT.Identity,
                                   bias=attb[0:1, c.l:c.l + 1]).then_inc(rowa_ready.sem, 1)
                if h == M_T:
                    act.wait_ge(*s_filled(c.n, 1))
                    act.activation(tE[:, :, :].rearrange("p g n -> p (g n)"), ps[:, SB, 0:CM], ACT.Copy,
                                   scale=SLOPE).then_inc(t_ready.sem, 1)
                if h == M_EXP:
                    act.wait_ge(*m_ready(c.n, 1))
                    for g in range(GM):
                        i = act.activation(tE[:, g, :], lE[:, g, :], ACT.Exp, bias=nmx[:, g:g + 1],
                                           accum_out=ssum[:, g:g + 1])
                    i.then_inc(e_ready.sem, 1)
                if h == M_ET_COPY:
                    act.wait_ge(*eT_filled(c.n, 1))
                    act.activation(lE[:, :, :].rearrange("p g n -> p (g n)"), ps[:, SB, 0:CM],
                                   ACT.Copy).then_inc(eT_ready.sem, 1)
                if h == M_HT_COPY:
                    act.wait_ge(*hnT_filled(c.n, 1))
                    for k in range(KC):
                        act.activation(hT[c.s][:, k, :], ps[:, XB, k * CM:(k + 1) * CM], ACT.Identity,
                                       scale=g1T[:, c.l, k:k + 1],
                                       bias=beta1T[:, c.l, k:k + 1]).then_inc(hT_ready.sem, 1)

            def tail(h, it, s, w):
                q = w.segment(it, s)
                for stage_no in (1, 2, 3):
                    if h == N_ZT_COPY[stage_no - 1]:
                        for c in range(KC):
                            act.wait_ge(*w.q_zT(q, KC * (stage_no - 1) + c + 1))
                            act.activation(w.qT[:, c, :], ps[:, w.bank + c, :], ACT.Relu).then_inc(w.q_T.sem, 1)
                if h in G1_V_COPY:
                    c = G1_V_COPY.index(h)
                    act.wait_ge(*w.v1_filled(q, c + 1))
                    act.activation(w.V[:, 2 * c:2 * c + 2, 0:D],
                                   ps[:, w.bank + c, :].rearrange("p (g d) -> p g d", g=2),
                                   ACT.Copy).then_inc(w.v1_ready.sem, 1)
                if h == G1_ROW_COPY:
                    act.wait_ge(*w.r1_filled(q, 1))
                    act.activation(rowL[w.base:w.base + 1, :], ps[w.base:w.base + 1, w.bank, :], ACT.Copy).then_inc(w.r1a_ready.sem, 1)
                if h == G1_T:
                    act.wait_ge(*w.s1_filled(q, 1))
                    act.wait_ge(*w.cnt_ready(q, 2))
                    act.activation(w.u[:, 0, 0:G, :].rearrange("p g n -> p (g n)"), ps[:, w.bank + 1, :],
                                   ACT.Copy, scale=SLOPE).then_inc(w.t1_ready.sem, 1)
                if h == G1_EXP:
                    act.wait_ge(*w.m1_ready(q, 1))
                    for g in range(G):
                        i = act.activation(w.u[:, 0, g, :], w.u[:, 0, G + g, :], ACT.Exp,
                                           bias=w.nmxT[:, 0, g:g + 1], accum_out=w.ssumT[:, 0, g:g + 1])
                    i.then_inc(w.e1_ready.sem, 1)
                if h == G1_ET_COPY:
                    act.wait_ge(*w.eT1_filled(q, 1))
                    act.activation(w.z[:, 0:C], ps[:, w.bank, :], ACT.Copy).then_inc(w.eT1_ready.sem, 1)
                if h == G1_ELU_EXP:
                    act.wait_ge(*w.mn_ready(q, 1))
                    u1 = w.u[:, 1, :, :].rearrange("p h n -> p (h n)")
                    act.activation(u1, u1, ACT.Exp).then_inc(w.ex_ready.sem, 1)
                if h in G2_V_COPY:
                    g = G2_V_COPY.index(h)
                    act.wait_ge(*w.v2_filled(q, g + 1))
                    act.activation(w.V[:, g, :], ps[:, w.bank + g % 2, 0:D], ACT.Copy).then_inc(w.v2_ready.sem, 1)
                if h == G2_BT_COPY:
                    act.wait_ge(*w.b2_filled(q, 1))
                    act.activation(w.bT, ps[0:G * H, w.bank, 0:P], ACT.Copy).then_inc(w.b2_ready.sem, 1)
                for g in range(G):
                    if h == G2_EXP[g]:
                        act.wait_ge(*w.m2_ready(q, g + 1))
                        for hd in range(H):
                            i = act.activation(w.u[:, g % 2, hd, :], w.u[:, g % 2, hd, :], ACT.Exp,
                                               bias=w.nmxT[:, g % 2, hd:hd + 1], accum_out=w.ssumT[:, g, hd:hd + 1])
                        i.then_inc(w.e2_ready.sem, 1)
                    if h == G2_ET_COPY[g]:
                        for c in range(2):
                            act.wait_ge(*w.eT2_filled(q, 2 * g + c + 1))
                            act.activation(w.z[:, c * C:(c + 1) * C], ps[:, w.bank + c, :], ACT.Copy).then_inc(w.eT2_ready.sem, 1)
                    if h == G2_AGG_COPY[g]:
                        act.wait_ge(*w.agg2_filled(q, g + 1))
                        act.activation(w.qT[:, :, g * P:(g + 1) * P],
                                       ps[:, w.bank, 0:2 * P].rearrange("p (c n) -> p c n", c=2),
                                       ACT.Copy).then_inc(w.agg2_ready.sem, 1)
                if h == G3_CNT_COPY:
                    act.wait_ge(*w.cntT_filled(q, 1))
                    act.activation(w.cntT, ps[0:NLAB, w.bank, :], ACT.Copy).then_inc(w.cntT_ready.sem, 1)

            def ff(h, it, o):
                n, before, l = Seg(it, SL, o), Seg(it, SL, o - 1), o // NSTR % L
                if h in GELU_AT:
                    p = GELU_AT.index(h)
                    act.wait_ge(*ff1_filled(n, p + 1))
                    if p >= NG:
                        act.wait_ge(*gl_ready(n, p + 1 - NG))
                    elif exists(it, o - 1):
                        act.wait_ge(*gl_ready(before, FP + p + 1 - NG))
                    for c in range(2):
                        i = act.activation(gf[:, (FP * o + p) % NG, c * CM:(c + 1) * CM],
                                           ps[:, FF1 + p % 2, c * CM:(c + 1) * CM], ACT.Gelu,
                                           bias=b1T[:, l, 2 * p + c:2 * p + c + 1])
                    i.then_inc(gf_ready.sem, 1)

            schedule(act, init, ff, main, tail)

        @block.vector
        def _(dve):
            dve.memset(wrow0[:, :, :, :], 0.0).then_inc(i_zero.sem, 1)
            dve.memset(wrow1[:, :, :], 0.0).then_inc(i_zero.sem, 1)
            dve.memset(rowL[:, :], 0.0).then_inc(i_zero.sem, 1)
            dve.memset(rowR[:, :], 0.0).then_inc(i_zero.sem, 1)
            dve.memset(idleV[:, :], 0.0)
            dve.memset(b2x, 0.0).then_inc(i_b2z.sem, 1)
            dve.memset(onesb[:, :], 1.0).then_inc(i_b2.sem, 1)
            dve.wait_ge(*i_zero(0, 4))
            for p in (0, 64):
                dve.memset(rowR[p:p + 1, :], 1.0).then_inc(i_rows0.sem, 1)
                dve.memset(rowL[p + 32:p + 33, :], 1.0).then_inc(i_rows0.sem, 1)

            def stats(i, src, bn_ready_, mv_ready, seg, k=1):
                for g in range(ng[i]):
                    ins = dve.bn_stats(st6[i][:, g, :], src(g))
                ins.then_inc(bn_ready_.sem, 1)
                dve.wait_ge(*bn_ready_(seg, k))
                dve.tensor_copy(idleV[:, 1:2], idleV[:, 0:1])
                for g in range(ng[i]):
                    ins = dve.bn_aggr(mv[i][:, g, :], st6[i][:, g, :])
                ins.then_inc(mv_ready.sem, 1)

            def normalise(i, dst, src, rstd_ready, done, seg, k=1):
                dve.wait_ge(*rstd_ready(seg, k))
                for g in range(ng[i]):
                    ins = dve.tensor_scalar(dst(g), src(g), mv[i][:, g, 0:1], rstd[i][:, g:g + 1],
                                            ALU.subtract, ALU.mult)
                ins.then_inc(done.sem, 1)

            def main(h, c):
                if c.post:
                    l, s = c.before_l, c.s
                    yp = lambda g: ps[:, FF2 + c.o % 2, g * D:(g + 1) * D]
                if h == M_N2 and c.post:
                    dve.wait_ge(*g_used(c.before, FP))
                    stats(N2, yp, n2_bn, n2_mv, c.before)
                if h == M_XN and c.post:
                    dve.wait_ge(*n2_mv(c.before, 1))
                    for g in range(GM):
                        i = dve.scalar_tensor_tensor(wxN[:, g, :], yp(g), mv[N2][:, g, 0:1], gamma2[:, l, :],
                                                     ALU.subtract, ALU.mult)
                    i.then_inc(xn_ready.sem, 1)
                if h == M_XB and c.post:
                    dve.wait_ge(*n2_rstd(c.before, 1))
                    dve.wait_ge(*xn_ready(c.before, 1))
                    for g in range(GM):
                        dst = wxN[:, g, :] if c.new else xc[s][:, g, :]
                        i = dve.scalar_tensor_tensor(dst, wxN[:, g, :], rstd[N2][:, g:g + 1], betab2[:, l, :],
                                                     ALU.mult, ALU.add)
                    i.then_inc((xg_ready if c.new else xc_ready).sem, 1)
                if not c.attend:
                    return
                if h == M_LN0 and c.new:
                    dve.wait_ge(*x_loaded[c.s](Seg(c.it, 1, c.group), 1))
                    stats(N0, lambda g: xc[c.s][:, g, :], ln0_bn, ln0_mv, c.n0)
                if h == M_Z0 and c.new:
                    normalise(N0, lambda g: xc[c.s][:, g, :], lambda g: xc[c.s][:, g, :], ln0_rstd,
                              ln0_z, c.n0)
                    dve.wait_ge(*ln0_z(c.n0, 1))
                    dve.tensor_scalar(xc[c.s][:, :, :], xc[c.s][:, :, :], 0.0, None,
                                      ALU.max).then_inc(xc_ready.sem, 1)
                if h == M_ROW_COPY:
                    dve.wait_ge(*rows_filled(c.n, 1))
                    dve.tensor_copy(rowR[32:33, 0:CM], ps[32:33, XB, 0:CM]).then_inc(rowb_ready.sem, 1)
                if h == M_MAX:
                    flat = lambda t: t[:, :, :].rearrange("p g n -> p (g n)")
                    dve.wait_ge(*t_ready(c.n, 1))
                    dve.tensor_tensor(flat(lE), ps[:, SB, 0:CM], flat(tE), ALU.max).then_inc(l_ready.sem, 1)
                    dve.wait_ge(*l_ready(c.n, 1))
                    dve.tensor_reduce(nmx[:, :], lE[:, :, :], AX.X, ALU.max, negate=True).then_inc(m_ready.sem, 1)
                if h == M_RECIP:
                    dve.wait_ge(*e_ready(c.n, 1))
                    dve.reciprocal(rsum[:, :], ssum[:, :]).then_inc(r_ready.sem, 1)
                if h == M_HP:
                    dve.wait_ge(*r_ready(c.n, 1))
                    dve.wait_ge(*agg_filled(c.n, 1))
                    for g in range(GM):
                        i = dve.scalar_tensor_tensor(wh[:, g, :], ps[:, SB, g * D:(g + 1) * D],
                                                     rsum[:, g:g + 1], xc[c.s][:, g, :], ALU.mult, ALU.add)
                    i.then_inc(hp_ready.sem, 1)
                    dve.wait_ge(*hp_ready(c.n, 1))
                    stats(N1, lambda g: wh[:, g, :], n1_bn, n1_mv, c.n)
                if h == M_HN:
                    normalise(N1, lambda g: wh[:, g, :], lambda g: wh[:, g, :], n1_rstd, hn_ready, c.n)
                if h == M_HTH:
                    dve.wait_ge(*hT_ready(c.n, KC))
                    dve.tensor_copy(hTh[c.s][:, :, :], hT[c.s][:, :, :]).then_inc(hTh_ready.sem, 1)

            def tail(h, it, s, w):
                q = w.segment(it, s)
                if h in COUNT_AT:
                    part = COUNT_AT.index(h)
                    k = part // 2
                    if part == 0:
                        dve.wait_ge(*w.adjT_loaded(q, 1))
                        if not w.first(it, s):
                            dve.wait_ge(*w.o_filled(Seg(it, 2, s - 1), 2))
                    elif part == 2:
                        dve.wait_ge(*w.cnt_ready(q, 1))
                    for v in range(part % 2 * (NLAB // 4), (part % 2 + 1) * (NLAB // 4)):
                        i = dve.tensor_scalar(w.oh[:, v, :, :], w.adjT[:, :, :], k * (NLAB // 2) + v, None,
                                              ALU.is_equal)
                    if part % 2 == 1:
                        i.then_inc(w.oh_ready.sem, 1)
                if h in TREE_AT:
                    k = TREE_AT.index(h)
                    dve.wait_ge(*w.oh_ready(q, k + 1))
                    for m, done in ((P // 2, w.sum1_ready), (P // 4, w.sum2_ready), (P // 8, w.sum3_ready)):
                        dve.tensor_tensor(w.oh[:, :, :, 0:m], w.oh[:, :, :, 0:m], w.oh[:, :, :, m:2 * m],
                                          ALU.add).then_inc(done.sem, 1)
                        dve.wait_ge(*done(q, k + 1))
                    dve.tensor_reduce(w.cnt[:, :, k * (NLAB // 2):(k + 1) * (NLAB // 2)].rearrange("p g v -> p v g"),
                                      w.oh[:, :, :, 0:P // 8], AX.X, ALU.add).then_inc(w.cnt_ready.sem, 1)
                for stage_no in (1, 2, 3):
                    if h == N_AT[stage_no - 1]:
                        dve.wait_ge(*(x1_ready(seg2(it, s), 2), w.x2_ready(q, 1), w.x3_ready(q, 1))[stage_no - 1])
                        stats(w.stat, lambda g: xt[s][:, g, :], w.q_bn, w.q_mv, q, stage_no)
                    if h == N_Z[stage_no - 1]:
                        normalise(w.stat, lambda g: w.zN[:, g, :], lambda g: xt[s][:, g, :], w.q_rstd, w.q_z, q, stage_no)
                if h == G1_ROW_COPY:
                    dve.wait_ge(*w.r1_filled(q, 1))
                    dve.tensor_copy(rowR[w.base + 32:w.base + 33, :], ps[w.base + 32:w.base + 33, w.bank, :]).then_inc(w.r1b_ready.sem, 1)
                if h == G1_MAX:
                    dve.wait_ge(*w.t1_ready(q, 1))
                    fl = lambda a: w.u[:, 0, a * G:(a + 1) * G, :].rearrange("p g n -> p (g n)")
                    dve.tensor_tensor(fl(1), ps[:, w.bank + 1, :], fl(0), ALU.max).then_inc(w.l1_ready.sem, 1)
                    dve.wait_ge(*w.l1_ready(q, 1))
                    dve.tensor_reduce(w.nmxT[:, 0, 0:G], w.u[:, 0, G:2 * G, :], AX.X, ALU.max,
                                      negate=True).then_inc(w.m1_ready.sem, 1)
                if h == G1_RECIP:
                    dve.wait_ge(*w.e1_ready(q, 1))
                    dve.reciprocal(w.rsumT[:, 0, 0:G], w.ssumT[:, 0, 0:G]).then_inc(w.d1_ready.sem, 1)
                if h == G1_MIN:
                    dve.wait_ge(*w.d1_ready(q, 1))
                    for g in range(G):
                        if g % 2 == 0:
                            dve.wait_ge(*w.agg1_filled(q, g // 2 + 1))
                        i = dve.tensor_scalar(w.u[:, 1, 2 * g:2 * g + 2, :].rearrange("p h n -> p (h n)"),
                                              ps[:, w.bank + g // 2, (g % 2) * D:(g % 2 + 1) * D],
                                              w.rsumT[:, 0, g:g + 1], 0.0, ALU.mult, ALU.min)
                    i.then_inc(w.mn_ready.sem, 1)
                if h == G1_ELU:
                    dve.wait_ge(*w.ex_ready(q, 1))
                    u1 = w.u[:, 1, :, :].rearrange("p h n -> p (h n)")
                    dve.tensor_scalar(u1, u1, -1.0, None, ALU.add).then_inc(w.em_ready.sem, 1)
                    dve.wait_ge(*w.em_ready(q, 1))
                    for g in range(G):
                        ug = w.u[:, 1, 2 * g:2 * g + 2, :].rearrange("p h n -> p (h n)")
                        i = dve.scalar_tensor_tensor(ug, ps[:, w.bank + g // 2, (g % 2) * D:(g % 2 + 1) * D],
                                                     w.rsumT[:, 0, g:g + 1], ug, ALU.mult, ALU.max)
                    i.then_inc(w.el_ready.sem, 1)
                    dve.wait_ge(*w.el_ready(q, 1))
                    xf = xt[s][:, :, :].rearrange("p g d -> p (g d)")
                    dve.tensor_tensor(xf, xf, u1, ALU.add).then_inc(w.x2_ready.sem, 1)
                if h in G2_V_COPY:
                    g = G2_V_COPY.index(h)
                    dve.wait_ge(*w.v2_ready(q, g + 1))
                    dve.tensor_copy(w.dstT[:, g * H:(g + 1) * H], ps[:, w.bank + g % 2, D + H:D + 2 * H])
                    dve.tensor_tensor(w.srcT[:, g, :], ps[:, w.bank + g % 2, D:D + H], batt[:, :],
                                      ALU.add).then_inc(w.a2_ready.sem, 1)
                if h in G2_SUM:
                    g = G2_SUM.index(h)
                    if g == 0:
                        dve.wait_ge(*w.a2_ready(q, G))
                    dve.wait_ge(*w.b2_spread[g % 2](q, g // 2 + 1))
                    for hd in range(H):
                        i = dve.scalar_tensor_tensor(w.u[:, g % 2, hd, :], w.u[:, g % 2, hd, :],
                                                     w.srcT[:, g, hd:hd + 1], w.neg1[:, g, :],
                                                     ALU.add, ALU.add)
                    i.then_inc(w.u2_ready.sem, 1)
                if h in G2_LEAKY:
                    g = G2_LEAKY.index(h)
                    dve.wait_ge(*w.u2_ready(q, g + 1))
                    ug = w.u[:, g % 2, :, :].rearrange("p h n -> p (h n)")
                    dve.scalar_tensor_tensor(ug, ug, SLOPE, ug, ALU.mult, ALU.max).then_inc(w.l2_ready.sem, 1)
                if h in G2_MAX:
                    g = G2_MAX.index(h)
                    dve.wait_ge(*w.l2_ready(q, g + 1))
                    if g >= 2:
                        dve.wait_ge(*w.e2_ready(q, g - 1))
                    dve.tensor_reduce(w.nmxT[:, g % 2, :], w.u[:, g % 2, :, :], AX.X, ALU.max,
                                      negate=True).then_inc(w.m2_ready.sem, 1)
                if h == G2_X3:
                    dve.wait_ge(*w.e2_ready(q, G))
                    dve.reciprocal(w.rsumT[:, :, :], w.ssumT[:, :, :]).then_inc(w.d2_ready.sem, 1)
                    dve.wait_ge(*w.d2_ready(q, 1))
                    for c in range(2):
                        dve.wait_ge(*w.back_filled(q, c + 1))
                        dve.tensor_tensor(w.z[:, c * C:(c + 1) * C].rearrange("p (g h k) -> p (g h) k", g=2, h=H),
                                          ps[:, w.bank + c, :].rearrange("p (g h k) -> p (g h) k", g=2, h=H),
                                          w.rsumT[:, 2 * c:2 * c + 2, :].rearrange("p g (h a) -> p (g h) a", a=1)
                                          .to_broadcast([P, 2 * H, DH]), ALU.mult).then_inc(w.bn_ready.sem, 1)
                    dve.wait_ge(*w.bn_ready(q, 2))
                    xf = xt[s][:, :, :].rearrange("p g d -> p (g d)")
                    dve.scalar_tensor_tensor(xf, w.z[:, :], 0.0, xf, ALU.max, ALU.add).then_inc(w.x3_ready.sem, 1)
                if h == G3_RES:
                    xf = xt[s][:, :, :].rearrange("p g d -> p (g d)")
                    dve.wait_ge(*w.q_zT(q, 3 * KC))
                    dve.scalar_tensor_tensor(w.z[:, :], w.z[:, :], 0.0, xf, ALU.max, ALU.add).then_inc(w.res_ready.sem, 1)
                if h in G3_SUM:
                    c = G3_SUM.index(h)
                    dve.wait_ge(*w.res_ready(q, 1))
                    dve.wait_ge(*w.o_filled(q, c + 1))
                    dve.tensor_tensor(w.V[:, 2 * c:2 * c + 2, 0:D],
                                      ps[:, w.bank + c, :].rearrange("p (g d) -> p g d", g=2),
                                      w.zN[:, 2 * c:2 * c + 2, :], ALU.add).then_inc(w.o_ready.sem, 1)

            def init(h, o):
                k = piece_at(h, o)
                if k is not None:
                    dve.wait_ge(*i_hi(0, k + 1))
                    dve.tensor_tensor(pieces[k][1], stage[k % 2], pieces[k][0].bitcast(F32),
                                      ALU.subtract).then_inc(i_lo.sem, 1)
                if (o, h) == (-LEAD, 27):
                    dve.wait_ge(*i_b2x(0, 3))
                    dve.tensor_copy(b2s[:, :], b2x).then_inc(i_b2.sem, 1)
                    dve.wait_ge(*i_b2(0, 2))
                    dve.tensor_tensor(b2r, b2x, b2s[:, :], ALU.subtract).then_inc(i_b2.sem, 1)
                    dve.wait_ge(*i_b2(0, 3))
                    dve.tensor_copy(b2s[32:33, :], b2r[32:33, :])
                    dve.tensor_copy(b2s[64:65, :], b2r[64:65, :]).then_inc(i_b2.sem, 1)
                    dve.wait_ge(*i_b2(0, 4))
                    dve.tensor_tensor(b2x[64:65, :], b2r[64:65, :], b2s[64:65, :],
                                      ALU.subtract).then_inc(i_b2.sem, 1)
                    dve.wait_ge(*i_b2(0, 5))
                    dve.tensor_copy(b2s[64:65, :], b2x[64:65, :]).then_inc(i_b2.sem, 1)
                if (o, h) == (0, 0):
                    dve.wait_ge(*i_tabs(0, i_tabs.per))
                if (o, h) == (4, 12):
                    dve.wait_ge(*i_small(0, i_small.per))
                    for c in range(KC):
                        for t in range(2):
                            dve.tensor_tensor_reduce(prod, Wg1[:, c, :], abc[:, t * D:(t + 1) * D], 1.0, 0.0,
                                                     ALU.mult, ALU.add,
                                                     wrow1[:, c, 32 * t:32 * t + 1]).then_inc(i_fold.sem, 1)
                            wa = wabc.rearrange("p (h t k) -> p h t k", h=H, t=2)[:, :, t, :]
                            dve.tensor_tensor(prod2.rearrange("p (h k) -> p h k", h=H),
                                              Wg2[:, c, 0:D].rearrange("p (h k) -> p h k", h=H), wa,
                                              ALU.mult).then_inc(i_cols.sem, 1)
                            dve.wait_ge(*i_cols(0, 2 * c + t + 1))
                            dve.tensor_reduce(Wg2[:, c, D + t * H:D + (t + 1) * H],
                                              prod2.rearrange("p (h k) -> p h k", h=H), AX.X,
                                              ALU.add).then_inc(i_fold.sem, 1)
                            dve.wait_ge(*i_fold(0, 4 * c + 2 * t + 2))
                    dve.tensor_tensor(prod3, raw3[:, 0:2, :], raw3[:, 2:4, :], ALU.add).then_inc(i_sum3.sem, 1)

            def ff(h, it, o):
                n, before = Seg(it, SL, o), Seg(it, SL, o - 1)
                if h in GH_AT:
                    p = GH_AT.index(h)
                    dve.wait_ge(*gf_ready(n, p + 1))
                    if p >= NS:
                        dve.wait_ge(*g_used(n, p + 1 - NS))
                    elif exists(it, o - 1):
                        dve.wait_ge(*g_used(before, FP + p + 1 - NS))
                    dve.tensor_copy(gh[:, (FP * o + p) % NS, :], gf[:, (FP * o + p) % NG, :]).then_inc(gh_ready.sem, 1)

            schedule(dve, init, ff, main, tail)

        @block.tensor
        def _(pe):
            def transposes(bank, src, n, done):
                for i in range(n):
                    ins = pe.transpose(ps[:, bank, i * P:(i + 1) * P], src(i), identf[:, :])
                ins.then_inc(done.sem, 1)

            def rows(bank, w, src, base, n, done):
                for c in range(KC):
                    ins = pe.matmul(ps[base:base + 33, bank, 0:n * P], w(c), src[:, c, :], start=(c == 0),
                                    stop=(c == KC - 1))
                ins.then_inc(done.sem, 1)

            def scores(bank, neg, base, n, done):
                pe.matmul(ps[:, bank, 0:n * P], identb[:, :], neg[:, :, :].rearrange("p g n -> p (g n)"),
                          start=True, stop=False, skip_group_check=True)
                for g in range(n):
                    ins = pe.matmul(ps[:, bank, g * P:(g + 1) * P], rowL[base:base + 33, g * P:(g + 1) * P],
                                    rowR[base:base + 33, g * P:(g + 1) * P], start=False, stop=(g == n - 1),
                                    skip_group_check=True)
                ins.then_inc(done.sem, 1)

            def aggregate(bank, eT, v, n, done):
                for c in range(n // 2):
                    for g in (2 * c, 2 * c + 1):
                        ins = pe.matmul(ps[:, bank + c, (g % 2) * D:(g % 2 + 1) * D], eT(g), v(g),
                                        start=True, stop=True)
                    ins.then_inc(done.sem, 1)

            def main(h, c):
                it, o = c.it, c.o
                if not c.attend:
                    return
                if h == M_XT:
                    pe.wait_ge(*xc_ready(c.n, 1))
                    if exists(it, o - 2):
                        pe.wait_ge(*hT_ready(Seg(it, SL, o - 2), KC))
                    elif exists(it, o - 1):
                        pe.wait_ge(*rowa_ready(Seg(it, SL, o - 1), 1))
                        pe.wait_ge(*rowb_ready(Seg(it, SL, o - 1), 1))
                    transposes(XB, lambda i: xc[c.s][:, i % GM, i // GM * P:(i // GM + 1) * P], GM * KC,
                               xT_filled)
                if h == M_ROWS:
                    pe.wait_ge(*xT_ready(c.n, 1))
                    rows(XB, lambda k: wrow0[:, c.l, k, :], wxT, 0, GM, rows_filled)
                if h == M_SCORES:
                    pe.wait_ge(*rowa_ready(c.n, 1))
                    pe.wait_ge(*rowb_ready(c.n, 1))
                    if c.new:
                        pe.wait_ge(*neg0_ready(c.n0, 1))
                    if exists(it, o - 1):
                        pe.wait_ge(*hp_ready(Seg(it, SL, o - 1), 1))
                    scores(SB, neg0[c.s], 0, GM, s_filled)
                if h == M_ET:
                    pe.wait_ge(*e_ready(c.n, 1))
                    transposes(SB, lambda g: tE[:, g, :], GM, eT_filled)
                if h == M_AGG:
                    pe.wait_ge(*eT_ready(c.n, 1))
                    aggregate(SB, lambda g: lE[:, g, :], lambda g: xc[c.s][:, g, :], GM, agg_filled)
                if h == M_HT:
                    pe.wait_ge(*hn_ready(c.n, 1))
                    if exists(it, o + 1):
                        pe.wait_ge(*rowa_ready(Seg(it, SL, o + 1), 1))
                        pe.wait_ge(*rowb_ready(Seg(it, SL, o + 1), 1))
                    else:
                        pe.wait_ge(*hT_ready(Seg(it, SL, o - 1), KC))
                    transposes(XB, lambda i: wh[:, i % GM, i // GM * P:(i // GM + 1) * P], GM * KC,
                               hnT_filled)

            def tail(h, it, s, w):
                q = w.segment(it, s)
                first = w.first(it, s)
                for stage_no in (1, 2, 3):
                    if h == N_ZT[stage_no - 1]:
                        pe.wait_ge(*w.q_z(q, stage_no))
                        if stage_no == 3:
                            pe.wait_ge(*w.cntT_ready(q, 1))
                        if stage_no == 1 and not first:
                            pe.wait_ge(*w.o_ready(Seg(it, 2, s - 1), 2))
                        for c in range(KC):
                            transposes(w.bank + c, lambda g: w.zN[:, g, c * P:(c + 1) * P], G, w.q_zT)
                if h in G1_V:
                    g = G1_V.index(h)
                    if g == 0:
                        pe.wait_ge(*w.q_T(q, KC))
                        if not first:
                            pe.wait_ge(*w.o_stored(Seg(it, 2, s - 1), 1))
                    for k in range(KC):
                        i = pe.matmul(ps[:, w.bank + g // 2, (g % 2) * D:(g % 2 + 1) * D],
                                      w.qT[:, k, g * P:(g + 1) * P], Wg1[:, k, :],
                                      start=(k == 0), stop=(k == KC - 1))
                    if g % 2 == 1:
                        i.then_inc(w.v1_filled.sem, 1)
                if h == G1_ROWS:
                    pe.wait_ge(*w.v1_ready(q, 1))
                    rows(w.bank, lambda c: wrow1[:, c, :], w.qT, w.base, G, w.r1_filled)
                if h == G1_SCORES:
                    pe.wait_ge(*w.r1a_ready(q, 1))
                    pe.wait_ge(*w.r1b_ready(q, 1))
                    pe.wait_ge(*w.neg1_ready(q, 1))
                    pe.wait_ge(*w.v1_ready(q, 2))
                    scores(w.bank + 1, w.neg1, w.base, G, w.s1_filled)
                if h == G1_ET:
                    pe.wait_ge(*w.e1_ready(q, 1))
                    transposes(w.bank, lambda g: w.u[:, 0, g, :], G, w.eT1_filled)
                if h == G1_AGG:
                    pe.wait_ge(*w.eT1_ready(q, 1))
                    aggregate(w.bank, lambda g: w.z[:, g * P:(g + 1) * P], lambda g: w.V[:, g, 0:D], G,
                              w.agg1_filled)
                if h in G2_V:
                    g = G2_V.index(h)
                    pe.wait_ge(*w.q_T(q, 2 * KC))
                    if g >= 2:
                        pe.wait_ge(*w.a2_ready(q, g - 1))
                    for k in range(KC):
                        i = pe.matmul(ps[:, w.bank + g % 2, 0:VW], w.qT[:, k, g * P:(g + 1) * P],
                                      Wg2[:, k, :], start=(k == 0), stop=(k == KC - 1))
                    i.then_inc(w.v2_filled.sem, 1)
                if h == G2_BT:
                    pe.wait_ge(*w.a2_ready(q, G))
                    pe.transpose(ps[0:G * H, w.bank, 0:P], w.dstT[:, :], identf[:, :]).then_inc(w.b2_filled.sem, 1)
                for g in range(G):
                    if h == G2_ET[g]:
                        pe.wait_ge(*w.e2_ready(q, g + 1))
                        if g >= 1:
                            pe.wait_ge(*w.agg2_ready(q, g))
                        for c in range(2):
                            transposes(w.bank + c, lambda i: w.u[:, g % 2, 4 * c + i, :], 4, w.eT2_filled)
                    if h == G2_AGG[g]:
                        pe.wait_ge(*w.eT2_ready(q, 2 * g + 2))
                        for hd in range(H):
                            r = hd % HPB * DH
                            i = pe.matmul(ps[r:r + DH, w.bank, hd // HPB * P:(hd // HPB + 1) * P],
                                          w.V[:, g, hd * DH:(hd + 1) * DH], w.z[:, hd * P:(hd + 1) * P],
                                          start=True, stop=True)
                        i.then_inc(w.agg2_filled.sem, 1)
                if h == G2_BACK:
                    pe.wait_ge(*w.agg2_ready(q, G))
                    for c in range(2):
                        transposes(w.bank + c, lambda i: w.qT[:, i % 2, (2 * c + i // 2) * P:(2 * c + i // 2 + 1) * P],
                                   4, w.back_filled)
                if h == G3_CNT:
                    pe.wait_ge(*w.cnt_ready(q, 2))
                    pe.wait_ge(*w.back_filled(q, 2))
                    pe.wait_ge(*w.bn_ready(q, 2))
                    for g in range(G):
                        i = pe.transpose(ps[0:NLAB, w.bank, g * P:(g + 1) * P], w.cnt[:, g, :], identf[:, :])
                    i.then_inc(w.cntT_filled.sem, 1)
                if h in G3_OUT:
                    g = G3_OUT.index(h)
                    if g == 0:
                        pe.wait_ge(*w.cntT_ready(q, 1))
                        pe.wait_ge(*w.q_T(q, 3 * KC))
                    o = ps[:, w.bank + g // 2, (g % 2) * D:(g % 2 + 1) * D]
                    for k in range(KC):
                        pe.matmul(o, w.qT[:, k, g * P:(g + 1) * P], Wg3[:, k, :], start=(k == 0), stop=False)
                    i = pe.matmul(o, w.cntT[:, g * P:(g + 1) * P], table[:, :], start=False, stop=True)
                    if g % 2 == 1:
                        i.then_inc(w.o_filled.sem, 1)

            def ff1(it, o, p):
                n, l, s = Seg(it, SL, o), o // NSTR % L, o % NSTR
                if p >= 2:
                    pe.wait_ge(*gf_ready(n, p - 1))
                elif exists(it, o - 1):
                    pe.wait_ge(*gf_ready(Seg(it, SL, o - 1), FP + p - 1))
                ins = None
                for c in (2 * p, 2 * p + 1):
                    for i, (w, v) in enumerate(((W1h, hTh), (W1l, hTh), (W1h, hTl))):
                        if c == 0 and i != 1:
                            pe.wait_ge(*(hTh_ready if i == 0 else hTl_ready)(n, 1))
                        for k in range(KC):
                            ins = pe.matmul(ps[:, FF1 + p % 2, c % 2 * CM:(c % 2 + 1) * CM],
                                            w[:, l, k, c * P:(c + 1) * P], v[s][:, k, :],
                                            start=(i == 0 and k == 0), stop=(i == 2 and k == KC - 1))
                ins.then_inc(ff1_filled.sem, 1)

            def ff2(it, o, p):
                n, l, s, r = Seg(it, SL, o), o // NSTR % L, o % NSTR, (FP * o + p) % NS
                y = [ps[:, FF2 + o % 2, g * D:(g + 1) * D] for g in range(GM)]
                ins = None
                if p == 0:
                    if exists(it, o - 2):
                        pe.wait_ge(*xn_ready(Seg(it, SL, o - 2), 1))
                    for g in range(GM):
                        pe.matmul(y[g], onesb[:, :], b2s[:, l * D:(l + 1) * D], start=(g == 0), stop=False,
                                  skip_group_check=True)
                        for k in range(KC):
                            pe.matmul(y[g][:, k * P:(k + 1) * P], hT[s][:, k, g * P:(g + 1) * P],
                                      identf[:, :], start=False, stop=False, skip_group_check=True)
                for i, (w, v) in enumerate(((W2h, gh), (W2l, gh), (W2h, gl))):
                    if i != 1:
                        pe.wait_ge(*(gh_ready if i == 0 else gl_ready)(n, p + 1))
                    for c in (2 * p, 2 * p + 1):
                        for g in range(GM):
                            m = c % 2 * CM + g * P
                            ins = pe.matmul(y[g], v[:, r, m:m + P], w[:, l, c, :], start=False,
                                            stop=(c == FC - 1 and i == 2), skip_group_check=True)
                ins.then_inc(g_used.sem, 1)

            def ff(h, it, o):
                if h in FF1_AT:
                    ff1(it, o, FF1_AT.index(h))
                if h in FF2_AT:
                    ff2(it, o, FF2_AT.index(h))

            def init(h, o):
                if (o, h) == (0, 0):
                    pe.wait_ge(*i_b2(0, i_b2.per))
                if (o, h) == (-LEAD, M_ROWS):
                    pe.wait_ge(*i_rows0(0, 4))
                    pe.wait_ge(*i_small(0, i_small.per))
                if h == 0 and o in range(0, SL, NSTR):
                    pe.wait_ge(*i_lo(0, PPL * (o // NSTR + 1)))
                if (o, h) == (6, 10):
                    pe.wait_ge(*i_sum3(0, 1))
                    pe.wait_ge(*i_fold(0, 8))
                    for c in range(KC):
                        transposes(TB + c, lambda i: prod3[:, i, c * P:(c + 1) * P], KC, i_t3)
                if (o, h) == (7, 0):
                    pe.wait_ge(*i_w3(0, KC))

            pe.wait_ge(*i_ident(0, 3))
            schedule(pe, init, ff, main, tail)


_INS = ["x", "adj", "L0_gnn_attn_w", "L0_gnn_attn_b", "L0_gnn_W1", "L0_gnn_b1", "L0_gnn_W2", "L0_gnn_b2",
        "L0_gnn_g1", "L0_gnn_beta1", "L0_gnn_g2", "L0_gnn_beta2", "L1_gnn_W", "L1_gnn_a", "L2_gnn_W_proj",
        "L2_gnn_W_att", "L2_gnn_b_att", "L3_gnn_weights", "L3_gnn_bias"]


def kernel(**inputs):
    import numpy as _np
    import concourse.bacc as _bacc
    from concourse import mybir as _mybir
    from concourse.bass_utils import run_bass_kernel_spmd as _run

    nc = _bacc.Bacc("TRN2", target_bir_lowering=False, num_devices=1)
    arrays, args = {}, []
    for name in _INS:
        a = _np.ascontiguousarray(inputs[name])
        arrays[f"in_{name}_dram"] = a
        args.append(nc.dram_tensor(f"in_{name}_dram", a.shape, _mybir.dt.from_np(a.dtype), kind="ExternalInput").ap())
    shape = inputs["x"].shape
    out = nc.dram_tensor("out_dram", shape, _mybir.dt.float32, kind="ExternalOutput").ap()
    build(nc, *args, out)
    r = _run(nc, [arrays], core_ids=[0])
    return r.results[0]["out_dram"]
```
